# Optimizing a Trainium2 kernel written in Bass

```python
import numpy as np
import jax
import jax.numpy as jnp

def _softmax(x, axis=-1):
    return jax.nn.softmax(x, axis=axis)

def _gelu(x):
    return jax.nn.gelu(x, approximate=True)

def _silu(x):
    return jax.nn.silu(x)

def _sigmoid(x):
    return jax.nn.sigmoid(x)

def _layernorm(x, axis=-1, eps=1e-05):
    m = jnp.mean(x, axis=axis, keepdims=True)
    v = jnp.var(x, axis=axis, keepdims=True)
    return (x - m) / jnp.sqrt(v + eps)

def _scatter_add(tgt, idx, src, axis=0):
    return tgt.at[idx].add(src)

def _segment_sum(src, seg, n):
    return jax.ops.segment_sum(src, seg, n)
kernel_name = 'mk_xattn_ffn_d4_seqx_r8_47db79'

def setup_inputs(seed: int=0):
    np.random.seed(seed)
    _w = jnp.asarray

    def _rec_inputs():
        import jax
        import jax.numpy as jnp
        _rk = jax.random.key(seed)
        x = -0.0003929 + 0.9999 * jax.random.normal(jax.random.fold_in(_rk, 1), (32, 64, 512), jnp.float32)
        _lenS = 64 - jax.random.randint(jax.random.fold_in(_rk, 7), (32,), 0, max(1, 64 // 4) + 1, jnp.int32)
        _lenS2 = 64 - jax.random.randint(jax.random.fold_in(_rk, 8), (32,), 0, max(1, 64 // 4) + 1, jnp.int32)
        _ctx_4096P = jax.random.normal(jax.random.fold_in(_rk, 11), (32, 16, 512), jnp.float32)
        _ctx_4096c = jax.random.dirichlet(jax.random.fold_in(_rk, 511), 0.3 * jnp.ones((16,), jnp.float32), (32, 64))
        _ctx_4096t = jnp.einsum('bsk,bkd->bsd', _ctx_4096c, _ctx_4096P)
        _ctx_4096t = _ctx_4096t * jax.lax.rsqrt(jnp.mean(jnp.square(_ctx_4096t)) + 1e-12) * 0.953939
        ctx_4096 = 2.81802e-05 + 1.00001 * (_ctx_4096t + 0.3 * jax.random.normal(jax.random.fold_in(_rk, 611), (32, 64, 512), jnp.float32))
        return (x, ctx_4096)
    x, ctx_4096 = _rec_inputs()

    def _L0_xattn_setup():
        import jax, jax.numpy as jnp
        import numpy as np
        EPS = 1e-08

        def _cosine_sim(a, b):
            na = jnp.maximum(jnp.sqrt(jnp.sum(a * a, axis=1)), EPS)
            nb = jnp.maximum(jnp.sqrt(jnp.sum(b * b, axis=1)), EPS)
            return jnp.sum(a * b, axis=1) / (na * nb)
        key = jax.random.key(seed)
        k1, k2, k3 = jax.random.split(key, 3)
        B, C, T, O, K = (8, 64, 512, 64, 3)
        feature = jax.random.normal(k1, (B, C, T), dtype=jnp.float32)
        embedding = jax.random.normal(k2, (B, C, T), dtype=jnp.float32)
        weight = jax.random.normal(k3, (O, C, K), dtype=jnp.float32) * 0.05
        return {'feature': feature, 'embedding': embedding, 'weight': weight}
    _L0_xattn_all = _L0_xattn_setup()
    _L0_xattn_in = {k: v for k, v in _L0_xattn_all.items() if k in ('weight',)}
    del _L0_xattn_all

    def _L0_ffn_setup():
        import jax, jax.numpy as jnp
        import numpy as np
        B, S, D, O, E, R = (4, 256, 512, 512, 8, 16)
        SCALING = 32.0 / 16.0
        MAX_THRESHOLD = 0.125
        key = jax.random.key(seed)
        ks = jax.random.split(key, 8)
        return {'x': jax.random.normal(ks[0], (B, S, D), jnp.float32), 'W_base': jax.random.normal(ks[1], (O, D), jnp.float32) * (1.0 / np.sqrt(D)), 'b_base': jax.random.normal(ks[2], (O,), jnp.float32) * 0.02, 'W_gate': jax.random.normal(ks[3], (E, D), jnp.float32) * (1.0 / np.sqrt(D)), 'W_thr': jax.random.normal(ks[4], (D,), jnp.float32) * (1.0 / np.sqrt(D)), 'b_thr': jax.random.normal(ks[5], (1,), jnp.float32) * 0.02, 'A_w': jax.random.normal(ks[6], (E, R, D), jnp.float32) * (1.0 / np.sqrt(D)), 'B_w': jax.random.normal(ks[7], (E, O, R), jnp.float32) * (1.0 / np.sqrt(R))}
    _L0_ffn_all = _L0_ffn_setup()
    _L0_ffn_in = {k: v for k, v in _L0_ffn_all.items() if k in ('W_base', 'b_base', 'W_gate', 'W_thr', 'b_thr', 'A_w', 'B_w')}
    del _L0_ffn_all

    def _L1_xattn_setup():
        import jax, jax.numpy as jnp
        import numpy as np
        EMB_DIM = 64
        HEADS = 8
        key = jax.random.key(seed)
        kq, kk, kv = jax.random.split(key, 3)
        B, C, N = (8, EMB_DIM, 512)
        q = jax.random.normal(kq, (B, C, N), dtype=jnp.float32)
        k = jax.random.normal(kk, (B, C, N), dtype=jnp.float32)
        v = jax.random.normal(kv, (B, C, N), dtype=jnp.float32)
        return {'q': q, 'k': k, 'v': v}
    _L1_xattn_all = _L1_xattn_setup()
    _L1_xattn_in = {k: v for k, v in _L1_xattn_all.items() if k in ()}
    del _L1_xattn_all

    def _L1_ffn_setup():
        import jax, jax.numpy as jnp
        import numpy as np
        SCALING = 32.0 / 16.0
        key = jax.random.key(seed)
        ks = jax.random.split(key, 7)
        B, T, D, O, R, E = (4, 256, 512, 512, 16, 8)
        x = jax.random.normal(ks[0], (B, T, D), dtype=jnp.float32)
        base_W = jax.random.normal(ks[1], (O, D), dtype=jnp.float32) * D ** (-0.5)
        base_b = jax.random.normal(ks[2], (O,), dtype=jnp.float32) * 0.01
        router_W = jax.random.normal(ks[3], (2 * E - 1, D), dtype=jnp.float32) * D ** (-0.5)
        router_b = jax.random.normal(ks[4], (2 * E - 1,), dtype=jnp.float32) * 0.01
        A = jax.random.normal(ks[5], (E, R, D), dtype=jnp.float32) * D ** (-0.5)
        Bm = jax.random.normal(ks[6], (E, O, R), dtype=jnp.float32) * R ** (-0.5)
        assigned_idx = 0
        others = [i for i in range(E) if i != assigned_idx]
        expert_map = jnp.array([assigned_idx] * E + others, dtype=jnp.int32)
        return {'x': x, 'base_W': base_W, 'base_b': base_b, 'router_W': router_W, 'router_b': router_b, 'A': A, 'B': Bm, 'expert_map': expert_map}
    _L1_ffn_all = _L1_ffn_setup()
    _L1_ffn_in = {k: v for k, v in _L1_ffn_all.items() if k in ('base_W', 'base_b', 'router_W', 'router_b', 'A', 'B', 'expert_map')}
    del _L1_ffn_all

    def _L2_xattn_setup():
        import jax, jax.numpy as jnp
        import numpy as np
        N, C, S = (16, 64, 512)
        rng = jax.random.key(seed)
        k1, k2, k3 = jax.random.split(rng, 3)
        return {'key': jax.random.normal(k1, (N, C, S), dtype=jnp.float32), 'value': jax.random.normal(k2, (N, C, S), dtype=jnp.float32), 'query': jax.random.normal(k3, (N, C, S), dtype=jnp.float32)}
    _L2_xattn_all = _L2_xattn_setup()
    _L2_xattn_in = {k: v for k, v in _L2_xattn_all.items() if k in ()}
    del _L2_xattn_all

    def _L2_ffn_setup():
        import jax, jax.numpy as jnp
        import numpy as np
        RANKS = (8, 16, 32, 64)
        TOPK = 1
        SCALING = 1.0 / 4
        key = jax.random.key(seed)
        ks = jax.random.split(key, 7)
        D_IN, D_OUT, MAX_R, N_RANKS = (512, 512, 64, len(RANKS))
        B_, S_ = (4, 256)
        return {'hidden_states': jax.random.normal(ks[0], (B_, S_, D_IN), jnp.float32), 'W': jax.random.normal(ks[1], (D_OUT, D_IN), jnp.float32) * 0.02, 'b': jax.random.normal(ks[2], (D_OUT,), jnp.float32) * 0.02, 'A': jax.random.normal(ks[3], (MAX_R, D_IN), jnp.float32) * 0.02, 'B': jnp.zeros((D_OUT, MAX_R), jnp.float32) + jax.random.normal(ks[4], (D_OUT, MAX_R), jnp.float32) * 0.02, 'gate_w': jax.random.normal(ks[5], (N_RANKS, D_IN), jnp.float32) * 0.02, 'gate_b': jax.random.normal(ks[6], (N_RANKS,), jnp.float32) * 0.02}
    _L2_ffn_all = _L2_ffn_setup()
    _L2_ffn_in = {k: v for k, v in _L2_ffn_all.items() if k in ('W', 'b', 'A', 'B', 'gate_w', 'gate_b')}
    del _L2_ffn_all

    def _L3_xattn_setup():
        import jax, jax.numpy as jnp
        import numpy as np
        import math
        D_MODEL = 128
        NHEAD = 16
        MAX_SUP = 4
        DK = D_MODEL // NHEAD
        DM = D_MODEL * MAX_SUP
        B, S = (2, 128)
        key = jax.random.key(seed)
        ks = jax.random.split(key, 12)
        std = 0.02
        inp = {'q': jax.random.normal(ks[0], (B, S, DM), jnp.float32), 'k': jax.random.normal(ks[1], (B, S, DM), jnp.float32), 'v': jax.random.normal(ks[2], (B, S, DM), jnp.float32), 'Wq': jax.random.normal(ks[3], (DM, DM), jnp.float32) * std, 'bq': jnp.zeros((DM,), jnp.float32), 'Wk': jax.random.normal(ks[4], (DM, DM), jnp.float32) * std, 'bk': jnp.zeros((DM,), jnp.float32), 'Wv': jax.random.normal(ks[5], (DM, DM), jnp.float32) * std, 'bv': jnp.zeros((DM,), jnp.float32), 'interference': jax.random.normal(ks[6], (NHEAD, MAX_SUP, MAX_SUP), jnp.float32), 'amp': jnp.ones((1,), jnp.float32), 'Wo': jax.random.normal(ks[7], (DM, DM), jnp.float32) * std, 'bo': jnp.zeros((DM,), jnp.float32)}
        return inp
    _L3_xattn_all = _L3_xattn_setup()
    _L3_xattn_in = {k: v for k, v in _L3_xattn_all.items() if k in ('Wq', 'bq', 'Wk', 'bk', 'Wv', 'bv', 'interference', 'amp', 'Wo', 'bo')}
    del _L3_xattn_all

    def _L3_ffn_setup():
        import jax, jax.numpy as jnp
        import numpy as np
        H, FF = (512, 1792)
        B, S = (4, 256)
        key = jax.random.key(seed)
        ks = jax.random.split(key, 7)
        x = jax.random.normal(ks[0], (B, S, H), dtype=jnp.float32)
        gate_t = jax.random.randint(ks[1], (FF, H), -1, 2, dtype=jnp.int32)
        up_t = jax.random.randint(ks[2], (FF, H), -1, 2, dtype=jnp.int32)
        down_t = jax.random.randint(ks[3], (H, FF), -1, 2, dtype=jnp.int32)
        gate_s = jax.random.uniform(ks[4], (FF,), jnp.float32, 0.01, 0.1)
        up_s = jax.random.uniform(ks[5], (FF,), jnp.float32, 0.01, 0.1)
        down_s = jax.random.uniform(ks[6], (H,), jnp.float32, 0.01, 0.1)
        return {'x': x, 'gate_t': gate_t, 'up_t': up_t, 'down_t': down_t, 'gate_s': gate_s, 'up_s': up_s, 'down_s': down_s}
    _L3_ffn_all = _L3_ffn_setup()
    _L3_ffn_in = {k: v for k, v in _L3_ffn_all.items() if k in ('gate_t', 'up_t', 'down_t', 'gate_s', 'up_s', 'down_s')}
    del _L3_ffn_all
    return {'x': x, 'ctx_4096': ctx_4096, 'L0_xattn_weight': _L0_xattn_in['weight'], 'L0_ffn_W_base': _L0_ffn_in['W_base'], 'L0_ffn_b_base': _L0_ffn_in['b_base'], 'L0_ffn_W_gate': _L0_ffn_in['W_gate'], 'L0_ffn_W_thr': _L0_ffn_in['W_thr'], 'L0_ffn_b_thr': _L0_ffn_in['b_thr'], 'L0_ffn_A_w': _L0_ffn_in['A_w'], 'L0_ffn_B_w': _L0_ffn_in['B_w'], 'L1_ffn_base_W': _L1_ffn_in['base_W'], 'L1_ffn_base_b': _L1_ffn_in['base_b'], 'L1_ffn_router_W': _L1_ffn_in['router_W'], 'L1_ffn_router_b': _L1_ffn_in['router_b'], 'L1_ffn_A': _L1_ffn_in['A'], 'L1_ffn_B': _L1_ffn_in['B'], 'L1_ffn_expert_map': _L1_ffn_in['expert_map'], 'L2_ffn_W': _L2_ffn_in['W'], 'L2_ffn_b': _L2_ffn_in['b'], 'L2_ffn_A': _L2_ffn_in['A'], 'L2_ffn_B': _L2_ffn_in['B'], 'L2_ffn_gate_w': _L2_ffn_in['gate_w'], 'L2_ffn_gate_b': _L2_ffn_in['gate_b'], 'L3_xattn_Wq': _L3_xattn_in['Wq'], 'L3_xattn_bq': _L3_xattn_in['bq'], 'L3_xattn_Wk': _L3_xattn_in['Wk'], 'L3_xattn_bk': _L3_xattn_in['bk'], 'L3_xattn_Wv': _L3_xattn_in['Wv'], 'L3_xattn_bv': _L3_xattn_in['bv'], 'L3_xattn_interference': _L3_xattn_in['interference'], 'L3_xattn_amp': _L3_xattn_in['amp'], 'L3_xattn_Wo': _L3_xattn_in['Wo'], 'L3_xattn_bo': _L3_xattn_in['bo'], 'L3_ffn_gate_t': _L3_ffn_in['gate_t'], 'L3_ffn_up_t': _L3_ffn_in['up_t'], 'L3_ffn_down_t': _L3_ffn_in['down_t'], 'L3_ffn_gate_s': _L3_ffn_in['gate_s'], 'L3_ffn_up_s': _L3_ffn_in['up_s'], 'L3_ffn_down_s': _L3_ffn_in['down_s']}

def reference(x, ctx_4096, L0_xattn_weight, L0_ffn_W_base, L0_ffn_b_base, L0_ffn_W_gate, L0_ffn_W_thr, L0_ffn_b_thr, L0_ffn_A_w, L0_ffn_B_w, L1_ffn_base_W, L1_ffn_base_b, L1_ffn_router_W, L1_ffn_router_b, L1_ffn_A, L1_ffn_B, L1_ffn_expert_map, L2_ffn_W, L2_ffn_b, L2_ffn_A, L2_ffn_B, L2_ffn_gate_w, L2_ffn_gate_b, L3_xattn_Wq, L3_xattn_bq, L3_xattn_Wk, L3_xattn_bk, L3_xattn_Wv, L3_xattn_bv, L3_xattn_interference, L3_xattn_amp, L3_xattn_Wo, L3_xattn_bo, L3_ffn_gate_t, L3_ffn_up_t, L3_ffn_down_t, L3_ffn_gate_s, L3_ffn_up_s, L3_ffn_down_s):
    import jax
    import jax.numpy as jnp

    def _L0_xattn_ref(feature, embedding, weight):
        import jax, jax.numpy as jnp
        import numpy as np
        EPS = 1e-08

        def _cosine_sim(a, b):
            na = jnp.maximum(jnp.sqrt(jnp.sum(a * a, axis=1)), EPS)
            nb = jnp.maximum(jnp.sqrt(jnp.sum(b * b, axis=1)), EPS)
            return jnp.sum(a * b, axis=1) / (na * nb)
        B, C, T = feature.shape
        O = weight.shape[0]
        K = 3
        emb_l = jnp.pad(embedding[:, :, :-1], ((0, 0), (0, 0), (1, 0)))
        emb_r = jnp.pad(embedding[:, :, 1:], ((0, 0), (0, 0), (0, 1)))
        sim = jnp.stack([_cosine_sim(embedding, emb_l), _cosine_sim(embedding, embedding), _cosine_sim(embedding, emb_r)], axis=1)
        att = jnp.repeat(sim, C, axis=1)
        f_pad = jnp.pad(feature, ((0, 0), (0, 0), (1, 1)))
        inp_unf = jnp.stack([f_pad[:, :, k:k + T] for k in range(K)], axis=2)
        inp_unf = inp_unf.reshape(B, C * K, T)
        w_flat = weight.reshape(O, C * K)
        out = jnp.einsum('bit,oi->bot', inp_unf * att, w_flat)
        return out

    def _L0_ffn_ref(x, W_base, b_base, W_gate, W_thr, b_thr, A_w, B_w):
        import jax, jax.numpy as jnp
        import numpy as np
        B, S, D, O, E, R = (4, 256, 512, 512, 8, 16)
        SCALING = 32.0 / 16.0
        MAX_THRESHOLD = 0.125
        base = jnp.einsum('bsd,od->bso', x, W_base) + b_base
        xf = x.reshape(-1, D)
        gate = jax.nn.softmax(xf @ W_gate.T, axis=-1)
        thr = jax.nn.sigmoid(xf @ W_thr + b_thr[0]) * MAX_THRESHOLD
        adapted = gate - thr[:, None]
        selected = (adapted >= 0).astype(x.dtype)
        w = adapted * selected
        wsum = jnp.sum(w, axis=-1, keepdims=True)
        wsum = jnp.where(wsum == 0, jnp.ones_like(wsum), wsum)
        w = w / wsum
        h = jnp.einsum('nd,erd->ner', xf, A_w)
        moe = jnp.einsum('ner,ne,eor->no', h, w, B_w) * SCALING
        return base + moe.reshape(base.shape)

    def _L1_xattn_ref(q, k, v):
        import jax, jax.numpy as jnp
        import numpy as np
        EMB_DIM = 64
        HEADS = 8
        B, C, N = q.shape
        H = HEADS
        dh = C // H
        qh = q.transpose(0, 2, 1).reshape(B, N, H, dh)
        kh = k.transpose(0, 2, 1).reshape(B, N, H, dh)
        vh = v.transpose(0, 2, 1).reshape(B, N, H, dh)
        qh = jax.nn.softmax(qh, axis=3)
        kh = jax.nn.softmax(kh, axis=1)
        kvs = jnp.einsum('bnhd,bnhe->bhde', kh, vh)
        out = jnp.einsum('bnhd,bhde->bnhe', qh, kvs)
        return out.transpose(0, 2, 3, 1).reshape(B, C, N)

    def _L1_ffn_ref(x, base_W, base_b, router_W, router_b, A, B, expert_map):
        import jax, jax.numpy as jnp
        import numpy as np
        SCALING = 32.0 / 16.0
        E = A.shape[0]
        base_out = jnp.einsum('btd,od->bto', x, base_W) + base_b
        logits = jnp.einsum('btd,nd->btn', x, router_W) + router_b
        probs = jax.nn.softmax(logits, axis=-1)
        topk_p, topk_i = jax.lax.top_k(probs, E)
        mapped = expert_map[topk_i]
        onehot = (mapped[..., None] == jnp.arange(E)).astype(x.dtype)
        w = jnp.einsum('btk,btke->bte', topk_p, onehot)
        h = jnp.einsum('btd,erd->bter', x, A)
        lora = jnp.einsum('bter,eor->bto', h * w[..., None], B) * SCALING
        return base_out + lora

    def _L2_xattn_ref(key, value, query):
        import jax, jax.numpy as jnp
        import numpy as np
        N, C, S = (16, 64, 512)
        KC = key.shape[1]
        sim = jnp.einsum('ncs,nds->ncd', key, query) * KC ** (-0.5)
        sim = jax.nn.softmax(sim, axis=1)
        context = jnp.einsum('ncd,nds->ncs', sim, value)
        return context

    def _L2_ffn_ref(hidden_states, W, b, A, B, gate_w, gate_b):
        import jax, jax.numpy as jnp
        import numpy as np
        RANKS = (8, 16, 32, 64)
        TOPK = 1
        SCALING = 1.0 / 4
        bsz, seq, d_in = hidden_states.shape
        out = jnp.einsum('bsd,od->bso', hidden_states, W) + b
        x = hidden_states.reshape(-1, d_in)
        scores = x @ gate_w.T + gate_b
        probs = jax.nn.softmax(scores, axis=-1)
        routing_weights, selected = jax.lax.top_k(probs, TOPK)
        routing_weights = routing_weights / jnp.sum(routing_weights, axis=-1, keepdims=True)
        lora_outputs = jnp.stack([x @ A[:r, :].T @ B[:, :r].T for r in RANKS], axis=1)
        sel = jnp.take_along_axis(lora_outputs, selected[:, :, None], axis=1)
        final = jnp.sum(sel * routing_weights[:, :, None], axis=1)
        return out + final.reshape(bsz, seq, -1)

    def _L3_xattn_ref(q, k, v, Wq, bq, Wk, bk, Wv, bv, interference, amp, Wo, bo):
        import jax, jax.numpy as jnp
        import numpy as np
        import math
        D_MODEL = 128
        NHEAD = 16
        MAX_SUP = 4
        DK = D_MODEL // NHEAD
        DM = D_MODEL * MAX_SUP
        B, S = (2, 128)
        b, s, dm = q.shape
        H, M = (interference.shape[0], interference.shape[1])
        dk = dm // (H * M)

        def proj(x, W, bias):
            y = x @ W.T + bias
            y = y.reshape(b, s, H, dk, M)
            return jnp.transpose(y, (0, 2, 1, 3, 4))
        qh = proj(q, Wq, bq)
        kh = proj(k, Wk, bk)
        vh = proj(v, Wv, bv)

        def interfere(x):
            return x + 0.1 * amp[0] * jnp.einsum('bhsdi,hij->bhsdj', x, interference)
        qh, kh, vh = (interfere(qh), interfere(kh), interfere(vh))
        scores = jnp.einsum('bhqdm,bhkdm->bhqkm', qh, kh) / math.sqrt(dk)
        weights = jax.nn.softmax(scores, axis=3)
        out = jnp.einsum('bhqkm,bhkdm->bhqdm', weights, vh)
        out = jnp.transpose(out, (0, 2, 1, 3, 4)).reshape(b, s, dm)
        return out @ Wo.T + bo

    def _L3_ffn_ref(x, gate_t, up_t, down_t, gate_s, up_s, down_s):
        import jax, jax.numpy as jnp
        import numpy as np
        H, FF = (512, 1792)
        B, S = (4, 256)
        Bb, Ss, Hh = x.shape
        x_flat = x.reshape(Bb * Ss, Hh)
        gate_w = gate_t.astype(jnp.float32) * gate_s[:, None]
        up_w = up_t.astype(jnp.float32) * up_s[:, None]
        down_w = down_t.astype(jnp.float32) * down_s[:, None]
        gate_out = x_flat @ gate_w.T
        up_out = x_flat @ up_w.T
        hidden = jax.nn.silu(gate_out) * up_out
        out_flat = hidden @ down_w.T
        return out_flat.reshape(Bb, Ss, -1)
    x = x + _L0_xattn_ref(_layernorm(x, axis=-1), ctx_4096, L0_xattn_weight)
    x = x + _L0_ffn_ref(_layernorm(x, axis=-1), L0_ffn_W_base, L0_ffn_b_base, L0_ffn_W_gate, L0_ffn_W_thr, L0_ffn_b_thr, L0_ffn_A_w, L0_ffn_B_w)
    x = x + _L1_xattn_ref(_layernorm(x, axis=-1), ctx_4096, ctx_4096)
    x = x + _L1_ffn_ref(_layernorm(x, axis=-1), L1_ffn_base_W, L1_ffn_base_b, L1_ffn_router_W, L1_ffn_router_b, L1_ffn_A, L1_ffn_B, L1_ffn_expert_map)
    x = x + _L2_xattn_ref(ctx_4096, ctx_4096, _layernorm(x, axis=-1))
    x = x + _L2_ffn_ref(_layernorm(x, axis=-1), L2_ffn_W, L2_ffn_b, L2_ffn_A, L2_ffn_B, L2_ffn_gate_w, L2_ffn_gate_b)
    x = x + _L3_xattn_ref(_layernorm(x, axis=-1), ctx_4096, ctx_4096, L3_xattn_Wq, L3_xattn_bq, L3_xattn_Wk, L3_xattn_bk, L3_xattn_Wv, L3_xattn_bv, L3_xattn_interference, L3_xattn_amp, L3_xattn_Wo, L3_xattn_bo)
    x = x + _L3_ffn_ref(_layernorm(x, axis=-1), L3_ffn_gate_t, L3_ffn_up_t, L3_ffn_down_t, L3_ffn_gate_s, L3_ffn_up_s, L3_ffn_down_s)
    return x

_drawn_inputs = setup_inputs


def setup_inputs(seed=0):
    import zlib

    import numpy as np

    out = dict(_drawn_inputs(seed))
    spreads = {'L3_xattn_bq': (0.0, 0.8),
     'L3_xattn_bk': (0.0, 0.8),
     'L3_xattn_bv': (0.0, 0.509),
     'L3_xattn_bo': (0.0, 0.1)}
    factors = {'L0_ffn_b_base': 4.779,
     'L1_ffn_base_b': 8.0,
     'L1_ffn_router_b': 8.0,
     'L2_ffn_b': 8.0,
     'L2_ffn_A': 3.227,
     'L2_ffn_B': 3.245,
     'L2_ffn_gate_w': 5.24,
     'L2_ffn_gate_b': 8.0,
     'L3_xattn_Wq': 8.0,
     'L3_xattn_Wk': 8.0,
     'L3_xattn_interference': 6.49}
    for name, (base, spread) in spreads.items():
        noise = np.random.default_rng([zlib.crc32(name.encode()), seed]).standard_normal(out[name].shape)
        drawn = base * np.exp(spread * noise) if base else spread * noise
        out[name] = jnp.asarray(drawn.astype(out[name].dtype))
    for name, factor in factors.items():
        out[name] = (out[name] * factor).astype(out[name].dtype)
    return out
```

```python
import concourse.bass as bass
from concourse import mybir
from contextlib import ExitStack

F32 = mybir.dt.float32
F16 = mybir.dt.float16
BF16 = mybir.dt.bfloat16
I32 = mybir.dt.int32
ALU = mybir.AluOpType
ACT = mybir.ActivationFunctionType
AX = mybir.AxisListType

P = 128
B, C, D = 32, 64, 512
BT = P // C
TILES = B * C // P
KD = D // P
EPS_LN = 1e-5
EPS_COS = 1e-8
TAPS = 3
SIM_SCALE = 1024.0
E0, R0 = 8, 16
LORA_SCALE = 2.0
MAX_THR = 0.125
NR1 = 2 * E0 - 1
R2 = 64
RANK_CUTS = [0, 8, 16, 32, 64]
H3, M3, DK3 = 16, 4, 8
HEADS = H3 * M3
FF = 1792
FC = FF // P
SPLIT_TOP = 4096.0
P_SCALE = 1024.0
RMAX = bass.bass_isa.ReduceOp.max
STAT_OPS = 3


def xattn_ffn_program(nc, a, out):
    top = ExitStack()
    sems = {}

    def sem(name):
        if name not in sems:
            sems[name] = top.enter_context(nc.semaphore(name))
        return sems[name]

    with top:
        def sb(name, shape, dt, ctx=top):
            return ctx.enter_context(nc.sbuf_tensor(name, shape, dt))

        x = sb("x", [P, TILES, D], F32)
        wide = sb("wide", [P, 3 * FC * D], F32)
        wf = sb("wf", [P, 3, KD, D], F32)
        wo = sb("wo", [P, KD, D], F32)
        ident = sb("ident", [P, P], F32)
        ident16 = sb("ident16", [P, P], F16)
        st6 = sb("st6", [P, 6], F32)
        mv2 = sb("mv2", [P, 2], F32)
        zero_eps = sb("zero_eps", [P, 2], F32)
        neg_half = sb("neg_half", [P, 2], F32)
        mean_var = sb("mean_var", [P, 2, TILES, 2], F32)
        rstd = sb("rstd", [P, 2, TILES], F32)
        nmr = sb("nmr", [P, TILES], F32)
        small = sb("small", [P, 64], F32)
        ps = top.enter_context(nc.psum_tensor("ps", [P, 8, D], F32))

        def bk(n):
            return ps[:, n, :]

        at = [0]

        def carve(shape, dt=F32):
            n = 1
            for s in shape:
                n *= s
            words = n * (2 if dt == F16 else 4) // 4
            v = wide[:, at[0]:at[0] + words]
            at[0] += words
            v = v if dt == F32 else v.bitcast(dt)
            if len(shape) == 2:
                v = v.rearrange("p (a b) -> p a b", a=shape[0])
            elif len(shape) == 3:
                v = v.rearrange("p (a b c) -> p a b c", a=shape[0], b=shape[1])
            return v

        HC = {"f0": E0 * R0 + E0 + 1, "f1": E0 * R0 + NR1, "f2": R2 + 4}
        RK = {"f0": E0 * R0, "f1": E0 * R0, "f2": R2}
        LNQ = {"x0": 0, "f0": 1, "x1": 2, "f1": 3, "x2": 4, "f2": 5, "x3": 6, "f3": 7}
        wbase = {f: carve([KD, D]) for f in HC}
        wag = {f: carve([KD, HC[f]]) for f in HC}
        wb = {f: carve([D]) for f in HC}
        bias = {f: carve([D]) for f in HC}
        wnat = carve([3, KD, D])
        b3rep = carve([3, KD, P])
        csel = carve([TILES, TAPS, P], F16)
        assert at[0] <= 3 * FC * D, at[0]

        def alone(eng):
            eng.wait_ge(sem("zeros"), 1)

        def hold(dve):
            nc.vector.memset(small[0:1, 0:1], 0.0)

        def hold_pool():
            nc.gpsimd.tensor_tensor(small[0:1, 1:2], neg_half[0:1, 0:1], neg_half[0:1, 1:2], ALU.add)

        def after(eng, s, value):
            if not isinstance(value, int) or value > 0:
                eng.wait_ge(s, value)

        def stats(dve, q, t):
            s = sem(f"stats{q}")
            nc.vector.bn_stats(st6[:, :], x[:, t, :]).then_inc(s, 1)
            dve.wait_ge(s, STAT_OPS * t + 1)
            hold(dve)
            nc.vector.bn_aggr(mv2[:, :], st6[:, :]).then_inc(s, 1)
            dve.wait_ge(s, STAT_OPS * t + 2)
            nc.vector.tensor_tensor(mean_var[:, q % 2, t, :], mv2[:, :], zero_eps[:, :], ALU.add).then_inc(s, 1)

        def pool_rstd(pool, q, t):
            pool.wait_ge(sem(f"stats{q}"), STAT_OPS * (t + 1))
            nc.gpsimd.tensor_tensor(rstd[:, q % 2, t:t + 1] if isinstance(t, int) else rstd[:, q % 2, bass.ds(t, 1)],
                                    mean_var[:, q % 2, t, 1:2], neg_half[:, 0:1], ALU.pow).then_inc(sem(f"rstd{q}"), 1)

        def col(v, t):
            return v[:, t:t + 1] if isinstance(t, int) else v[:, bass.ds(t, 1)]

        def normalise(dve, q, t, dst, done):
            dve.wait_ge(sem(f"rstd{q}"), t + 1)
            nc.vector.tensor_scalar(dst, x[:, t, :], mean_var[:, q % 2, t, 0:1], col(rstd[:, q % 2, :], t),
                                    ALU.subtract, ALU.mult).then_inc(done, 1)

        def all_tiles(eng, body, first=0, last=TILES):
            if first == 0:
                body(0, 0)
                body(1, 1)
                first = 2
            with eng.Fori(first // 2, last // 2) as i:
                for par in range(2):
                    body(2 * i + par, par)

        def tiles_with_last(eng, body):
            body(0, 0, False)
            body(1, 1, False)
            with eng.Fori(1, TILES // 2 - 1) as i:
                for par in range(2):
                    body(2 * i + par, par, False)
            body(TILES - 2, 0, False)
            body(TILES - 1, 1, True)

        def transpose4(dst, src, idm=ident):
            for k in range(KD):
                last = nc.tensor.transpose(dst[:, k * P:(k + 1) * P], src[:, k * P:(k + 1) * P], idm[:, :])
            return last

        xv = a["x"].rearrange("(t p) d -> t p d", p=P)
        ctxv = a["ctx"].rearrange("(t p) d -> t p d", p=P)
        ctxTv = a["ctxT"]
        outv = out.rearrange("(t p) d -> t p d", p=P)

        with ExitStack() as c1:
            def s1(name, shape, dt=F32):
                return sb(name, shape, dt, c1)
            erow = s1("erow", [P, 2, D])
            eT = s1("eT", [P, 2, KD, P])
            xn = s1("xn", [P, 2, D])
            xnT = s1("xnT", [P, 2, KD, P])
            fpad = s1("fpad", [P, 2, D + 2])
            fs = s1("fs", [P, TAPS, D])
            ebuf = s1("ebuf", [P, 2, D])
            ebuf2 = s1("ebuf2", [P, 2, D])
            simr = s1("simr", [32, 5, D])
            sim_h = s1("sim_h", [96, D], F16)
            sim_l = s1("sim_l", [96, D], F16)
            pick = s1("pick", [P, TILES, B])
            convw = s1("convw", [P, TAPS, P])
            g8 = s1("g8", [P, P])
            kvm = s1("kvm", [P, 2, P])
            pmat = s1("pmat", [P, 2, P])
            hw = s1("hw", [P, 2, P])
            hwT = s1("hwT", [P, 2, P])
            gs = s1("gs", [P, 2, 64])
            sm = s1("sm", [P, 2, 8])
            tmp15 = s1("tmp15", [P, E0, NR1])
            emap = s1("emap", [P, E0, NR1])
            emap_i = s1("emap_i", [P, NR1], I32)
            emap_f = s1("emap_f", [P, NR1])
            rb1 = s1("rb1", [P, NR1])
            gb2 = s1("gb2", [P, 4])
            nbthr = s1("nbthr", [P, 2])
            block = c1.enter_context(nc.Block())

            @block.sync
            def _(sp):
                sp.dma_start(pick[:], a["c_pick"]).then_inc(sem("ld_pick"), 16)
                for par in range(2):
                    sp.dma_start(erow[:, par, :], ctxv[par]).then_inc(sem(f"ld_e0_{par}"), 16)
                for g in range(4):
                    sp.dma_start(x[:, 4 * g:4 * g + 4, :], xv[4 * g:4 * g + 4].rearrange("t p d -> p t d")).then_inc(
                        sem("ld_x"), 16)

                def load_e0(t, par):
                    sp.wait_ge(sem("sq_done"), t - 1)
                    sp.wait_ge(sem("dp_done"), t - 1)
                    sp.dma_start(erow[:, par, :], ctxv[t]).then_inc(sem(f"ld_e0_{par}"), 16)
                all_tiles(sp, load_e0, 2)
                sp.dma_start(csel[0:96], a["c_sel"]).then_inc(sem("ld_conv"), 16)
                sp.dma_start(convw[:], a["convw"]).then_inc(sem("ld_conv"), 16)
                sp.dma_start(ident[:], a["c_ident"]).then_inc(sem("ld_conv"), 16)
                sp.dma_start(nbthr[:, 0:1], a["thr_b"].partition_broadcast(P)).then_inc(sem("ld_small"), 16)
                sp.dma_start(rb1[:], a["router_b"].partition_broadcast(P)).then_inc(sem("ld_small"), 16)
                sp.dma_start(emap_i[:], a["expert_map"].partition_broadcast(P)).then_inc(sem("ld_small"), 16)
                sp.dma_start(gb2[:], a["gate_b2"].partition_broadcast(P)).then_inc(sem("ld_small"), 16)
                sp.dma_start(g8[:], a["c_g8"]).then_inc(sem("ld_small"), 16)
                for f in ("f0", "f1", "f2"):
                    w = sem(f"ld_{f}")
                    sp.dma_start(wbase[f], a[f"{f}_base"].rearrange("(k p) n -> p k n", p=P)).then_inc(w, 16)
                    sp.dma_start(wag[f], a[f"{f}_ag"].rearrange("(k p) n -> p k n", p=P)).then_inc(w, 16)
                    sp.dma_start(wb[f][0:RK[f]], a[f"{f}_b"]).then_inc(w, 16)
                    sp.dma_start(bias[f], a[f"{f}_bias"].partition_broadcast(P)).then_inc(w, 16)

                def load_ctx(ph, t, par):
                    sp.dma_start(erow[:, par, :], ctxv[t]).then_inc(sem(f"ld_{ph}_{par}"), 16)
                    sp.dma_start(eT[:, par], ctxTv[t]).then_inc(sem(f"ld_{ph}_{par}"), 16)

                sp.wait_ge(sem("sq_done"), TILES)
                sp.wait_ge(sem("dp_done"), TILES)
                for par in range(2):
                    load_ctx("x1", par, par)

                def more1(t, par):
                    sp.wait_ge(sem("x1_ek"), t - 1)
                    sp.wait_ge(sem("x1_kv"), t - 1)
                    load_ctx("x1", t, par)
                all_tiles(sp, more1, 2)
                sp.dma_start(wnat, a["w3"].rearrange("w (k p) n -> p w k n", p=P)).then_inc(sem("ld_w3"), 16)
                sp.dma_start(wo[:], a["wo3"].rearrange("(k p) n -> p k n", p=P)).then_inc(sem("ld_w3"), 16)
                sp.dma_start(b3rep, a["b3rep"].rearrange("w (k p) n -> p w k n", p=P)).then_inc(sem("ld_w3"), 16)
                sp.wait_ge(sem("x1_ek"), TILES)
                sp.wait_ge(sem("x1_kv"), TILES)
                for par in range(2):
                    load_ctx("x2", par, par)

                def more2(t, par):
                    sp.wait_ge(sem("x2_out"), t - 1)
                    load_ctx("x2", t, par)
                all_tiles(sp, more2, 2)

            @block.gpsimd
            def _(pool):
                nc.gpsimd.memset(zero_eps[:, 0:1], 0.0)
                nc.gpsimd.memset(zero_eps[:, 1:2], EPS_LN)
                nc.gpsimd.memset(neg_half[:, 0:1], -0.5)
                nc.gpsimd.memset(neg_half[:, 1:2], -1.0)
                nc.gpsimd.memset(ebuf2[:, :, 0:1], 0.0)
                nc.gpsimd.memset(fpad[:, :, 0:1], 0.0)
                nc.gpsimd.memset(fpad[:, :, D + 1:D + 2], 0.0)
                nc.gpsimd.memset(simr[:, 0, :], -0.5)
                nc.gpsimd.memset(pmat[:, :, :], 0.0).then_inc(sem("zeros"), 1)
                pool.wait_ge(sem("zeros"), 1)
                all_tiles(pool, lambda t, par: pool_rstd(pool, 0, t))
                pool.wait_ge(sem("sim_steps"), 1)
                nc.gpsimd.tensor_tensor(simr[:, 2, :], simr[:, 1, :], simr[:, 0, :], ALU.pow).then_inc(sem("rnorm"), 1)
                for ph in ("x0", "f0", "x1", "f1", "x2", "f2"):
                    q = LNQ[ph]
                    if ph[0] == "f":
                        pool.wait_ge(sem(f"ld_{ph}"), 64)

                    def body(t, par, ph=ph, q=q):
                        if ph[0] == "f":
                            pool.wait_ge(sem(f"{ph}_xn"), t + 1)
                            nc.gpsimd.tensor_tensor(x[:, t, :], x[:, t, :], bias[ph], ALU.add).then_inc(
                                sem(f"{ph}_biased"), 1)
                        pool_rstd(pool, q + 1, t)
                        if q + 1 == 2:
                            alone(pool)
                            pool.wait_ge(sem("rstd2"), t + 1)
                            nc.gpsimd.tensor_tensor(col(nmr, t), mean_var[:, 0, t, 0:1], col(rstd[:, 0, :], t),
                                                    ALU.mult).then_inc(sem("nmr_steps"), 1)
                            alone(pool)
                            pool.wait_ge(sem("nmr_steps"), 2 * t + 1)
                            nc.gpsimd.tensor_tensor(col(nmr, t), col(nmr, t), neg_half[:, 1:2],
                                                    ALU.mult).then_inc(sem("nmr_steps"), 1)
                    all_tiles(pool, body)

            @block.vector
            def _(dve):
                dve.wait_ge(sem("zeros"), 1)

                def neighbours(t, par, i=None):
                    dve.wait_ge(sem(f"ld_e0_{par}"), 16 * i + 16)
                    after(dve, sem("sim_mm"), t - 1)
                    nc.vector.tensor_tensor(ebuf2[:, par, 1:D], erow[:, par, 1:D], erow[:, par, 0:D - 1],
                                            ALU.mult).then_inc(sem("dp_done"), 1)
                neighbours(0, 0, 0)
                neighbours(1, 1, 0)
                with dve.Fori(1, TILES // 2) as i:
                    for par in range(2):
                        neighbours(2 * i + par, par, i)
                dve.wait_ge(sem("ld_x"), 64)
                all_tiles(dve, lambda t, par: stats(dve, 0, t))
                ss = sem("sim_steps")
                dve.wait_ge(sem("sim_mm"), TILES)
                nn, dd = ps[0:32, 0, :], ps[0:32, 1, :]
                nc.vector.tensor_scalar(simr[:, 1, :], nn, EPS_COS * EPS_COS, None, ALU.max).then_inc(ss, 1)
                dve.wait_ge(sem("rnorm"), 1)
                rn = simr[:, 2, :]
                nc.vector.tensor_tensor(simr[:, 3, :], nn, rn, ALU.mult).then_inc(ss, 1)
                dve.wait_ge(ss, 2)
                nc.vector.scalar_tensor_tensor(simr[:, 3, :], simr[:, 3, :], SIM_SCALE, rn, ALU.mult, ALU.mult).then_inc(ss, 1)
                nc.vector.scalar_tensor_tensor(simr[:, 4, :], rn, SIM_SCALE, dd, ALU.mult, ALU.mult).then_inc(ss, 1)
                dve.wait_ge(ss, 4)
                nc.vector.memset(simr[:, 1, :], 0.0).then_inc(ss, 1)
                dve.wait_ge(ss, 5)
                nc.vector.tensor_tensor(simr[:, 1, 1:D], simr[:, 4, 1:D], simr[:, 2, 0:D - 1], ALU.mult).then_inc(ss, 1)
                dve.wait_ge(ss, 6)
                nc.vector.memset(simr[:, 0, :], 0.0).then_inc(ss, 1)
                dve.wait_ge(ss, 7)
                nc.vector.tensor_copy(simr[:, 0, 0:D - 1], simr[:, 1, 1:D]).then_inc(ss, 1)
                dve.wait_ge(ss, 8)
                for g, src in enumerate((1, 3, 0)):
                    nc.vector.tensor_copy(sim_h[32 * g:32 * g + 32, :], simr[:, src, :]).then_inc(ss, 1)
                for g, src in enumerate((1, 3, 0)):
                    dve.wait_ge(ss, 9 + g)
                    nc.vector.tensor_copy(simr[:, 4, :], sim_h[32 * g:32 * g + 32, :]).then_inc(ss, 1)
                    dve.wait_ge(ss, 12 + 2 * g)
                    nc.vector.tensor_tensor(sim_l[32 * g:32 * g + 32, :], simr[:, src, :], simr[:, 4, :],
                                            ALU.subtract).then_inc(ss, 1)
                    dve.wait_ge(ss, 13 + 2 * g)

                def taps(t, par):
                    normalise(dve, 0, t, fpad[:, par, 1:D + 1], sem("x0_xn"))
                    dve.wait_ge(sem("x0_xn"), t + 1)
                    dve.wait_ge(sem("x0_sel"), t + 1)
                    for k in range(TAPS):
                        nc.vector.scalar_tensor_tensor(fs[:, k, :], fpad[:, par, k:k + D], 1.0 / SIM_SCALE, bk(k),
                                                       ALU.mult, ALU.mult).then_inc(sem("x0_fs"), 1)
                    dve.wait_ge(sem("x0_conv"), t + 1)
                    nc.vector.tensor_tensor(x[:, t, :], x[:, t, :], bk(3), ALU.add).then_inc(sem("x0_x"), 1)
                    dve.wait_ge(sem("x0_x"), t + 1)
                    hold(dve)
                    stats(dve, 1, t)
                all_tiles(dve, taps)

                def ffn(ph, gate, steps):
                    q = LNQ[ph]

                    def norm(t, par):
                        normalise(dve, q, t, xn[:, par, :], sem(f"{ph}_xn"))

                    norm(0, 0)

                    def body(t, par, last):
                        dve.wait_ge(sem(f"{ph}_h"), t + 1)
                        gate(t, par, steps * t)
                        if not last:
                            norm(t + 1, 1 - par)
                        dve.wait_ge(sem(f"{ph}_out"), t + 1)
                        dve.wait_ge(sem(f"{ph}_biased"), t + 1)
                        nc.vector.tensor_tensor(x[:, t, :], x[:, t, :], bk(2 + par), ALU.add).then_inc(sem(f"{ph}_x"), 1)
                        dve.wait_ge(sem(f"{ph}_x"), t + 1)
                        hold(dve)
                        stats(dve, q + 1, t)
                    tiles_with_last(dve, body)

                def gate0(t, par, n):
                    s, hb, g = sem("f0_gate"), bk(4 + par), gs[:, par, :]
                    hr = E0 * R0
                    nc.vector.reduce_max(g[:, 0:1], hb[:, hr:hr + E0], AX.X, negate=True).then_inc(s, 1)
                    dve.wait_ge(sem("f0_exp"), 2 * t + 2)
                    nc.vector.tensor_scalar(g[:, 2:3], g[:, 32:33], 1.0, None, ALU.add).then_inc(s, 1)
                    nc.vector.reciprocal(g[:, 3:4], g[:, 1:2]).then_inc(s, 1)
                    dve.wait_ge(s, n + 3)
                    nc.vector.reciprocal(g[:, 4:5], g[:, 2:3]).then_inc(s, 1)
                    dve.wait_ge(s, n + 4)
                    nc.vector.tensor_scalar(g[:, 5:6], g[:, 4:5], MAX_THR, None, ALU.mult).then_inc(s, 1)
                    dve.wait_ge(s, n + 5)
                    nc.vector.tensor_scalar(g[:, 16:24], g[:, 8:16], g[:, 3:4], g[:, 5:6], ALU.mult,
                                            ALU.subtract).then_inc(s, 1)
                    dve.wait_ge(s, n + 6)
                    nc.vector.tensor_scalar(g[:, 24:32], g[:, 16:24], 0.0, None, ALU.max).then_inc(s, 1)
                    dve.wait_ge(s, n + 7)
                    nc.vector.reduce_sum(g[:, 6:7], g[:, 24:32], AX.X).then_inc(s, 1)
                    dve.wait_ge(s, n + 8)
                    nc.vector.scalar_tensor_tensor(g[:, 7:8], g[:, 6:7], 0.0, g[:, 6:7], ALU.is_equal, ALU.add).then_inc(s, 1)
                    dve.wait_ge(s, n + 9)
                    nc.vector.reciprocal(g[:, 40:41], g[:, 7:8]).then_inc(s, 1)
                    dve.wait_ge(s, n + 10)
                    nc.vector.tensor_scalar(g[:, 48:56], g[:, 24:32], g[:, 40:41], LORA_SCALE, ALU.mult,
                                            ALU.mult).then_inc(s, 1)
                    dve.wait_ge(s, n + 11)
                    nc.vector.tensor_tensor(hw[:, par, :].rearrange("p (e r) -> p e r", e=E0),
                                            hb[:, 0:hr].rearrange("p (e r) -> p e r", e=E0),
                                            g[:, 48:56].unsqueeze(2).broadcast_to([P, E0, R0]), ALU.mult).then_inc(
                                                sem("f0_hw"), 1)

                def gate1(t, par, n):
                    s, hb, g = sem("f1_gate"), bk(4 + par), gs[:, par, :]
                    hr = E0 * R0
                    nc.vector.tensor_tensor(g[:, 16:16 + NR1], hb[:, hr:hr + NR1], rb1[:], ALU.add).then_inc(s, 1)
                    dve.wait_ge(s, n + 1)
                    nc.vector.reduce_max(g[:, 0:1], g[:, 16:16 + NR1], AX.X, negate=True).then_inc(s, 1)
                    dve.wait_ge(sem("f1_exp"), t + 1)
                    nc.vector.reciprocal(g[:, 3:4], g[:, 1:2]).then_inc(s, 1)
                    nc.vector.max(g[:, 8:16], g[:, 32:32 + NR1]).then_inc(s, 1)
                    dve.wait_ge(s, n + 4)
                    hold(dve)
                    nc.vector.match_replace(g[:, 48:48 + NR1], g[:, 8:16], g[:, 32:32 + NR1], -1.0).then_inc(s, 1)
                    dve.wait_ge(s, n + 5)
                    nc.vector.scalar_tensor_tensor(g[:, 48:48 + NR1], g[:, 48:48 + NR1], 0.0, g[:, 32:32 + NR1],
                                                   ALU.is_lt, ALU.mult).then_inc(s, 1)
                    dve.wait_ge(s, n + 6)
                    nc.vector.tensor_tensor(tmp15[:], emap[:], g[:, 48:48 + NR1].unsqueeze(1).broadcast_to([P, E0, NR1]),
                                            ALU.mult).then_inc(s, 1)
                    dve.wait_ge(s, n + 7)
                    nc.vector.reduce_sum(g[:, 8:16], tmp15[:], AX.X).then_inc(s, 1)
                    dve.wait_ge(s, n + 8)
                    nc.vector.tensor_scalar(g[:, 16:24], g[:, 8:16], g[:, 3:4], LORA_SCALE, ALU.mult, ALU.mult).then_inc(s, 1)
                    dve.wait_ge(s, n + 9)
                    nc.vector.tensor_tensor(hw[:, par, :].rearrange("p (e r) -> p e r", e=E0),
                                            hb[:, 0:hr].rearrange("p (e r) -> p e r", e=E0),
                                            g[:, 16:24].unsqueeze(2).broadcast_to([P, E0, R0]), ALU.mult).then_inc(
                                                sem("f1_hw"), 1)

                def gate2(t, par, n):
                    s, hb, g = sem("f2_gate"), bk(4 + par), gs[:, par, :]
                    nc.vector.tensor_tensor(g[:, 0:4], hb[:, R2:R2 + 4], gb2[:], ALU.add).then_inc(s, 1)
                    dve.wait_ge(s, n + 1)
                    nc.vector.tensor_tensor(g[:, 4:5], g[:, 0:1], g[:, 1:2], ALU.max).then_inc(s, 1)
                    nc.vector.tensor_tensor(g[:, 5:6], g[:, 2:3], g[:, 3:4], ALU.max).then_inc(s, 1)
                    dve.wait_ge(s, n + 3)
                    nc.vector.tensor_tensor(g[:, 6:7], g[:, 4:5], g[:, 2:3], ALU.max).then_inc(s, 1)
                    nc.vector.tensor_tensor(g[:, 7:8], g[:, 5:6], g[:, 1:2], ALU.max).then_inc(s, 1)
                    nc.vector.tensor_tensor(g[:, 10:11], g[:, 5:6], g[:, 4:5], ALU.is_gt).then_inc(s, 1)
                    dve.wait_ge(s, n + 5)
                    nc.vector.tensor_tensor(g[:, 9:10], g[:, 7:8], g[:, 0:1], ALU.is_gt).then_inc(s, 1)
                    nc.vector.tensor_tensor(g[:, 11:12], g[:, 3:4], g[:, 6:7], ALU.is_gt).then_inc(s, 1)
                    dve.wait_ge(s, n + 8)
                    nc.vector.tensor_copy(hw[:, par, 0:RANK_CUTS[1]], hb[:, 0:RANK_CUTS[1]]).then_inc(s, 1)
                    for c in range(1, 4):
                        lo, hi = RANK_CUTS[c], RANK_CUTS[c + 1]
                        last = nc.vector.tensor_scalar(hw[:, par, lo:hi], hb[:, lo:hi], g[:, 8 + c:9 + c], None, ALU.mult)
                        last.then_inc(s if c < 3 else sem("f2_hw"), 1)

                dve.wait_ge(sem("ld_small"), 80)
                nc.vector.tensor_scalar(nbthr[:, 1:2], nbthr[:, 0:1], -1.0, None, ALU.mult).then_inc(sem("nbthr"), 1)
                ffn("f0", gate0, 11)

                def kmax(t, par, i):
                    dve.wait_ge(sem(f"ld_x1_{par}"), 32 * i + 32)
                    nc.vector.reduce_max(sm[:, par, 0:1], erow[:, par, :], AX.X, negate=True).then_inc(sem("x1_kmax"), 1)

                def lin(t, par, i):
                    kmax(t, par, i)
                    dve.wait_ge(sem("x1_ek"), t + 1)
                    nc.vector.reciprocal(sm[:, par, 2:3], sm[:, par, 1:2]).then_inc(sem("x1_rk"), 1)
                    dve.wait_ge(sem("x1_kv"), t + 1)
                    dve.wait_ge(sem("x1_rk"), t + 1)
                    nc.vector.scalar_tensor_tensor(kvm[:, par, :], ps[:, 2, 0:P], sm[:, par, 2:3], g8[:], ALU.mult,
                                                   ALU.mult).then_inc(sem("x1_kvm"), 1)
                    dve.wait_ge(sem("x1_nd"), t + 1)
                    nc.vector.reciprocal(xn[:, par, :], bk(4)).then_inc(sem("x1_fin"), 1)
                    dve.wait_ge(sem("x1_fin"), 3 * t + 1)
                    nc.vector.tensor_tensor(xn[:, par, :], xn[:, par, :], bk(3), ALU.mult).then_inc(sem("x1_fin"), 1)
                    dve.wait_ge(sem("x1_fin"), 3 * t + 2)
                    nc.vector.tensor_tensor(x[:, t, :], x[:, t, :], xn[:, par, :], ALU.add).then_inc(sem("x1_fin"), 1)
                    dve.wait_ge(sem("x1_fin"), 3 * t + 3)
                    hold(dve)
                    stats(dve, 3, t)
                with dve.Fori(0, TILES // 2) as i:
                    for par in range(2):
                        lin(2 * i + par, par, i)

                nc.vector.tensor_copy(emap_f[:], emap_i[:]).then_inc(sem("emap"), 1)
                dve.wait_ge(sem("emap"), 1)
                for e in range(E0):
                    nc.vector.tensor_scalar(emap[:, e, :], emap_f[:], float(e), None, ALU.is_equal).then_inc(sem("emap"), 1)
                dve.wait_ge(sem("emap"), 1 + E0)
                ffn("f1", gate1, 9)

                def chan(t, par, last):
                    for b in range(BT):
                        if b == 0:
                            dve.wait_ge(sem("x2_s"), t + 1)
                        r = slice(b * C, (b + 1) * C)
                        nc.vector.reduce_max(sm[r, par, 0:1], ps[r, 2, b * C:(b + 1) * C], AX.X).then_inc(sem("x2_m"), 1)
                    dve.wait_ge(sem("x2_m"), 3 * t + 2)
                    nc.vector.tensor_scalar(sm[:, par, 1:2], sm[:, par, 0:1], -float(C) ** -0.5, None,
                                            ALU.mult).then_inc(sem("x2_m"), 1)
                    dve.wait_ge(sem("x2_e"), 2 * t + 2)
                    nc.vector.reciprocal(sm[:, par, 3:4], sm[:, par, 2:3]).then_inc(sem("x2_r"), 1)
                    dve.wait_ge(sem("x2_r"), 2 * t + 1)
                    nc.vector.tensor_scalar(pmat[:, par, :], pmat[:, par, :], sm[:, par, 3:4], None,
                                            ALU.mult).then_inc(sem("x2_r"), 1)
                    if not last:
                        normalise(dve, 4, t + 1, xn[:, 1 - par, :], sem("x2_xn"))
                    dve.wait_ge(sem("x2_out"), t + 1)
                    nc.vector.tensor_tensor(x[:, t, :], x[:, t, :], bk(3), ALU.add).then_inc(sem("x2_x"), 1)
                    dve.wait_ge(sem("x2_x"), t + 1)
                    hold(dve)
                    stats(dve, 5, t)
                normalise(dve, 4, 0, xn[:, 0, :], sem("x2_xn"))
                tiles_with_last(dve, chan)
                ffn("f2", gate2, 11)

            @block.scalar
            def _(act):
                def squares(t, par, i):
                    act.wait_ge(sem(f"ld_e0_{par}"), 16 * i + 16)
                    after(act, sem("sim_mm"), t - 1)
                    nc.scalar.activation(ebuf[:, par, :], erow[:, par, :], ACT.Square).then_inc(sem("sq_done"), 1)
                squares(0, 0, 0)
                squares(1, 1, 0)
                with act.Fori(1, TILES // 2) as i:
                    for par in range(2):
                        squares(2 * i + par, par, i)

                def xt_copy(ph, t, par):
                    act.wait_ge(sem(f"{ph}_tr"), t + 1)
                    nc.scalar.activation(xnT[:, par].rearrange("p k n -> p (k n)"), bk(par), ACT.Copy).then_inc(
                        sem(f"{ph}_xnT"), 1)

                def ffn(ph, gate):
                    xt_copy(ph, 0, 0)

                    def body(t, par, last):
                        gate(t, par)
                        act.wait_ge(sem(f"{ph}_hwTr"), t + 1)
                        nc.scalar.activation(hwT[0:RK[ph], par, :], ps[0:RK[ph], 4 + par, 256:384], ACT.Copy).then_inc(
                            sem(f"{ph}_hwT"), 1)
                        if not last:
                            xt_copy(ph, t + 1, 1 - par)
                    tiles_with_last(act, body)

                def gate0(t, par):
                    g, hb, hr = gs[:, par, :], bk(4 + par), E0 * R0
                    act.wait_ge(sem("f0_gate"), 11 * t + 1)
                    nc.scalar.activation(g[:, 8:16], hb[:, hr:hr + E0], ACT.Exp, bias=g[:, 0:1], accum_out=g[:, 1:2]).then_inc(
                        sem("f0_exp"), 1)
                    nc.scalar.activation(g[:, 32:33], hb[:, hr + E0:hr + E0 + 1], ACT.Exp, bias=nbthr[:, 1:2],
                                         scale=-1.0).then_inc(sem("f0_exp"), 1)

                def gate1(t, par):
                    g = gs[:, par, :]
                    act.wait_ge(sem("f1_gate"), 9 * t + 2)
                    nc.scalar.activation(g[:, 32:32 + NR1], g[:, 16:16 + NR1], ACT.Exp, bias=g[:, 0:1],
                                         accum_out=g[:, 1:2]).then_inc(sem("f1_exp"), 1)

                act.wait_ge(sem("nbthr"), 1)
                ffn("f0", gate0)

                def lin(t, par, last):
                    act.wait_ge(sem("x1_kmax"), t + 1)
                    nc.scalar.activation(ebuf2[:, par, :], erow[:, par, :], ACT.Exp, bias=sm[:, par, 0:1],
                                         accum_out=sm[:, par, 1:2]).then_inc(sem("x1_ek"), 1)
                    act.wait_ge(sem("nmr_steps"), 2 * t + 2)
                    nc.scalar.activation(ebuf[:, par, :], x[:, t, :], ACT.Exp, bias=col(nmr, t),
                                         scale=col(rstd[:, 0, :], t)).then_inc(sem("x1_eq"), 1)
                    act.wait_ge(sem("x1_tr"), t + 1)
                    nc.scalar.activation(xnT[:, par].rearrange("p k n -> p (k n)"), bk(par), ACT.Copy).then_inc(
                        sem("x1_ekT"), 1)
                tiles_with_last(act, lin)
                ffn("f1", gate1)

                xt_copy("x2", 0, 0)

                def chan(t, par, last):
                    act.wait_ge(sem("x2_m"), 3 * t + 3)
                    for b in range(BT):
                        r, cs = slice(b * C, (b + 1) * C), slice(b * C, (b + 1) * C)
                        nc.scalar.activation(pmat[r, par, cs], ps[r, 2, cs], ACT.Exp, bias=sm[r, par, 1:2],
                                             scale=float(C) ** -0.5, accum_out=sm[r, par, 2:3]).then_inc(sem("x2_e"), 1)
                    if not last:
                        xt_copy("x2", t + 1, 1 - par)
                tiles_with_last(act, chan)
                ffn("f2", lambda t, par: None)

            @block.tensor
            def _(pe):
                pe.wait_ge(sem("ld_pick"), 16)
                for t in range(TILES):
                    par = t % 2
                    pe.wait_ge(sem("sq_done"), t + 1)
                    nc.tensor.matmul(ps[0:32, 0, :], pick[:, t, :], ebuf[:, par, :], start=t == 0, stop=t == TILES - 1)
                    pe.wait_ge(sem("dp_done"), t + 1)
                    nc.tensor.matmul(ps[0:32, 1, :], pick[:, t, :], ebuf2[:, par, :], start=t == 0,
                                     stop=t == TILES - 1).then_inc(sem("sim_mm"), 1)
                pe.wait_ge(sem("ld_conv"), 48)
                pe.wait_ge(sem("sim_steps"), 17)

                def conv(t, par):
                    after(pe, sem("x0_fs"), TAPS * t)
                    for k in range(TAPS):
                        sel = csel[0:96, t, k, :]
                        nc.tensor.matmul(bk(k), sel, sim_h[:, :], start=True, stop=False)
                        last = nc.tensor.matmul(bk(k), sel, sim_l[:, :], start=False, stop=True)
                    last.then_inc(sem("x0_sel"), 1)
                    pe.wait_ge(sem("x0_fs"), TAPS * t + TAPS)
                    after(pe, sem("x0_x"), t)
                    for k in range(TAPS):
                        last = nc.tensor.matmul(bk(3), convw[:, k, :], fs[:, k, :], start=k == 0, stop=k == TAPS - 1)
                    last.then_inc(sem("x0_conv"), 1)
                all_tiles(pe, conv)

                def ffn(ph):
                    n, rk, hcols = sem(f"{ph}_xnT"), RK[ph], HC[ph]

                    def rows(t, par):
                        pe.wait_ge(sem(f"{ph}_xn"), t + 1)
                        transpose4(bk(par), xn[:, par, :]).then_inc(sem(f"{ph}_tr"), 1)

                    rows(0, 0)

                    def body(t, par, last_tile):
                        pe.wait_ge(n, t + 1)
                        after(pe, sem(f"{ph}_x"), t - 1)
                        for k in range(KD):
                            last = nc.tensor.matmul(ps[:, 4 + par, 0:hcols], xnT[:, par, k, :], wag[ph][:, k, :],
                                                    start=k == 0, stop=k == KD - 1)
                        last.then_inc(sem(f"{ph}_h"), 1)
                        for k in range(KD):
                            nc.tensor.matmul(bk(2 + par), xnT[:, par, k, :], wbase[ph][:, k, :], start=k == 0, stop=False)
                        alone(pe)
                        pe.wait_ge(sem(f"{ph}_hw"), t + 1)
                        nc.tensor.transpose(ps[0:rk, 4 + par, 256:384], hw[:, par, 0:rk], ident[:, :]).then_inc(
                            sem(f"{ph}_hwTr"), 1)
                        if not last_tile:
                            rows(t + 1, 1 - par)
                        pe.wait_ge(sem(f"{ph}_hwT"), t + 1)
                        nc.tensor.matmul(bk(2 + par), hwT[0:rk, par, :], wb[ph][0:rk, :], start=False,
                                         stop=True).then_inc(sem(f"{ph}_out"), 1)
                    tiles_with_last(pe, body)

                pe.wait_ge(sem("ld_f0"), 64)
                ffn("f0")

                def lin(t, par, i):
                    pe.wait_ge(sem("x1_ek"), t + 1)
                    after(pe, sem("x1_ekT"), t)
                    transpose4(bk(par), ebuf2[:, par, :]).then_inc(sem("x1_tr"), 1)
                    pe.wait_ge(sem(f"ld_x1_{par}"), 32 * i + 32)
                    pe.wait_ge(sem("x1_ekT"), t + 1)
                    after(pe, sem("x1_kvm"), t)
                    for k in range(KD):
                        last = nc.tensor.matmul(ps[:, 2, 0:P], xnT[:, par, k, :], eT[:, par, k, :], start=k == 0,
                                                stop=k == KD - 1)
                    last.then_inc(sem("x1_kv"), 1)
                    pe.wait_ge(sem("x1_eq"), t + 1)
                    after(pe, sem("x1_fin"), 3 * t)
                    nc.tensor.matmul(bk(4), g8[:, :], ebuf[:, par, :], start=True, stop=True)
                    pe.wait_ge(sem("x1_kvm"), t + 1)
                    nc.tensor.matmul(bk(3), kvm[:, par, :], ebuf[:, par, :], start=True, stop=True).then_inc(sem("x1_nd"), 1)
                pe.wait_ge(sem("ld_small"), 80)
                pe.wait_ge(sem("f0_x"), TILES)
                lin(0, 0, 0)
                lin(1, 1, 0)
                with pe.Fori(1, TILES // 2) as i:
                    for par in range(2):
                        lin(2 * i + par, par, i)
                pe.wait_ge(sem("x1_fin"), 3 * TILES)
                pe.wait_ge(sem("ld_f1"), 64)
                ffn("f1")

                def rows2(t, par):
                    pe.wait_ge(sem("x2_xn"), t + 1)
                    transpose4(bk(par), xn[:, par, :]).then_inc(sem("x2_tr"), 1)

                def chan(t, par, i, last_tile):
                    pe.wait_ge(sem("x2_xnT"), t + 1)
                    pe.wait_ge(sem(f"ld_x2_{par}"), 32 * i + 32)
                    after(pe, sem("x2_e"), 2 * t)
                    for k in range(KD):
                        last = nc.tensor.matmul(ps[:, 2, 0:P], xnT[:, par, k, :], eT[:, par, k, :], start=k == 0,
                                                stop=k == KD - 1)
                    last.then_inc(sem("x2_s"), 1)
                    if not last_tile:
                        rows2(t + 1, 1 - par)
                    pe.wait_ge(sem("x2_r"), 2 * t + 2)
                    after(pe, sem("x2_x"), t)
                    nc.tensor.matmul(bk(3), pmat[:, par, :], erow[:, par, :], start=True, stop=True).then_inc(
                        sem("x2_out"), 1)
                pe.wait_ge(sem("f1_x"), TILES)
                rows2(0, 0)
                chan(0, 0, 0, False)
                chan(1, 1, 0, False)
                with pe.Fori(1, TILES // 2 - 1) as i:
                    for par in range(2):
                        chan(2 * i + par, par, i, False)
                chan(TILES - 2, 0, TILES // 2 - 1, False)
                chan(TILES - 1, 1, TILES // 2 - 1, True)
                pe.wait_ge(sem("x2_x"), TILES)
                pe.wait_ge(sem("ld_f2"), 64)
                ffn("f2")

        G3, J3, RG = 16, 4, 4
        ROUNDS = G3 // RG
        OPC = 256
        VW = 26
        NQ, NK, NV, NO = 6, 5, 5, 4
        LATE_FC = 4
        LATE = (3 * FC - LATE_FC) * D
        FG, FU, FD = (wide[:, n * FC * D:(n + 1) * FC * D] for n in range(3))
        with ExitStack() as c2:
            def s2(name, shape, dt=F32):
                return sb(name, shape, dt, c2)
            xn = s2("xn3", [P, D])
            xT = s2("xT3", [P, KD, P])
            eT = s2("eT3", [P, 2, KD, P])
            p32 = s2("p32", [P, J3, RG, C])
            pth = s2("pth", [P, 2 * J3, P], F16)
            ptl = s2("ptl", [P, 2 * J3, P], F16)
            qT = s2("qT", [P, 2, G3, P], F16)
            kT = s2("kT", [P, 2, G3, P], F16)
            qrow = s2("qrow", [P, HEADS, 4, DK3], F16)
            krow = s2("krow", [P, HEADS, 4, DK3], F16)
            t32 = s2("t32", [P, 2, D])
            vc = s2("vc", [P, HEADS, 3, DK3], BF16)
            vd = s2("vd", [P, BT, G3 // 2, J3, 2, VW], BF16)
            orow = s2("orow", [P, D])
            osum = s2("osum", [P, 4 * RG, DK3])
            irep = s2("irep", [P, KD, M3])
            b3 = wide[:, LATE:LATE + 3 * D].rearrange("p (w n) -> p w n", w=3)
            bo = wide[:, LATE + 3 * D:LATE + 4 * D]
            pf = p32[:].rearrange("p j g k -> p (j g k)")
            tmix = pf[:, 0:KD * P].rearrange("p (c n) -> p c n", c=KD)
            m4 = pf[:, KD * P:(KD + 1) * P]
            ip = pf[:, (KD + 1) * P:(KD + 2) * P]
            amp = s2("amp", [P, 1])
            am = s2("am", [P, 16])
            sc = s2("sc", [P, 2])
            mx = s2("mx", [P, J3 * RG])
            rden = s2("rden", [P, 4 * RG])
            block = c2.enter_context(nc.Block())
            PAIRS = TILES // 2

            def schedule(eng, body):
                body(0, 0, 0, True, False)
                body(1, 1, 0, False, False)
                with eng.Fori(1, PAIRS - 1) as i:
                    for par in range(2):
                        body(2 * i + par, par, i, False, False)
                body(TILES - 2, 0, PAIRS - 1, False, False)
                body(TILES - 1, 1, PAIRS - 1, False, True)

            @block.sync
            def _(sp):
                sp.dma_start(irep[:], a["irep"].rearrange("(k p) n -> p k n", p=P)).then_inc(sem("ld_mix"), 16)
                sp.dma_start(m4, a["c_m4"]).then_inc(sem("ld_mix"), 16)
                sp.dma_start(ip, a["c_ip"]).then_inc(sem("ld_mix"), 16)
                sp.dma_start(amp[:], a["amp"].partition_broadcast(P)).then_inc(sem("ld_mix"), 16)
                sp.dma_start(ident16[:], a["c_ident16"]).then_inc(sem("ld_mix"), 16)
                for par in range(2):
                    sp.dma_start(eT[:, par], ctxTv[par]).then_inc(sem(f"ld_x3_{par}"), 16)
                sp.dma_start(FG.bitcast(I32).rearrange("p (k n) -> p k n", k=KD),
                             a["gate_t"].rearrange("(k p) n -> p k n", p=P)).then_inc(sem("ld_ffn"), 16)
                sp.wait_ge(sem("fold_mm"), 15)
                sp.dma_start(FU.bitcast(I32).rearrange("p (k n) -> p k n", k=KD),
                             a["up_t"].rearrange("(k p) n -> p k n", p=P)).then_inc(sem("ld_ffn"), 16)
                sp.dma_start(bo, a["bo3"].partition_broadcast(P)).then_inc(sem("ld_bo"), 16)
                sp.dma_start(FD.bitcast(I32).rearrange("p (k n) -> p k n", k=FC)[:, 0:FC - LATE_FC],
                             a["down_t"].rearrange("(k p) n -> p k n", p=P)[:, 0:FC - LATE_FC]).then_inc(sem("ld_ffn"), 16)

                def more(t, par):
                    sp.wait_ge(sem("x3_v"), t - 1)
                    sp.dma_start(eT[:, par], ctxTv[t]).then_inc(sem(f"ld_x3_{par}"), 16)
                all_tiles(sp, more, 2)

            @block.gpsimd
            def _(pool):
                nc.gpsimd.memset(qrow[:, :, 3, :], 0.0).then_inc(sem("zeros3"), 1)
                nc.gpsimd.memset(krow[:, :, 3, :], 0.0).then_inc(sem("zeros3"), 1)
                nc.gpsimd.memset(vd[:].rearrange("p b g j h w -> p (b g j h w)"), 0.0).then_inc(sem("zeros3"), 1)
                pool.wait_ge(sem("zeros3"), 3)
                for hd in range(2):
                    r = slice(hd * C, (hd + 1) * C)
                    nc.gpsimd.memset(vd[r].rearrange("p b g j h w -> p (b g j) h w")[:, :, hd, 24:25], 1.0).then_inc(
                        sem("zeros3"), 1)
                pool.wait_ge(sem("ld_bo"), 16)

                def kmax(t):
                    pool.wait_ge(sem("k_steps"), NK * t + 2)
                    hold_pool()
                    nc.gpsimd.partition_all_reduce(am[:, 9:10], am[:, 8:9], P, RMAX).then_inc(sem("k_all"), 1)

                def body(t, par, pair, first, last, conv):
                    pool.wait_ge(sem("x3_xn"), t + 1)
                    nc.gpsimd.tensor_tensor(x[:, t, :], x[:, t, :], bo, ALU.add).then_inc(sem("x3_biased"), 1)
                    if not last:
                        kmax(t + 1)
                    if not first:
                        pool_rstd(pool, 7, t - 1)
                    if conv is not None:
                        n = LATE // (TILES // 2)
                        at = slice(conv * n, (conv + 1) * n) if isinstance(conv, int) else bass.ds(conv * n, n)
                        nc.gpsimd.tensor_copy(wide[:, at], wide[:, at].bitcast(I32)).then_inc(sem("converted"), 1)
                kmax(0)
                body(0, 0, 0, True, False, None)
                body(1, 1, 0, False, False, None)
                with pool.Fori(1, PAIRS // 2) as i:
                    for par in range(2):
                        body(2 * i + par, par, i, False, False, None)
                pool.wait_ge(sem("ld_ffn"), 48)
                with pool.Fori(PAIRS // 2, PAIRS - 1) as i:
                    for par in range(2):
                        body(2 * i + par, par, i, False, False, 2 * i + par - TILES // 2)
                body(TILES - 2, 0, 0, False, False, TILES // 2 - 2)
                body(TILES - 1, 1, 0, False, True, TILES // 2 - 1)
                pool_rstd(pool, 7, TILES - 1)

            @block.vector
            def _(dve):
                ms = sem("mix_steps")
                dve.wait_ge(sem("ld_mix"), 80)
                nc.vector.tensor_scalar(irep[:], irep[:], amp[:, 0:1], 0.1, ALU.mult, ALU.mult).then_inc(ms, 1)
                dve.wait_ge(ms, 1)
                for c in range(KD):
                    nc.vector.tensor_tensor(tmix[:, c, :].rearrange("p (h m d) -> p h m d", h=4, m=M3),
                                            irep[:, c, :].unsqueeze(1).unsqueeze(3).broadcast_to([P, 4, M3, DK3]),
                                            m4.rearrange("p (h m d) -> p h m d", h=4, m=M3), ALU.mult).then_inc(ms, 1)
                dve.wait_ge(ms, 1 + KD)
                for c in range(KD):
                    nc.vector.tensor_tensor(tmix[:, c, :], tmix[:, c, :], ip, ALU.add).then_inc(ms, 1)
                for n in range(1, 15, 2):
                    dve.wait_ge(sem("fold_mm"), n + 1)
                    dst = wf[:, n // 4, n % 4, :] if n < 12 else b3[:, n - 12, :]
                    nc.vector.tensor_copy(dst, bk(n % 8)).then_inc(sem("fold_dve"), 1)
                dve.wait_ge(sem("fold_act"), 8)
                dve.wait_ge(sem("fold_dve"), 7)
                dve.wait_ge(sem("zeros3"), 5)

                def norm(t):
                    normalise(dve, 6, t, xn[:], sem("x3_xn"))

                def heads(v):
                    return v.rearrange("p (h d) -> p h d", d=DK3)

                def q_ops(t, par):
                    s, n = sem("q_steps"), NQ * t
                    dve.wait_ge(sem("x3_q"), t + 1)
                    nc.vector.tensor_tensor(t32[:, 0, :], bk(6), b3[:, 0, :], ALU.add).then_inc(s, 1)
                    dve.wait_ge(s, n + 1)
                    nc.vector.tensor_reduce(am[:, 0:1], t32[:, 0, :], AX.X, ALU.max, apply_absolute_value=True).then_inc(s, 1)
                    dve.wait_ge(s, n + 2)
                    nc.vector.tensor_scalar(am[:, 1:2], am[:, 0:1], 1e-30, 1.0 / SPLIT_TOP, ALU.max, ALU.mult).then_inc(s, 1)
                    dve.wait_ge(s, n + 3)
                    nc.vector.reciprocal(am[:, 2:3], am[:, 1:2]).then_inc(s, 1)
                    nc.vector.scalar_tensor_tensor(sc[:, par:par + 1], am[:, 1:2], float(DK3) ** -0.5, am[:, 10:11],
                                                   ALU.mult, ALU.mult).then_inc(s, 1)
                    dve.wait_ge(s, n + 4)
                    dve.wait_ge(sem("q_hi"), t + 1)
                    nc.vector.scalar_tensor_tensor(qrow[:, :, 2, :], heads(t32[:, 0, :]), am[:, 2:3], qrow[:, :, 0, :],
                                                   ALU.mult, ALU.subtract).then_inc(s, 1)

                def k_ops(t):
                    s, n = sem("k_steps"), NK * t
                    dve.wait_ge(sem("x3_k"), t + 1)
                    nc.vector.tensor_tensor(t32[:, 1, :], bk(6), b3[:, 1, :], ALU.add).then_inc(s, 1)
                    dve.wait_ge(s, n + 1)
                    nc.vector.tensor_reduce(am[:, 8:9], t32[:, 1, :], AX.X, ALU.max, apply_absolute_value=True).then_inc(s, 1)
                    dve.wait_ge(sem("k_all"), t + 1)
                    nc.vector.tensor_scalar(am[:, 10:11], am[:, 9:10], 1e-30, 1.0 / SPLIT_TOP, ALU.max, ALU.mult).then_inc(s, 1)
                    dve.wait_ge(s, n + 3)
                    nc.vector.reciprocal(am[:, 11:12], am[:, 10:11]).then_inc(s, 1)
                    dve.wait_ge(sem("k_hi"), t + 1)
                    dve.wait_ge(s, n + 4)
                    nc.vector.scalar_tensor_tensor(krow[:, :, 1, :], heads(t32[:, 1, :]), am[:, 11:12], krow[:, :, 0, :],
                                                   ALU.mult, ALU.subtract).then_inc(s, 1)

                def v_ops(t):
                    s, n = sem("v_steps"), NV * t
                    dve.wait_ge(sem("q_steps"), NQ * t + NQ)
                    dve.wait_ge(sem("x3_v"), t + 1)
                    nc.vector.tensor_tensor(t32[:, 0, :], bk(6), b3[:, 2, :], ALU.add).then_inc(s, 1)
                    dve.wait_ge(s, n + 1)
                    nc.vector.tensor_copy(vc[:, :, 0, :], heads(t32[:, 0, :])).then_inc(s, 1)
                    dve.wait_ge(s, n + 2)
                    nc.vector.tensor_tensor(heads(t32[:, 1, :]), heads(t32[:, 0, :]), vc[:, :, 0, :], ALU.subtract).then_inc(s, 1)
                    dve.wait_ge(s, n + 3)
                    nc.vector.tensor_copy(vc[:, :, 1, :], heads(t32[:, 1, :])).then_inc(s, 1)
                    dve.wait_ge(s, n + 4)
                    nc.vector.tensor_tensor(vc[:, :, 2, :], heads(t32[:, 1, :]), vc[:, :, 1, :], ALU.subtract).then_inc(s, 1)

                def vd_ops(t):
                    dve.wait_ge(sem("v_steps"), NV * t + NV)
                    for b in range(BT):
                        for hd in range(2):
                            src = vc[b * C:(b + 1) * C].rearrange("p (g h j) m d -> p g h (j m d)", h=2, j=J3)[:, :, hd, :]
                            dst = vd[hd * C:(hd + 1) * C, b, :, :, hd, 0:24]
                            nc.vector.tensor_copy(dst, src.rearrange("p g (j w) -> p g j w", j=J3)).then_inc(sem("x3_vd"), 1)

                def out_norm(rr, r, t):
                    so = sem("o_steps")
                    if r == 0:
                        after(dve, sem("x3_otr"), t)
                    for n in range(2):
                        o = ps[:, n, OPC:OPC + 4 * 2 * VW].rearrange("p (h w) -> p h w", w=VW)
                        nc.vector.reciprocal(rden[:, 8 * n:8 * n + 8], o[:, :, 24]).then_inc(so, 1)
                        nc.vector.tensor_reduce(osum[:, 8 * n:8 * n + 8, :],
                                                o[:, :, 0:24].rearrange("p h (m d) -> p h d m", m=3), AX.X,
                                                ALU.add).then_inc(so, 1)
                    dve.wait_ge(so, (NO + 1) * rr + NO)
                    dst = orow[:, r * RG * 32:(r + 1) * RG * 32].rearrange("p (g j d) -> p j g d", g=RG, j=J3)
                    nc.vector.tensor_tensor(dst, osum[:].rearrange("p (j g) d -> p j g d", j=J3),
                                            rden[:].rearrange("p (j g) -> p j g", j=J3).unsqueeze(3).broadcast_to(
                                                [P, J3, RG, DK3]), ALU.mult).then_inc(so, 1)

                def finish(t):
                    dve.wait_ge(sem("x3_wo"), t + 1)
                    dve.wait_ge(sem("x3_biased"), t + 1)
                    nc.vector.tensor_tensor(x[:, t, :], x[:, t, :], bk(6), ALU.add).then_inc(sem("x3_x"), 1)
                    dve.wait_ge(sem("x3_x"), t + 1)
                    hold(dve)
                    stats(dve, 7, t)

                norm(0)
                k_ops(0)
                q_ops(0, 0)
                v_ops(0)

                def body(t, par, pair, first, last):
                    for r in range(ROUNDS):
                        rr = ROUNDS * t + r
                        s_ps = ps[:, 0:J3, 0:RG * C].rearrange("p j (g k) -> p j g k", g=RG)
                        dve.wait_ge(sem("x3_s"), rr + 1)
                        nc.vector.tensor_reduce(mx[:].rearrange("p (j g) -> p j g", j=J3), s_ps, AX.X, ALU.max).then_inc(
                            sem("x3_max"), 1)
                        dve.wait_ge(sem("x3_max"), rr + 1)
                        for j in range(J3):
                            last_sub = nc.vector.tensor_tensor(
                                p32[:, j], s_ps[:, j], mx[:, j * RG:(j + 1) * RG].unsqueeze(2).broadcast_to([P, RG, C]),
                                ALU.subtract)
                        last_sub.then_inc(sem("x3_sub"), 1)
                        if not (first and r == 0):
                            out_norm(rr - 1, (r - 1) % ROUNDS, t)
                        dve.wait_ge(sem("x3_pt"), rr + 1)
                        dve.wait_ge(sem("x3_pth"), rr + 1)
                        nc.vector.scalar_tensor_tensor(ptl[:].rearrange("p n q -> p (n q)"),
                                                       ps[:, 4:6, :].rearrange("p b n -> p (b n)"), P_SCALE,
                                                       pth[:].rearrange("p n q -> p (n q)"), ALU.mult,
                                                       ALU.subtract).then_inc(sem("x3_ptl"), 1)
                        if r == 0:
                            vd_ops(t)
                            if not last:
                                k_ops(t + 1)
                                norm(t + 1)
                        elif r == 1 and not first:
                            finish(t - 1)
                        elif r == 2 and not last:
                            q_ops(t + 1, 1 - par)
                        elif r == 3 and not last:
                            v_ops(t + 1)
                schedule(dve, body)
                dve.wait_ge(sem("x3_pv"), ROUNDS * TILES)
                out_norm(ROUNDS * TILES - 1, ROUNDS - 1, TILES)
                finish(TILES - 1)

            @block.scalar
            def _(act):
                for n in range(0, 15, 2):
                    act.wait_ge(sem("fold_mm"), n + 1)
                    dst = wf[:, n // 4, n % 4, :] if n < 12 else b3[:, n - 12, :]
                    nc.scalar.activation(dst, bk(n % 8), ACT.Copy).then_inc(sem("fold_act"), 1)

                def xT_copy(tr, k, done):
                    act.wait_ge(sem(tr), k)
                    nc.scalar.activation(xT[:].rearrange("p k n -> p (k n)"), bk(7), ACT.Copy).then_inc(sem(done), 1)

                def hi(row, lo_part, src, scale, steps, need, done):
                    act.wait_ge(sem(steps), need)
                    dst = row[:, :, 0:2, :] if lo_part == 2 else row[:, :, 0:3:2, :]
                    nc.scalar.activation(dst, src.rearrange("p (h d) -> p h d", d=DK3).unsqueeze(2).broadcast_to(
                        [P, HEADS, 2, DK3]), ACT.Copy, scale=scale).then_inc(sem(done), 1)

                def q_hi(t):
                    hi(qrow, 2, t32[:, 0, :], am[:, 2:3], "q_steps", NQ * t + 4, "q_hi")

                def k_hi(t):
                    hi(krow, 1, t32[:, 1, :], am[:, 11:12], "k_steps", NK * t + 4, "k_hi")

                def t_copy(dst, par, n, tr, t, done):
                    act.wait_ge(sem(tr), 2 * t + n + 1)
                    nc.scalar.activation(dst[:, par, 8 * n:8 * n + 8, :].rearrange("p g n -> p (g n)"),
                                         bk(7).bitcast(F16), ACT.Copy).then_inc(sem(done), 1)

                act.wait_ge(sem("zeros3"), 5)
                xT_copy("x3_tr", 1, "x3_xT")
                k_hi(0)
                t_copy(kT, 0, 0, "x3_ktr", 0, "x3_kT")
                q_hi(0)
                t_copy(kT, 0, 1, "x3_ktr", 0, "x3_kT")
                t_copy(qT, 0, 0, "x3_qtr", 0, "x3_qT")
                t_copy(qT, 0, 1, "x3_qtr", 0, "x3_qT")

                def body(t, par, pair, first, last):
                    nxt = 1 - par
                    for r in range(ROUNDS):
                        rr = ROUNDS * t + r
                        if r == 0 and not first:
                            xT_copy("x3_otr", t, "x3_oT")
                        if r == 2 and not last:
                            t_copy(kT, nxt, 0, "x3_ktr", t + 1, "x3_kT")
                        act.wait_ge(sem("x3_sub"), rr + 1)
                        nc.scalar.activation(pf, pf, ACT.Exp, scale=sc[:, par:par + 1]).then_inc(sem("x3_exp"), 1)
                        if r == 3 and not last:
                            t_copy(qT, nxt, 0, "x3_qtr", t + 1, "x3_qT")
                        act.wait_ge(sem("x3_pt"), rr + 1)
                        nc.scalar.activation(pth[:].rearrange("p n q -> p (n q)"),
                                             ps[:, 4:6, :].rearrange("p b n -> p (b n)"), ACT.Copy,
                                             scale=P_SCALE).then_inc(sem("x3_pth"), 1)
                        if not last:
                            if r == 0:
                                k_hi(t + 1)
                            elif r == 1:
                                xT_copy("x3_tr", t + 2, "x3_xT")
                            elif r == 2:
                                t_copy(kT, nxt, 1, "x3_ktr", t + 1, "x3_kT")
                                q_hi(t + 1)
                            else:
                                t_copy(qT, nxt, 1, "x3_qtr", t + 1, "x3_qT")
                schedule(act, body)
                xT_copy("x3_otr", TILES, "x3_oT")

            @block.tensor
            def _(pe):
                pe.wait_ge(sem("f2_x"), TILES)
                pe.wait_ge(sem("ld_w3"), 48)
                pe.wait_ge(sem("mix_steps"), 1 + 2 * KD)
                for n in range(15):
                    if n >= 8:
                        m = n - 8
                        pe.wait_ge(sem("fold_dve" if m % 2 else "fold_act"), m // 2 + 1)
                    for c in range(KD):
                        w = wnat[:, n // 4, c, n % 4 * P:n % 4 * P + P] if n < 12 else b3rep[:, n - 12, c, :]
                        last = nc.tensor.matmul(ps[:, n % 8, c * P:(c + 1) * P], w, tmix[:, c, :], start=True, stop=True)
                    last.then_inc(sem("fold_mm"), 1)
                pe.wait_ge(sem("fold_act"), 8)
                pe.wait_ge(sem("fold_dve"), 7)

                def project(lhs, w, done):
                    for k in range(KD):
                        last = nc.tensor.matmul(bk(6), lhs[:, k, :], w[:, k, :], start=k == 0, stop=k == KD - 1)
                    last.then_inc(sem(done), 1)

                def rows(t):
                    pe.wait_ge(sem("x3_xn"), t + 1)
                    transpose4(bk(7), xn[:, :]).then_inc(sem("x3_tr"), 1)

                def q_mm(t):
                    pe.wait_ge(sem("x3_xT"), t + 1)
                    project(xT, wf[:, 0], "x3_q")

                def k_mm(t, par, pair):
                    pe.wait_ge(sem(f"ld_x3_{par}"), 16 * pair + 16)
                    project(eT[:, par], wf[:, 1], "x3_k")

                def v_mm(t, par):
                    pe.wait_ge(sem("q_steps"), NQ * t + 1)
                    project(eT[:, par], wf[:, 2], "x3_v")

                def stack_tr(row, n, done):
                    for g in range(8):
                        h = 4 * (8 * n + g)
                        last = nc.tensor.transpose(bk(7).bitcast(F16)[:, g * P:(g + 1) * P],
                                                   row[:, h:h + 4].rearrange("p h m d -> p (h m d)"), ident16[:, :])
                    last.then_inc(sem(done), 1)

                def k_tr(t, n):
                    if n == 0:
                        pe.wait_ge(sem("k_steps"), NK * t + NK)
                        pe.wait_ge(sem("x3_xT"), t + 1)
                    else:
                        pe.wait_ge(sem("x3_kT"), 2 * t + 1)
                    stack_tr(krow, n, "x3_ktr")

                def q_tr(t, n):
                    if n == 0:
                        pe.wait_ge(sem("q_steps"), NQ * t + NQ)
                        pe.wait_ge(sem("x3_kT"), 2 * t + 2)
                    else:
                        pe.wait_ge(sem("x3_qT"), 2 * t + 1)
                    stack_tr(qrow, n, "x3_qtr")

                def pv(rr, r, t):
                    pe.wait_ge(sem("x3_pth"), rr + 1)
                    pe.wait_ge(sem("x3_ptl"), rr + 1)
                    after(pe, sem("o_steps"), (NO + 1) * rr)
                    if r == 0:
                        pe.wait_ge(sem("x3_vd"), 4 * t + 4)
                    for j in range(J3):
                        for u in range(2):
                            n = 2 * j + u
                            c = OPC + n % 4 * 2 * VW
                            for b in range(BT):
                                for pt in (pth, ptl):
                                    last = nc.tensor.matmul(
                                        ps[b * C:(b + 1) * C, n // 4, c:c + 2 * VW], pt[:, n, b * C:(b + 1) * C],
                                        vd[:, b, 2 * r + u, j].rearrange("p h w -> p (h w)"), start=pt is pth, stop=pt is ptl)
                    last.then_inc(sem("x3_pv"), 1)

                def o_tr(t):
                    pe.wait_ge(sem("o_steps"), (NO + 1) * ROUNDS * (t + 1))
                    transpose4(bk(7), orow[:, :]).then_inc(sem("x3_otr"), 1)

                def wo_mm(t):
                    pe.wait_ge(sem("x3_oT"), t + 1)
                    project(xT, wo, "x3_wo")

                rows(0)
                k_mm(0, 0, 0)
                k_tr(0, 0)
                pe.wait_ge(sem("k_steps"), 1)
                q_mm(0)
                k_tr(0, 1)
                v_mm(0, 0)
                q_tr(0, 0)
                q_tr(0, 1)

                def body(t, par, pair, first, last):
                    nxt = 1 - par
                    npair = pair + 1 if par else pair
                    for r in range(ROUNDS):
                        rr = ROUNDS * t + r
                        after(pe, sem("x3_sub"), rr)
                        if not (first and r == 0):
                            pv(rr - 1, (r - 1) % ROUNDS, t)
                        if r == 0:
                            pe.wait_ge(sem("x3_qT"), 2 * t + 2)
                        for g in range(RG):
                            for b in range(BT):
                                for j in range(J3):
                                    rows_j, cols_b = slice(32 * j, 32 * j + 32), slice(b * C, (b + 1) * C)
                                    mm = nc.tensor.matmul(ps[cols_b, j, g * C:(g + 1) * C],
                                                          qT[rows_j, par, RG * r + g, cols_b],
                                                          kT[rows_j, par, RG * r + g, cols_b], start=True, stop=True)
                        mm.then_inc(sem("x3_s"), 1)
                        if r == 0:
                            if not first:
                                o_tr(t - 1)
                            if not last:
                                pe.wait_ge(sem("v_steps"), NV * t + 1)
                                k_mm(t + 1, nxt, npair)
                        elif r == 1:
                            if not first:
                                if last:
                                    pe.wait_ge(sem("v_steps"), NV * t + 1)
                                else:
                                    pe.wait_ge(sem("k_steps"), NK * (t + 1) + 1)
                                wo_mm(t - 1)
                        elif r == 2 and not last:
                            k_tr(t + 1, 0)
                            if first:
                                pe.wait_ge(sem("k_steps"), NK * (t + 1) + 1)
                            else:
                                pe.wait_ge(sem("x3_x"), t)
                            q_mm(t + 1)
                        elif r == 3 and not last:
                            v_mm(t + 1, nxt)
                            q_tr(t + 1, 0)
                        pe.wait_ge(sem("x3_exp"), rr + 1)
                        after(pe, sem("x3_ptl"), rr)
                        for j in range(J3):
                            for u in range(2):
                                n = 2 * j + u
                                mm = nc.tensor.transpose(ps[:, 4 + n // 4, n % 4 * P:(n % 4 + 1) * P],
                                                         p32[:, j, 2 * u:2 * u + 2, :].rearrange("p g k -> p (g k)"),
                                                         ident[:, :])
                        mm.then_inc(sem("x3_pt"), 1)
                        if not last:
                            if r == 1:
                                if not first:
                                    pe.wait_ge(sem("x3_oT"), t)
                                rows(t + 1)
                            elif r == 2:
                                k_tr(t + 1, 1)
                            elif r == 3:
                                q_tr(t + 1, 1)
                schedule(pe, body)
                pv(ROUNDS * TILES - 1, ROUNDS - 1, TILES)
                pe.wait_ge(sem("x3_x"), TILES - 1)
                o_tr(TILES - 1)
                wo_mm(TILES - 1)

        GT = 4
        GROUPS = TILES // GT
        with ExitStack() as c3:
            def s3(name, shape, dt=F32):
                return sb(name, shape, dt, c3)
            xn = s3("xn8", [P, GT, D])
            xT = s3("xT8", [P, KD, GT * P])
            sg = s3("sg", [P, 2, GT * P])
            hid = s3("hid", [P, 2, GT * P])
            scaled = s3("scaled", [P, 2, D])
            gsc = s3("gsc", [P, FC])
            usc = s3("usc", [P, FC])
            dsc = s3("dsc", [P, D])
            block = c3.enter_context(nc.Block())
            gate_w = FG.rearrange("p (k n) -> p k n", k=KD)
            up_w = FU.rearrange("p (k n) -> p k n", k=KD)
            down_w = FD.rearrange("p (k n) -> p k n", k=FC)

            def groups(eng, body):
                body(0, False)
                with eng.Fori(1, GROUPS - 1) as g:
                    body(g, False)
                body(GROUPS - 1, True)

            @block.sync
            def _(sp):
                sp.dma_start(gsc[:], a["gate_s"]).then_inc(sem("ld_scales"), 16)
                sp.dma_start(usc[:], a["up_s"]).then_inc(sem("ld_scales"), 16)
                sp.dma_start(dsc[:], a["down_s"].partition_broadcast(P)).then_inc(sem("ld_scales"), 16)
                sp.wait_ge(sem("x3_x"), TILES)
                sp.dma_start(down_w[:, FC - LATE_FC:].bitcast(I32),
                             a["down_t"].rearrange("(k p) n -> p k n", p=P)[:, FC - LATE_FC:]).then_inc(sem("ld_late"), 16)
                with sp.Fori(0, TILES) as t:
                    sp.wait_ge(sem("f3_x"), 2 * t + 2)
                    sp.dma_start(outv[t], x[:, t, :]).then_inc(sem("stored"), 16)
                sp.wait_ge(sem("stored"), 16 * TILES)

            @block.gpsimd
            def _(pool):
                pool.wait_ge(sem("ld_late"), 16)
                nc.gpsimd.tensor_copy(wide[:, LATE:], wide[:, LATE:].bitcast(I32)).then_inc(sem("converted"), 1)

            @block.vector
            def _(dve):
                def norms(g):
                    for j in range(GT):
                        normalise(dve, 7, GT * g + j, xn[:, j, :], sem("f3_xn"))
                norms(0)
                dve.wait_ge(sem("ld_scales"), 48)

                def body(g, last):
                    for f in range(FC):
                        n = FC * g + f
                        dve.wait_ge(sem("f3_gu"), n + 1)
                        dve.wait_ge(sem("f3_silu"), n + 1)
                        nc.vector.scalar_tensor_tensor(hid[:, f % 2, :], bk(5 + 2 * (f % 2)), usc[:, f:f + 1], sg[:, f % 2, :],
                                                       ALU.mult, ALU.mult).then_inc(sem("f3_hid"), 1)
                        if f == FC // 2 and not last:
                            norms(g + 1)
                    for j in range(GT):
                        t = GT * g + j
                        dve.wait_ge(sem("f3_down"), t + 1)
                        nc.vector.tensor_tensor(scaled[:, j % 2, :], bk(j), dsc[:], ALU.mult).then_inc(sem("f3_x"), 1)
                        dve.wait_ge(sem("f3_x"), 2 * t + 1)
                        nc.vector.tensor_tensor(x[:, t, :], x[:, t, :], scaled[:, j % 2, :], ALU.add).then_inc(sem("f3_x"), 1)
                groups(dve, body)

            @block.scalar
            def _(act):
                def xT_copy(g):
                    for j in range(GT):
                        act.wait_ge(sem("f3_tr"), GT * g + j + 1)
                        nc.scalar.activation(xT[:, :, j * P:(j + 1) * P], bk(4 + j).rearrange("p (k n) -> p k n", k=KD),
                                             ACT.Copy).then_inc(sem("f3_xT"), 1)
                xT_copy(0)
                act.wait_ge(sem("ld_scales"), 48)

                def body(g, last):
                    for f in range(FC):
                        act.wait_ge(sem("f3_gu"), FC * g + f + 1)
                        if f >= 2:
                            act.wait_ge(sem("f3_hid"), FC * g + f - 1)
                        nc.scalar.activation(sg[:, f % 2, :], bk(4 + 2 * (f % 2)), ACT.Silu, scale=gsc[:, f:f + 1]).then_inc(
                            sem("f3_silu"), 1)
                    if not last:
                        xT_copy(g + 1)
                groups(act, body)

            @block.tensor
            def _(pe):
                pe.wait_ge(sem("x3_x"), TILES)
                pe.wait_ge(sem("converted"), TILES // 2)

                def rows(g, j):
                    pe.wait_ge(sem("f3_xn"), GT * g + j + 1)
                    transpose4(bk(4 + j), xn[:, j, :]).then_inc(sem("f3_tr"), 1)

                def gate_up(g, f):
                    for w, b in ((gate_w, 4 + 2 * (f % 2)), (up_w, 5 + 2 * (f % 2))):
                        for k in range(KD):
                            last = nc.tensor.matmul(bk(b), w[:, k, f * P:(f + 1) * P], xT[:, k, :], start=k == 0,
                                                    stop=k == KD - 1)
                    last.then_inc(sem("f3_gu"), 1)

                def down(g, f):
                    pe.wait_ge(sem("f3_hid"), FC * g + f + 1)
                    if f == FC - LATE_FC:
                        pe.wait_ge(sem("converted"), TILES // 2 + 1)
                    for j in range(GT):
                        mm = nc.tensor.matmul(bk(j), hid[:, f % 2, j * P:(j + 1) * P], down_w[:, f, :], start=f == 0,
                                              stop=f == FC - 1)
                        if f == FC - 1:
                            mm.then_inc(sem("f3_down"), 1)

                for j in range(GT):
                    rows(0, j)

                def body(g, last):
                    pe.wait_ge(sem("f3_xT"), GT * g + GT)
                    gate_up(g, 0)
                    gate_up(g, 1)
                    after(pe, sem("f3_x"), 2 * GT * g)
                    for f in range(FC):
                        down(g, f)
                        if f + 2 < FC:
                            gate_up(g, f + 2)
                        elif not last:
                            for j in (0, 1) if f + 2 == FC else (2, 3):
                                rows(g + 1, j)
                groups(pe, body)


_CORE_INPUTS = ["x", "ctx"]


def kernel(**inputs):
    import numpy as np
    import concourse.bacc as bacc
    from concourse.bass_utils import run_bass_kernel_spmd

    v = {k: np.asarray(w) for k, w in inputs.items()}
    f32 = np.float32
    tiles, kd = TILES, KD
    ctx = v["ctx_4096"].reshape(B * C, D)
    ar = {
        "x": v["x"].reshape(B * C, D),
        "ctx": ctx,
        "ctxT": ctx.reshape(tiles, P, kd, P).transpose(0, 3, 2, 1),
        "f0_base": v["L0_ffn_W_base"].T,
        "f0_ag": np.concatenate([v["L0_ffn_A_w"].reshape(E0 * R0, D), v["L0_ffn_W_gate"], v["L0_ffn_W_thr"][None]]).T,
        "f0_b": v["L0_ffn_B_w"].transpose(0, 2, 1).reshape(E0 * R0, D),
        "f0_bias": v["L0_ffn_b_base"],
        "thr_b": v["L0_ffn_b_thr"],
        "f1_base": v["L1_ffn_base_W"].T,
        "f1_ag": np.concatenate([v["L1_ffn_A"].reshape(E0 * R0, D), v["L1_ffn_router_W"]]).T,
        "f1_b": v["L1_ffn_B"].transpose(0, 2, 1).reshape(E0 * R0, D),
        "f1_bias": v["L1_ffn_base_b"],
        "router_b": v["L1_ffn_router_b"],
        "expert_map": v["L1_ffn_expert_map"],
        "f2_base": v["L2_ffn_W"].T,
        "f2_ag": np.concatenate([v["L2_ffn_A"], v["L2_ffn_gate_w"]]).T,
        "f2_b": v["L2_ffn_B"].T,
        "f2_bias": v["L2_ffn_b"],
        "gate_b2": v["L2_ffn_gate_b"],
        "w3": np.stack([v["L3_xattn_Wq"], v["L3_xattn_Wk"], v["L3_xattn_Wv"]]),
        "b3rep": np.stack([np.repeat(v[f"L3_xattn_b{c}"][:, None], P, 1) for c in "qkv"]),
        "wo3": v["L3_xattn_Wo"].T.reshape(H3, DK3, M3, D).transpose(0, 2, 1, 3).reshape(D, D),
        "bo3": v["L3_xattn_bo"],
        "irep": np.repeat(v["L3_xattn_interference"][:, None], DK3, 1).reshape(D, M3),
        "amp": v["L3_xattn_amp"],
        "gate_t": v["L3_ffn_gate_t"].T,
        "up_t": v["L3_ffn_up_t"].T,
        "down_t": v["L3_ffn_down_t"].T,
        "gate_s": v["L3_ffn_gate_s"].reshape(FC, P).T,
        "up_s": v["L3_ffn_up_s"].reshape(FC, P).T,
        "down_s": v["L3_ffn_down_s"],
    }
    w = v["L0_xattn_weight"].transpose(1, 2, 0)
    conv = np.zeros((BT, C, TAPS, BT, C), f32)
    for b in range(BT):
        conv[b, :, :, b, :] = w
    ar["convw"] = conv.reshape(P, TAPS, P)
    ar["c_ident"] = np.eye(P, dtype=f32)
    ar["c_ident16"] = np.eye(P, dtype=np.float16)
    ar["c_g8"] = np.kron(np.eye(P // 8), np.ones((8, 8))).astype(f32)
    pick = np.zeros((P, tiles, B), f32)
    for t in range(tiles):
        for b in range(BT):
            pick[b * C:(b + 1) * C, t, BT * t + b] = 1
    ar["c_pick"] = pick
    sel = np.zeros((TAPS, B, tiles, TAPS, BT, C), np.float16)
    for t in range(tiles):
        for b in range(BT):
            for k in range(TAPS):
                for c in range(C):
                    sel[(TAPS * c + k) // C, BT * t + b, t, k, b, c] = 1
    ar["c_sel"] = sel.reshape(TAPS * B, tiles, TAPS, P)
    hdi = np.arange(P)
    h_in, d_in, m_in = hdi // 32, hdi // 4 % 8, hdi % 4
    h_out, m_out, d_out = hdi // 32, hdi // 8 % 4, hdi % 8
    same = (h_in[:, None] == h_out) & (d_in[:, None] == d_out)
    ar["c_m4"] = same.astype(f32)
    ar["c_ip"] = (same & (m_in[:, None] == m_out)).astype(f32)

    nc = bacc.Bacc("TRN2", target_bir_lowering=False, num_devices=1)
    arrays, dram = {}, {}
    for name, arr in ar.items():
        arr = np.ascontiguousarray(arr)
        arrays[f"in_{name}"] = arr
        dram[name] = nc.dram_tensor(f"in_{name}", arr.shape, mybir.dt.from_np(arr.dtype), kind="ExternalInput").ap()
    out = nc.dram_tensor("out", (B * C, D), F32, kind="ExternalOutput").ap()
    xattn_ffn_program(nc, dram, out)
    r = run_bass_kernel_spmd(nc, [arrays], core_ids=[0])
    return np.asarray(r.results[0]["out"]).reshape(B, C, D)
```

```python
import concourse.bass as bass
from concourse import mybir
from contextlib import ExitStack

F32 = mybir.dt.float32
F16 = mybir.dt.float16
BF16 = mybir.dt.bfloat16
I32 = mybir.dt.int32
ALU = mybir.AluOpType
ACT = mybir.ActivationFunctionType
AX = mybir.AxisListType

P = 128
B, C, D = 32, 64, 512
BT = P // C
TILES = B * C // P
KD = D // P
EPS_LN = 1e-5
EPS_COS = 1e-8
TAPS = 3
SIM_SCALE = 1024.0
E0, R0 = 8, 16
LORA_SCALE = 2.0
MAX_THR = 0.125
HD1 = P // 8
NR1 = 2 * E0 - 1
R2 = 64
RANK_CUTS = [0, 8, 16, 32, 64]
H3, M3, DK3 = 16, 4, 8
HEADS = H3 * M3
FF = 1792
FC = FF // P
SPLIT_TOP = 4096.0
P_SCALE = 1024.0
RMAX = bass.bass_isa.ReduceOp.max
STAT_OPS = 3


def xattn_ffn_program(nc, a, out):
    top = ExitStack()
    sems = {}

    def sem(name):
        if name not in sems:
            sems[name] = top.enter_context(nc.semaphore(name))
        return sems[name]

    with top:
        def sb(name, shape, dt, ctx=top):
            return ctx.enter_context(nc.sbuf_tensor(name, shape, dt))

        x = sb("x", [P, TILES, D], F32)
        wide = sb("wide", [P, 3 * FC * D], F32)
        wf = sb("wf", [P, 3, KD, D], F32)
        wo = sb("wo", [P, KD, D], F32)
        ident = sb("ident", [P, P], F32)
        ident16 = sb("ident16", [P, P], F16)
        st6 = sb("st6", [P, 6], F32)
        mv2 = sb("mv2", [P, 2], F32)
        zero_eps = sb("zero_eps", [P, 2], F32)
        neg_half = sb("neg_half", [P, 2], F32)
        mean_var = sb("mean_var", [P, 2, TILES, 2], F32)
        rstd = sb("rstd", [P, 2, TILES], F32)
        nmr = sb("nmr", [P, TILES], F32)
        small = sb("small", [P, 64], F32)
        ps = top.enter_context(nc.psum_tensor("ps", [P, 8, D], F32))

        def bk(n):
            return ps[:, n, :]

        at = [0]

        def carve(shape, dt=F32):
            n = 1
            for s in shape:
                n *= s
            words = n * (2 if dt == F16 else 4) // 4
            v = wide[:, at[0]:at[0] + words]
            at[0] += words
            v = v if dt == F32 else v.bitcast(dt)
            if len(shape) == 2:
                v = v.rearrange("p (a b) -> p a b", a=shape[0])
            elif len(shape) == 3:
                v = v.rearrange("p (a b c) -> p a b c", a=shape[0], b=shape[1])
            return v

        HC = {"f0": E0 * R0 + E0 + 1, "f1": E0 * R0 + NR1, "f2": R2 + 4}
        RK = {"f0": E0 * R0, "f1": E0 * R0, "f2": R2}
        FFN = {"f0": 0, "f1": 1, "f2": 2}
        LNQ = {"x0": 0, "f0": 1, "x1": 2, "f1": 3, "x2": 4, "f2": 5, "x3": 6, "f3": 7}
        wbase = {f: carve([KD, D]) for f in HC}
        wag = {f: carve([KD, HC[f]]) for f in HC}
        wb = {f: carve([D]) for f in HC}
        bias = {f: carve([D]) for f in HC}
        wnat = carve([3, KD, D])
        b3rep = carve([3, KD, P])
        csel = carve([TILES, TAPS, P], F16)
        assert at[0] <= 3 * FC * D, at[0]

        def alone(eng):
            eng.wait_ge(sem("zeros"), 1)

        def hold(dve):
            nc.vector.memset(small[0:1, 0:1], 0.0)

        def hold_pool():
            nc.gpsimd.tensor_tensor(small[0:1, 1:2], neg_half[0:1, 0:1], neg_half[0:1, 1:2], ALU.add)

        def after(eng, s, value):
            if not isinstance(value, int) or value > 0:
                eng.wait_ge(s, value)

        def stats(dve, q, t):
            s = sem(f"stats{q}")
            nc.vector.bn_stats(st6[:, :], x[:, t, :]).then_inc(s, 1)
            dve.wait_ge(s, STAT_OPS * t + 1)
            hold(dve)
            nc.vector.bn_aggr(mv2[:, :], st6[:, :]).then_inc(s, 1)
            dve.wait_ge(s, STAT_OPS * t + 2)
            nc.vector.tensor_tensor(mean_var[:, q % 2, t, :], mv2[:, :], zero_eps[:, :], ALU.add).then_inc(s, 1)

        def pool_rstd(pool, q, t):
            pool.wait_ge(sem(f"stats{q}"), STAT_OPS * (t + 1))
            nc.gpsimd.tensor_tensor(rstd[:, q % 2, t:t + 1] if isinstance(t, int) else rstd[:, q % 2, bass.ds(t, 1)],
                                    mean_var[:, q % 2, t, 1:2], neg_half[:, 0:1], ALU.pow).then_inc(sem(f"rstd{q}"), 1)

        def col(v, t):
            return v[:, t:t + 1] if isinstance(t, int) else v[:, bass.ds(t, 1)]

        def normalise(dve, q, t, dst, done):
            dve.wait_ge(sem(f"rstd{q}"), t + 1)
            nc.vector.tensor_scalar(dst, x[:, t, :], mean_var[:, q % 2, t, 0:1], col(rstd[:, q % 2, :], t),
                                    ALU.subtract, ALU.mult).then_inc(done, 1)

        def all_tiles(eng, body, first=0, last=TILES):
            if first == 0:
                body(0, 0)
                body(1, 1)
                first = 2
            with eng.Fori(first // 2, last // 2) as i:
                for par in range(2):
                    body(2 * i + par, par)

        def pipelined(eng, body):
            for t in (0, 1):
                body(t, t, 0)
            with eng.Fori(1, TILES // 2 - 2) as i:
                for par in range(2):
                    body(2 * i + par, par, i)
            for t in range(TILES - 4, TILES):
                body(t, t % 2, t // 2)

        def inside(t):
            return not isinstance(t, int) or 0 <= t < TILES

        def loads(n, par, pair, ahead=0):
            return n * (pair + (par + ahead) // 2 + 1)

        def transpose4(dst, src, idm=ident):
            for k in range(KD):
                last = nc.tensor.transpose(dst[:, k * P:(k + 1) * P], src[:, k * P:(k + 1) * P], idm[:, :])
            return last

        xv = a["x"].rearrange("(t p) d -> t p d", p=P)
        ctxv = a["ctx"].rearrange("(t p) d -> t p d", p=P)
        ctxTv = a["ctxT"]
        outv = out.rearrange("(t p) d -> t p d", p=P)

        with ExitStack() as c1:
            def s1(name, shape, dt=F32):
                return sb(name, shape, dt, c1)
            erow = s1("erow", [P, 2, D])
            eT = s1("eT", [P, 2, KD, P])
            xn = s1("xn", [P, 2, D])
            xnT = s1("xnT", [P, 2, KD, P])
            fpad = s1("fpad", [P, 2, D + 2])
            fs = wf[:].rearrange("p w k n -> p (w k n)")[:, 0:2 * TAPS * D].rearrange("p (b k n) -> p b k n", b=2,
                                                                                      k=TAPS)
            ebuf = s1("ebuf", [P, 2, D])
            ebuf2 = s1("ebuf2", [P, 2, D])
            simr = s1("simr", [32, 5, D])
            sim_h = s1("sim_h", [96, D], F16)
            sim_l = s1("sim_l", [96, D], F16)
            pick = s1("pick", [P, TILES, B])
            convw = s1("convw", [P, TAPS, P])
            g8 = s1("g8", [P, P])
            kvm = s1("kvm", [P, 2, P])
            pmat = s1("pmat", [P, 2, P])
            hw = s1("hw", [P, 2, P])
            hwT = s1("hwT", [P, 2, P])
            gs = s1("gs", [P, 2, 64])
            sm = s1("sm", [P, 2, 8])
            tmp15 = s1("tmp15", [P, E0, NR1])
            emap = s1("emap", [P, E0, NR1])
            emap_i = s1("emap_i", [P, NR1], I32)
            emap_f = s1("emap_f", [P, NR1])
            rb1 = s1("rb1", [P, NR1])
            gb2 = s1("gb2", [P, 4])
            nbthr = s1("nbthr", [P, 2])
            block = c1.enter_context(nc.Block())

            @block.sync
            def _(sp):
                sp.dma_start(pick[:], a["c_pick"]).then_inc(sem("ld_pick"), 16)
                for par in range(2):
                    sp.dma_start(erow[:, par, :], ctxv[par]).then_inc(sem(f"ld_e0_{par}"), 16)
                for g in range(4):
                    sp.dma_start(x[:, 4 * g:4 * g + 4, :], xv[4 * g:4 * g + 4].rearrange("t p d -> p t d")).then_inc(
                        sem("ld_x"), 16)

                def load_e0(t, par):
                    sp.wait_ge(sem("sq_done"), t - 1)
                    sp.wait_ge(sem("dp_done"), t - 1)
                    sp.dma_start(erow[:, par, :], ctxv[t]).then_inc(sem(f"ld_e0_{par}"), 16)
                all_tiles(sp, load_e0, 2)
                sp.dma_start(csel[0:96], a["c_sel"]).then_inc(sem("ld_conv"), 16)
                sp.dma_start(convw[:], a["convw"]).then_inc(sem("ld_conv"), 16)
                sp.dma_start(ident[:], a["c_ident"]).then_inc(sem("ld_conv"), 16)
                sp.dma_start(nbthr[:, 0:1], a["thr_b"].partition_broadcast(P)).then_inc(sem("ld_small"), 16)
                sp.dma_start(rb1[:], a["router_b"].partition_broadcast(P)).then_inc(sem("ld_small"), 16)
                sp.dma_start(emap_i[:], a["expert_map"].partition_broadcast(P)).then_inc(sem("ld_small"), 16)
                sp.dma_start(gb2[:], a["gate_b2"].partition_broadcast(P)).then_inc(sem("ld_small"), 16)
                sp.dma_start(g8[:], a["c_g8"]).then_inc(sem("ld_small"), 16)
                for f in ("f0", "f1", "f2"):
                    w = sem(f"ld_{f}")
                    sp.dma_start(wbase[f], a[f"{f}_base"].rearrange("(k p) n -> p k n", p=P)).then_inc(w, 16)
                    sp.dma_start(wag[f], a[f"{f}_ag"].rearrange("(k p) n -> p k n", p=P)).then_inc(w, 16)
                    sp.dma_start(wb[f][0:RK[f]], a[f"{f}_b"]).then_inc(w, 16)
                    sp.dma_start(bias[f], a[f"{f}_bias"].partition_broadcast(P)).then_inc(w, 16)

                def load_rows(t, par):
                    sp.dma_start(erow[:, par, :], ctxv[t]).then_inc(sem(f"ld_rows_{par}"), 16)

                def load_T(t, par):
                    sp.dma_start(eT[:, par], ctxTv[t]).then_inc(sem(f"ld_cols_{par}"), 16)

                sp.wait_ge(sem("sq_done"), TILES)
                sp.wait_ge(sem("dp_done"), TILES)
                for par in range(2):
                    load_rows(par, par)
                    load_T(par, par)

                def more1(t, par):
                    sp.wait_ge(sem("x1_ek"), t - 1)
                    load_rows(t, par)
                    sp.wait_ge(sem("x1_kv"), t - 1)
                    load_T(t, par)
                all_tiles(sp, more1, 2)
                sp.dma_start(wnat, a["w3"].rearrange("w (k p) n -> p w k n", p=P)).then_inc(sem("ld_w3"), 16)
                sp.dma_start(wo[:], a["wo3"].rearrange("(k p) n -> p k n", p=P)).then_inc(sem("ld_w3"), 16)
                sp.dma_start(b3rep, a["b3rep"].rearrange("w (k p) n -> p w k n", p=P)).then_inc(sem("ld_w3"), 16)
                sp.wait_ge(sem("x1_ek"), TILES)
                sp.wait_ge(sem("x1_kv"), TILES)
                for par in range(2):
                    load_T(par, par)
                    load_rows(par, par)

                def more2(t, par):
                    sp.wait_ge(sem("x2_s"), t - 1)
                    load_T(t, par)
                    sp.wait_ge(sem("x2_out"), t - 1)
                    load_rows(t, par)
                all_tiles(sp, more2, 2)

            @block.gpsimd
            def _(pool):
                nc.gpsimd.memset(zero_eps[:, 0:1], 0.0)
                nc.gpsimd.memset(zero_eps[:, 1:2], EPS_LN)
                nc.gpsimd.memset(neg_half[:, 0:1], -0.5)
                nc.gpsimd.memset(neg_half[:, 1:2], -1.0)
                nc.gpsimd.memset(ebuf2[:, :, 0:1], 0.0)
                nc.gpsimd.memset(fpad[:, :, 0:1], 0.0)
                nc.gpsimd.memset(fpad[:, :, D + 1:D + 2], 0.0)
                nc.gpsimd.memset(pmat[:, :, :], 0.0).then_inc(sem("zeros"), 1)
                pool.wait_ge(sem("zeros"), 1)
                all_tiles(pool, lambda t, par: pool_rstd(pool, 0, t))
                for ph in ("x0", "f0", "x1", "f1", "x2", "f2"):
                    q = LNQ[ph]
                    if ph[0] == "f":
                        pool.wait_ge(sem(f"ld_{ph}"), 64)

                    def body(t, par, ph=ph, q=q):
                        if ph[0] == "f":
                            pool.wait_ge(sem(f"{ph}_xn"), t + 1)
                            nc.gpsimd.tensor_tensor(x[:, t, :], x[:, t, :], bias[ph], ALU.add).then_inc(
                                sem(f"{ph}_biased"), 1)
                        pool_rstd(pool, q + 1, t)
                        if q + 1 == 2:
                            alone(pool)
                            pool.wait_ge(sem("rstd2"), t + 1)
                            nc.gpsimd.tensor_tensor(col(nmr, t), mean_var[:, 0, t, 0:1], col(rstd[:, 0, :], t),
                                                    ALU.mult).then_inc(sem("nmr_steps"), 1)
                            alone(pool)
                            pool.wait_ge(sem("nmr_steps"), 2 * t + 1)
                            nc.gpsimd.tensor_tensor(col(nmr, t), col(nmr, t), neg_half[:, 1:2],
                                                    ALU.mult).then_inc(sem("nmr_steps"), 1)
                    all_tiles(pool, body)

            @block.vector
            def _(dve):
                dve.wait_ge(sem("zeros"), 1)

                def neighbours(t, par, i=None):
                    dve.wait_ge(sem(f"ld_e0_{par}"), 16 * i + 16)
                    after(dve, sem("sim_mm"), t - 1)
                    nc.vector.tensor_tensor(ebuf2[:, par, 1:D], erow[:, par, 1:D], erow[:, par, 0:D - 1],
                                            ALU.mult).then_inc(sem("dp_done"), 1)
                neighbours(0, 0, 0)
                neighbours(1, 1, 0)
                with dve.Fori(1, TILES // 2) as i:
                    for par in range(2):
                        neighbours(2 * i + par, par, i)
                dve.wait_ge(sem("ld_x"), 64)
                all_tiles(dve, lambda t, par: stats(dve, 0, t))
                ss = sem("sim_steps")
                dve.wait_ge(sem("sim_mm"), TILES)
                nn, dd = ps[0:32, 0, :], ps[0:32, 1, :]
                nc.vector.tensor_scalar(simr[:, 1, :], nn, EPS_COS * EPS_COS, None, ALU.max).then_inc(ss, 1)
                rs, rn = sem("rnorm"), simr[:, 2, :]
                dve.wait_ge(rs, 1)
                nc.vector.reciprocal(rn, simr[:, 3, :]).then_inc(rs, 1)
                dve.wait_ge(rs, 2)
                nc.vector.tensor_tensor(simr[:, 4, :], rn, rn, ALU.mult).then_inc(rs, 1)
                dve.wait_ge(rs, 3)
                nc.vector.tensor_tensor(simr[:, 4, :], simr[:, 4, :], simr[:, 1, :], ALU.mult).then_inc(rs, 1)
                dve.wait_ge(rs, 4)
                nc.vector.tensor_scalar(simr[:, 4, :], simr[:, 4, :], -0.5, 1.5, ALU.mult, ALU.add).then_inc(rs, 1)
                dve.wait_ge(rs, 5)
                nc.vector.tensor_tensor(rn, rn, simr[:, 4, :], ALU.mult).then_inc(rs, 1)
                dve.wait_ge(rs, 6)
                nc.vector.tensor_tensor(simr[:, 3, :], nn, rn, ALU.mult).then_inc(ss, 1)
                dve.wait_ge(ss, 2)
                nc.vector.scalar_tensor_tensor(simr[:, 3, :], simr[:, 3, :], SIM_SCALE, rn, ALU.mult, ALU.mult).then_inc(ss, 1)
                nc.vector.scalar_tensor_tensor(simr[:, 4, :], rn, SIM_SCALE, dd, ALU.mult, ALU.mult).then_inc(ss, 1)
                dve.wait_ge(ss, 4)
                nc.vector.memset(simr[:, 1, :], 0.0).then_inc(ss, 1)
                dve.wait_ge(ss, 5)
                nc.vector.tensor_tensor(simr[:, 1, 1:D], simr[:, 4, 1:D], simr[:, 2, 0:D - 1], ALU.mult).then_inc(ss, 1)
                dve.wait_ge(ss, 6)
                nc.vector.memset(simr[:, 0, :], 0.0).then_inc(ss, 1)
                dve.wait_ge(ss, 7)
                nc.vector.tensor_copy(simr[:, 0, 0:D - 1], simr[:, 1, 1:D]).then_inc(ss, 1)
                dve.wait_ge(ss, 8)
                for g, src in enumerate((1, 3, 0)):
                    nc.vector.tensor_copy(sim_h[32 * g:32 * g + 32, :], simr[:, src, :]).then_inc(ss, 1)
                for g, src in enumerate((1, 3, 0)):
                    dve.wait_ge(ss, 9 + g)
                    nc.vector.tensor_copy(simr[:, 4, :], sim_h[32 * g:32 * g + 32, :]).then_inc(ss, 1)
                    dve.wait_ge(ss, 12 + 2 * g)
                    nc.vector.tensor_tensor(sim_l[32 * g:32 * g + 32, :], simr[:, src, :], simr[:, 4, :],
                                            ALU.subtract).then_inc(ss, 1)
                    dve.wait_ge(ss, 13 + 2 * g)

                def taps_norm(t, par):
                    normalise(dve, 0, t, fpad[:, par, 1:D + 1], sem("x0_xn"))

                def x0_finish(t, par):
                    dve.wait_ge(sem("x0_conv"), t + 1)
                    nc.vector.tensor_tensor(x[:, t, :], x[:, t, :], bk(6 + par), ALU.add).then_inc(sem("x0_x"), 1)
                    dve.wait_ge(sem("x0_x"), t + 1)
                    hold(dve)
                    stats(dve, 1, t)

                def taps(t, par, pair):
                    dve.wait_ge(sem("x0_xn"), t + 1)
                    dve.wait_ge(sem("x0_sel"), t + 1)
                    for k in range(TAPS):
                        nc.vector.scalar_tensor_tensor(fs[:, par, k, :], fpad[:, par, k:k + D], 1.0 / SIM_SCALE,
                                                       bk(TAPS * par + k), ALU.mult, ALU.mult).then_inc(sem("x0_fs"), 1)
                    if inside(t + 1):
                        after(dve, sem("x0_fs"), TAPS * t)
                        taps_norm(t + 1, 1 - par)
                    if inside(t - 1):
                        x0_finish(t - 1, 1 - par)
                taps_norm(0, 0)
                pipelined(dve, taps)
                x0_finish(TILES - 1, 1)

                def ffn(ph, gate, steps):
                    q = LNQ[ph]

                    def norm(t, par):
                        normalise(dve, q, t, xn[:, par, :], sem(f"{ph}_xn"))

                    def gates(t, par):
                        dve.wait_ge(sem(f"{ph}_h"), t + 1)
                        gate(t, par, steps * t)

                    def finish(t, par):
                        dve.wait_ge(sem(f"{ph}_out"), t + 1)
                        dve.wait_ge(sem(f"{ph}_biased"), t + 1)
                        nc.vector.tensor_tensor(x[:, t, :], x[:, t, :], bk(2 + par), ALU.add).then_inc(sem(f"{ph}_x"), 1)
                        dve.wait_ge(sem(f"{ph}_x"), t + 1)
                        hold(dve)
                        stats(dve, q + 1, t)

                    def body(t, par, pair):
                        if inside(t + 1):
                            gates(t + 1, 1 - par)
                        if inside(t + 3):
                            norm(t + 3, 1 - par)
                        if inside(t - 1):
                            finish(t - 1, 1 - par)
                    norm(0, 0)
                    norm(1, 1)
                    gates(0, 0)
                    dve.wait_ge(sem(f"{ph}_tr"), 1)
                    norm(2, 0)
                    pipelined(dve, body)
                    finish(TILES - 1, 1)

                def gate0(t, par, n):
                    s, hb, g = sem("f0_gate"), bk(4 + par), gs[:, par, :]
                    hr = E0 * R0
                    nc.vector.reduce_max(g[:, 0:1], hb[:, hr:hr + E0], AX.X, negate=True).then_inc(s, 1)
                    dve.wait_ge(sem("f0_exp"), 2 * t + 2)
                    nc.vector.tensor_scalar(g[:, 2:3], g[:, 32:33], 1.0, None, ALU.add).then_inc(s, 1)
                    nc.vector.reciprocal(g[:, 3:4], g[:, 1:2]).then_inc(s, 1)
                    dve.wait_ge(s, n + 3)
                    nc.vector.reciprocal(g[:, 4:5], g[:, 2:3]).then_inc(s, 1)
                    dve.wait_ge(s, n + 4)
                    nc.vector.tensor_scalar(g[:, 5:6], g[:, 4:5], MAX_THR, None, ALU.mult).then_inc(s, 1)
                    dve.wait_ge(s, n + 5)
                    nc.vector.tensor_scalar(g[:, 16:24], g[:, 8:16], g[:, 3:4], g[:, 5:6], ALU.mult,
                                            ALU.subtract).then_inc(s, 1)
                    dve.wait_ge(s, n + 6)
                    nc.vector.tensor_scalar(g[:, 24:32], g[:, 16:24], 0.0, None, ALU.max).then_inc(s, 1)
                    dve.wait_ge(s, n + 7)
                    nc.vector.reduce_sum(g[:, 6:7], g[:, 24:32], AX.X).then_inc(s, 1)
                    dve.wait_ge(s, n + 8)
                    nc.vector.scalar_tensor_tensor(g[:, 7:8], g[:, 6:7], 0.0, g[:, 6:7], ALU.is_equal, ALU.add).then_inc(s, 1)
                    dve.wait_ge(s, n + 9)
                    nc.vector.reciprocal(g[:, 40:41], g[:, 7:8]).then_inc(s, 1)
                    dve.wait_ge(s, n + 10)
                    nc.vector.tensor_scalar(g[:, 48:56], g[:, 24:32], g[:, 40:41], LORA_SCALE, ALU.mult,
                                            ALU.mult).then_inc(s, 1)
                    dve.wait_ge(s, n + 11)
                    nc.vector.tensor_tensor(hw[:, par, :].rearrange("p (e r) -> p e r", e=E0),
                                            hb[:, 0:hr].rearrange("p (e r) -> p e r", e=E0),
                                            g[:, 48:56].unsqueeze(2).broadcast_to([P, E0, R0]), ALU.mult).then_inc(
                                                sem("hw_rows"), 1)

                def gate1(t, par, n):
                    s, hb, g = sem("f1_gate"), bk(4 + par), gs[:, par, :]
                    hr = E0 * R0
                    nc.vector.tensor_tensor(g[:, 16:16 + NR1], hb[:, hr:hr + NR1], rb1[:], ALU.add).then_inc(s, 1)
                    dve.wait_ge(s, n + 1)
                    nc.vector.reduce_max(g[:, 0:1], g[:, 16:16 + NR1], AX.X, negate=True).then_inc(s, 1)
                    dve.wait_ge(sem("f1_exp"), t + 1)
                    nc.vector.reciprocal(g[:, 3:4], g[:, 1:2]).then_inc(s, 1)
                    nc.vector.max(g[:, 8:16], g[:, 32:32 + NR1]).then_inc(s, 1)
                    dve.wait_ge(s, n + 4)
                    hold(dve)
                    nc.vector.match_replace(g[:, 48:48 + NR1], g[:, 8:16], g[:, 32:32 + NR1], -1.0).then_inc(s, 1)
                    dve.wait_ge(s, n + 5)
                    nc.vector.scalar_tensor_tensor(g[:, 48:48 + NR1], g[:, 48:48 + NR1], 0.0, g[:, 32:32 + NR1],
                                                   ALU.is_lt, ALU.mult).then_inc(s, 1)
                    dve.wait_ge(s, n + 6)
                    nc.vector.tensor_tensor(tmp15[:], emap[:], g[:, 48:48 + NR1].unsqueeze(1).broadcast_to([P, E0, NR1]),
                                            ALU.mult).then_inc(s, 1)
                    dve.wait_ge(s, n + 7)
                    nc.vector.reduce_sum(g[:, 8:16], tmp15[:], AX.X).then_inc(s, 1)
                    dve.wait_ge(s, n + 8)
                    nc.vector.tensor_scalar(g[:, 16:24], g[:, 8:16], g[:, 3:4], LORA_SCALE, ALU.mult, ALU.mult).then_inc(s, 1)
                    dve.wait_ge(s, n + 9)
                    nc.vector.tensor_tensor(hw[:, par, :].rearrange("p (e r) -> p e r", e=E0),
                                            hb[:, 0:hr].rearrange("p (e r) -> p e r", e=E0),
                                            g[:, 16:24].unsqueeze(2).broadcast_to([P, E0, R0]), ALU.mult).then_inc(
                                                sem("hw_rows"), 1)

                def gate2(t, par, n):
                    s, hb, g = sem("f2_gate"), bk(4 + par), gs[:, par, :]
                    nc.vector.tensor_tensor(g[:, 0:4], hb[:, R2:R2 + 4], gb2[:], ALU.add).then_inc(s, 1)
                    dve.wait_ge(s, n + 1)
                    nc.vector.tensor_tensor(g[:, 4:5], g[:, 0:1], g[:, 1:2], ALU.max).then_inc(s, 1)
                    nc.vector.tensor_tensor(g[:, 5:6], g[:, 2:3], g[:, 3:4], ALU.max).then_inc(s, 1)
                    dve.wait_ge(s, n + 3)
                    nc.vector.tensor_tensor(g[:, 6:7], g[:, 4:5], g[:, 2:3], ALU.max).then_inc(s, 1)
                    nc.vector.tensor_tensor(g[:, 7:8], g[:, 5:6], g[:, 1:2], ALU.max).then_inc(s, 1)
                    nc.vector.tensor_tensor(g[:, 10:11], g[:, 5:6], g[:, 4:5], ALU.is_gt).then_inc(s, 1)
                    dve.wait_ge(s, n + 5)
                    nc.vector.tensor_tensor(g[:, 9:10], g[:, 7:8], g[:, 0:1], ALU.is_gt).then_inc(s, 1)
                    nc.vector.tensor_tensor(g[:, 11:12], g[:, 3:4], g[:, 6:7], ALU.is_gt).then_inc(s, 1)
                    dve.wait_ge(s, n + 8)
                    nc.vector.tensor_copy(hw[:, par, 0:RANK_CUTS[1]], hb[:, 0:RANK_CUTS[1]]).then_inc(s, 1)
                    for c in range(1, 4):
                        lo, hi = RANK_CUTS[c], RANK_CUTS[c + 1]
                        last = nc.vector.tensor_scalar(hw[:, par, lo:hi], hb[:, lo:hi], g[:, 8 + c:9 + c], None, ALU.mult)
                        last.then_inc(s if c < 3 else sem("hw_rows"), 1)

                dve.wait_ge(sem("ld_small"), 80)
                nc.vector.tensor_scalar(nbthr[:, 1:2], nbthr[:, 0:1], -1.0, None, ALU.mult).then_inc(sem("nbthr"), 1)
                ffn("f0", gate0, 11)

                def kmax(t, par, count):
                    dve.wait_ge(sem(f"ld_rows_{par}"), count)
                    nc.vector.reduce_max(sm[:, par, 0:1], erow[:, par, :], AX.X, negate=True).then_inc(sem("x1_kmax"), 1)

                def rk(t, par):
                    dve.wait_ge(sem("x1_ek"), t + 1)
                    nc.vector.reciprocal(sm[:, par, 2:3], sm[:, par, 1:2]).then_inc(sem("x1_rk"), 1)

                def x1_finish(t, par):
                    dve.wait_ge(sem("x1_rd"), t + 1)
                    nc.vector.tensor_tensor(xn[:, par, :], xn[:, par, :], bk(4 + par), ALU.mult).then_inc(sem("x1_fin"), 1)
                    dve.wait_ge(sem("x1_fin"), 2 * t + 1)
                    nc.vector.tensor_tensor(x[:, t, :], x[:, t, :], xn[:, par, :], ALU.add).then_inc(sem("x1_fin"), 1)
                    dve.wait_ge(sem("x1_fin"), 2 * t + 2)
                    hold(dve)
                    stats(dve, 3, t)

                def lin(t, par, pair):
                    dve.wait_ge(sem("x1_kv"), t + 1)
                    dve.wait_ge(sem("x1_rk"), t + 1)
                    nc.vector.scalar_tensor_tensor(kvm[:, par, :], ps[:, 2 + par, 0:P], sm[:, par, 2:3], g8[:], ALU.mult,
                                                   ALU.mult).then_inc(sem("x1_kvm"), 1)
                    dve.wait_ge(sem("x1_den"), t + 1)
                    nc.vector.reciprocal(gs[:, par, :], ps[:, par, 0:KD * HD1]).then_inc(sem("x1_rden"), 1)
                    if inside(t + 2):
                        kmax(t + 2, par, loads(16, par, pair, 2))
                    if inside(t + 1):
                        rk(t + 1, 1 - par)
                    if inside(t - 1):
                        x1_finish(t - 1, 1 - par)
                kmax(0, 0, 16)
                kmax(1, 1, 16)
                rk(0, 0)
                pipelined(dve, lin)
                x1_finish(TILES - 1, 1)

                nc.vector.tensor_copy(emap_f[:], emap_i[:]).then_inc(sem("emap"), 1)
                dve.wait_ge(sem("emap"), 1)
                for e in range(E0):
                    nc.vector.tensor_scalar(emap[:, e, :], emap_f[:], float(e), None, ALU.is_equal).then_inc(sem("emap"), 1)
                dve.wait_ge(sem("emap"), 1 + E0)
                ffn("f1", gate1, 9)

                def x2_norm(t, par):
                    normalise(dve, 4, t, xn[:, par, :], sem("x2_xn"))

                def x2_max(t, par):
                    dve.wait_ge(sem("x2_s"), t + 1)
                    for b in range(BT):
                        r = slice(b * C, (b + 1) * C)
                        nc.vector.reduce_max(sm[r, par, 0:1], ps[r, 2 + par, b * C:(b + 1) * C], AX.X).then_inc(
                            sem("x2_m"), 1)
                    dve.wait_ge(sem("x2_m"), 3 * t + 2)
                    nc.vector.tensor_scalar(sm[:, par, 1:2], sm[:, par, 0:1], -float(C) ** -0.5, None,
                                            ALU.mult).then_inc(sem("x2_m"), 1)

                def x2_scale(t, par):
                    dve.wait_ge(sem("x2_e"), 2 * t + 2)
                    nc.vector.reciprocal(sm[:, par, 3:4], sm[:, par, 2:3]).then_inc(sem("x2_r"), 1)
                    dve.wait_ge(sem("x2_r"), 2 * t + 1)
                    nc.vector.tensor_scalar(pmat[:, par, :], pmat[:, par, :], sm[:, par, 3:4], None,
                                            ALU.mult).then_inc(sem("x2_r"), 1)

                def x2_finish(t, par):
                    dve.wait_ge(sem("x2_out"), t + 1)
                    nc.vector.tensor_tensor(x[:, t, :], x[:, t, :], bk(4 + par), ALU.add).then_inc(sem("x2_x"), 1)
                    dve.wait_ge(sem("x2_x"), t + 1)
                    hold(dve)
                    stats(dve, 5, t)

                def chan(t, par, pair):
                    if inside(t + 1):
                        x2_max(t + 1, 1 - par)
                    if inside(t - 1):
                        x2_finish(t - 1, 1 - par)
                    if inside(t + 1):
                        x2_scale(t + 1, 1 - par)
                    if inside(t + 3):
                        x2_norm(t + 3, 1 - par)
                x2_norm(0, 0)
                x2_norm(1, 1)
                x2_max(0, 0)
                x2_scale(0, 0)
                dve.wait_ge(sem("x2_tr"), 1)
                x2_norm(2, 0)
                pipelined(dve, chan)
                x2_finish(TILES - 1, 1)
                ffn("f2", gate2, 11)

            @block.scalar
            def _(act):
                def squares(t, par, i):
                    act.wait_ge(sem(f"ld_e0_{par}"), 16 * i + 16)
                    after(act, sem("sim_mm"), t - 1)
                    nc.scalar.activation(ebuf[:, par, :], erow[:, par, :], ACT.Square).then_inc(sem("sq_done"), 1)
                squares(0, 0, 0)
                squares(1, 1, 0)
                with act.Fori(1, TILES // 2) as i:
                    for par in range(2):
                        squares(2 * i + par, par, i)

                act.wait_ge(sem("sim_steps"), 1)
                nc.scalar.activation(simr[:, 3, :], simr[:, 1, :], ACT.Sqrt).then_inc(sem("rnorm"), 1)

                def xt_copy(ph, t, par):
                    act.wait_ge(sem(f"{ph}_tr"), t + 1)
                    nc.scalar.activation(xnT[:, par].rearrange("p k n -> p (k n)"), bk(par), ACT.Copy).then_inc(
                        sem(f"{ph}_xnT"), 1)

                def ffn(ph, gate):
                    def body(t, par, pair):
                        if inside(t + 1):
                            gate(t + 1, 1 - par)
                        act.wait_ge(sem("hwTr"), TILES * FFN[ph] + t + 1)
                        nc.scalar.activation(hwT[0:RK[ph], par, :], ps[0:RK[ph], 4 + par, 256:384], ACT.Copy).then_inc(
                            sem("hwT"), 1)
                        if inside(t + 2):
                            xt_copy(ph, t + 2, par)
                    xt_copy(ph, 0, 0)
                    xt_copy(ph, 1, 1)
                    gate(0, 0)
                    pipelined(act, body)

                def gate0(t, par):
                    g, hb, hr = gs[:, par, :], bk(4 + par), E0 * R0
                    act.wait_ge(sem("f0_gate"), 11 * t + 1)
                    nc.scalar.activation(g[:, 8:16], hb[:, hr:hr + E0], ACT.Exp, bias=g[:, 0:1], accum_out=g[:, 1:2]).then_inc(
                        sem("f0_exp"), 1)
                    nc.scalar.activation(g[:, 32:33], hb[:, hr + E0:hr + E0 + 1], ACT.Exp, bias=nbthr[:, 1:2],
                                         scale=-1.0).then_inc(sem("f0_exp"), 1)

                def gate1(t, par):
                    g = gs[:, par, :]
                    act.wait_ge(sem("f1_gate"), 9 * t + 2)
                    nc.scalar.activation(g[:, 32:32 + NR1], g[:, 16:16 + NR1], ACT.Exp, bias=g[:, 0:1],
                                         accum_out=g[:, 1:2]).then_inc(sem("f1_exp"), 1)

                act.wait_ge(sem("nbthr"), 1)
                ffn("f0", gate0)

                def exp_k(t, par):
                    act.wait_ge(sem("x1_kmax"), t + 1)
                    nc.scalar.activation(ebuf2[:, par, :], erow[:, par, :], ACT.Exp, bias=sm[:, par, 0:1],
                                         accum_out=sm[:, par, 1:2]).then_inc(sem("x1_ek"), 1)

                def exp_q(t, par):
                    act.wait_ge(sem("nmr_steps"), 2 * t + 2)
                    nc.scalar.activation(ebuf[:, par, :], x[:, t, :], ACT.Exp, bias=col(nmr, t),
                                         scale=col(rstd[:, 0, :], t)).then_inc(sem("x1_eq"), 1)

                def rden_spread(t, par):
                    act.wait_ge(sem("x1_rden"), t + 1)
                    nc.scalar.activation(xn[:, par, :].rearrange("p (h d) -> p h d", d=P // HD1),
                                         gs[:, par, :].unsqueeze(2).broadcast_to([P, KD * HD1, P // HD1]),
                                         ACT.Copy).then_inc(sem("x1_rx"), 1)

                def rd_copy(t, par):
                    act.wait_ge(sem("x1_nd"), t + 1)
                    nc.scalar.activation(xn[:, par, :], bk(6 + par), ACT.Copy).then_inc(sem("x1_rd"), 1)

                def lin(t, par, pair):
                    if inside(t + 1):
                        xt_copy("x1", t + 1, 1 - par)
                    if inside(t - 1):
                        rd_copy(t - 1, 1 - par)
                    rden_spread(t, par)
                    if inside(t + 2):
                        exp_k(t + 2, par)
                    if inside(t + 1):
                        exp_q(t + 1, 1 - par)
                exp_k(0, 0)
                exp_k(1, 1)
                xt_copy("x1", 0, 0)
                exp_q(0, 0)
                pipelined(act, lin)
                rd_copy(TILES - 1, 1)
                ffn("f1", gate1)

                def exp_scores(t, par):
                    act.wait_ge(sem("x2_m"), 3 * t + 3)
                    after(act, sem("x2_out"), t - 1)
                    for b in range(BT):
                        r, cs = slice(b * C, (b + 1) * C), slice(b * C, (b + 1) * C)
                        nc.scalar.activation(pmat[r, par, cs], ps[r, 2 + par, cs], ACT.Exp, bias=sm[r, par, 1:2],
                                             scale=float(C) ** -0.5, accum_out=sm[r, par, 2:3]).then_inc(sem("x2_e"), 1)

                def chan(t, par, pair):
                    if inside(t + 1):
                        exp_scores(t + 1, 1 - par)
                    if inside(t + 2):
                        xt_copy("x2", t + 2, par)
                xt_copy("x2", 0, 0)
                xt_copy("x2", 1, 1)
                exp_scores(0, 0)
                pipelined(act, chan)
                ffn("f2", lambda t, par: None)

            @block.tensor
            def _(pe):
                pe.wait_ge(sem("ld_pick"), 16)
                for t in range(TILES):
                    par = t % 2
                    pe.wait_ge(sem("sq_done"), t + 1)
                    nc.tensor.matmul(ps[0:32, 0, :], pick[:, t, :], ebuf[:, par, :], start=t == 0, stop=t == TILES - 1)
                    pe.wait_ge(sem("dp_done"), t + 1)
                    nc.tensor.matmul(ps[0:32, 1, :], pick[:, t, :], ebuf2[:, par, :], start=t == 0,
                                     stop=t == TILES - 1).then_inc(sem("sim_mm"), 1)
                pe.wait_ge(sem("ld_conv"), 48)
                pe.wait_ge(sem("sim_steps"), 17)

                def spread(t, par):
                    after(pe, sem("x0_fs"), TAPS * (t - 1))
                    for k in range(TAPS):
                        sel = csel[0:96, t, k, :]
                        nc.tensor.matmul(bk(TAPS * par + k), sel, sim_h[:, :], start=True, stop=False)
                        last = nc.tensor.matmul(bk(TAPS * par + k), sel, sim_l[:, :], start=False, stop=True)
                    last.then_inc(sem("x0_sel"), 1)

                def conv(t, par, pair):
                    if inside(t + 1):
                        spread(t + 1, 1 - par)
                    pe.wait_ge(sem("x0_fs"), TAPS * t + TAPS)
                    after(pe, sem("x0_x"), t - 1)
                    for k in range(TAPS):
                        last = nc.tensor.matmul(bk(6 + par), convw[:, k, :], fs[:, par, k, :], start=k == 0,
                                                stop=k == TAPS - 1)
                    last.then_inc(sem("x0_conv"), 1)
                spread(0, 0)
                pipelined(pe, conv)
                pe.wait_ge(sem("x0_x"), TILES)

                def ffn(ph):
                    n, rk, hcols = sem(f"{ph}_xnT"), RK[ph], HC[ph]

                    def rows(t, par):
                        pe.wait_ge(sem(f"{ph}_xn"), t + 1)
                        transpose4(bk(par), xn[:, par, :]).then_inc(sem(f"{ph}_tr"), 1)

                    def low_rank(t, par):
                        pe.wait_ge(n, t + 1)
                        for k in range(KD):
                            last = nc.tensor.matmul(ps[:, 4 + par, 0:hcols], xnT[:, par, k, :], wag[ph][:, k, :],
                                                    start=k == 0, stop=k == KD - 1)
                        last.then_inc(sem(f"{ph}_h"), 1)

                    def body(t, par, pair):
                        if inside(t + 1):
                            low_rank(t + 1, 1 - par)
                        after(pe, sem(f"{ph}_x"), t - 1)
                        for k in range(KD):
                            nc.tensor.matmul(bk(2 + par), xnT[:, par, k, :], wbase[ph][:, k, :], start=k == 0, stop=False)
                        pe.wait_ge(sem("hw_rows"), TILES * FFN[ph] + t + 1)
                        nc.tensor.transpose(ps[:, 4 + par, 256:384], hw[:, par, :], ident[:, :]).then_inc(
                            sem("hwTr"), 1)
                        if inside(t + 2):
                            rows(t + 2, par)
                        pe.wait_ge(sem("hwT"), TILES * FFN[ph] + t + 1)
                        nc.tensor.matmul(bk(2 + par), hwT[0:rk, par, :], wb[ph][0:rk, :], start=False,
                                         stop=True).then_inc(sem(f"{ph}_out"), 1)
                    rows(0, 0)
                    rows(1, 1)
                    low_rank(0, 0)
                    pipelined(pe, body)

                pe.wait_ge(sem("ld_f0"), 64)
                ffn("f0")

                def x1_rows(t, par):
                    pe.wait_ge(sem("x1_ek"), t + 1)
                    transpose4(bk(par), ebuf2[:, par, :]).then_inc(sem("x1_tr"), 1)

                def lin(t, par, pair):
                    pe.wait_ge(sem(f"ld_cols_{par}"), loads(16, par, pair))
                    pe.wait_ge(sem("x1_xnT"), t + 1)
                    after(pe, sem("x1_kvm"), t - 1)
                    for k in range(KD):
                        last = nc.tensor.matmul(ps[:, 2 + par, 0:P], xnT[:, par, k, :], eT[:, par, k, :], start=k == 0,
                                                stop=k == KD - 1)
                    last.then_inc(sem("x1_kv"), 1)
                    if inside(t - 1):
                        rden_rows(t - 1, 1 - par)
                    if inside(t + 1):
                        x1_rows(t + 1, 1 - par)
                    pe.wait_ge(sem("x1_eq"), t + 1)
                    for k in range(KD):
                        last = nc.tensor.matmul(ps[:, par, k * HD1:(k + 1) * HD1], ebuf[:, par, k * P:(k + 1) * P],
                                                g8[:, 0:P:P // HD1], start=True, stop=True)
                    last.then_inc(sem("x1_den"), 1)
                    pe.wait_ge(sem("x1_kvm"), t + 1)
                    after(pe, sem("x1_fin"), 2 * (t - 1))
                    nc.tensor.matmul(bk(4 + par), kvm[:, par, :], ebuf[:, par, :], start=True, stop=True)

                def rden_rows(t, par):
                    pe.wait_ge(sem("x1_rx"), t + 1)
                    transpose4(bk(6 + par), xn[:, par, :]).then_inc(sem("x1_nd"), 1)
                pe.wait_ge(sem("ld_small"), 80)
                pe.wait_ge(sem("f0_x"), TILES)
                x1_rows(0, 0)
                pipelined(pe, lin)
                rden_rows(TILES - 1, 1)
                pe.wait_ge(sem("x1_fin"), 2 * TILES)
                pe.wait_ge(sem("ld_f1"), 64)
                ffn("f1")

                def rows2(t, par):
                    pe.wait_ge(sem("x2_xn"), t + 1)
                    transpose4(bk(par), xn[:, par, :]).then_inc(sem("x2_tr"), 1)

                def scores2(t, par, count):
                    pe.wait_ge(sem("x2_xnT"), t + 1)
                    pe.wait_ge(sem(f"ld_cols_{par}"), 16 * TILES // 2 + count)
                    after(pe, sem("x2_e"), 2 * (t - 1))
                    for k in range(KD):
                        last = nc.tensor.matmul(ps[:, 2 + par, 0:P], xnT[:, par, k, :], eT[:, par, k, :], start=k == 0,
                                                stop=k == KD - 1)
                    last.then_inc(sem("x2_s"), 1)

                def chan(t, par, pair):
                    if inside(t + 1):
                        scores2(t + 1, 1 - par, loads(16, par, pair, 1))
                    if inside(t + 2):
                        rows2(t + 2, par)
                    pe.wait_ge(sem("x2_r"), 2 * t + 2)
                    pe.wait_ge(sem(f"ld_rows_{par}"), 16 * TILES // 2 + loads(16, par, pair))
                    after(pe, sem("x2_x"), t - 1)
                    nc.tensor.matmul(bk(4 + par), pmat[:, par, :], erow[:, par, :], start=True, stop=True).then_inc(
                        sem("x2_out"), 1)
                pe.wait_ge(sem("f1_x"), TILES)
                rows2(0, 0)
                rows2(1, 1)
                scores2(0, 0, 16)
                pipelined(pe, chan)
                pe.wait_ge(sem("x2_x"), TILES)
                pe.wait_ge(sem("ld_f2"), 64)
                ffn("f2")

        G3, J3, RG = 16, 4, 4
        ROUNDS = G3 // RG
        OPC = 256
        VW = 26
        NQ, NK, NV, NO = 6, 5, 5, 4
        LATE_FC = 4
        LATE = (3 * FC - LATE_FC) * D
        FG, FU, FD = (wide[:, n * FC * D:(n + 1) * FC * D] for n in range(3))
        with ExitStack() as c2:
            def s2(name, shape, dt=F32):
                return sb(name, shape, dt, c2)
            xn = s2("xn3", [P, D])
            xT = s2("xT3", [P, KD, P])
            eT = s2("eT3", [P, 2, KD, P])
            p32 = s2("p32", [P, J3, RG, C])
            pth = s2("pth", [P, 2 * J3, P], F16)
            ptl = s2("ptl", [P, 2 * J3, P], F16)
            qT = s2("qT", [P, 2, G3, P], F16)
            kT = s2("kT", [P, 2, G3, P], F16)
            qrow = s2("qrow", [P, HEADS, 4, DK3], F16)
            krow = s2("krow", [P, HEADS, 4, DK3], F16)
            t32 = s2("t32", [P, 2, D])
            vc = s2("vc", [P, HEADS, 3, DK3], BF16)
            vd = s2("vd", [P, BT, G3 // 2, J3, 2, VW], BF16)
            orow = s2("orow", [P, D])
            osum = s2("osum", [P, 4 * RG, DK3])
            irep = s2("irep", [P, KD, M3])
            b3 = wide[:, LATE:LATE + 3 * D].rearrange("p (w n) -> p w n", w=3)
            bo = wide[:, LATE + 3 * D:LATE + 4 * D]
            pf = p32[:].rearrange("p j g k -> p (j g k)")
            tmix = pf[:, 0:KD * P].rearrange("p (c n) -> p c n", c=KD)
            m4 = pf[:, KD * P:(KD + 1) * P]
            ip = pf[:, (KD + 1) * P:(KD + 2) * P]
            amp = s2("amp", [P, 1])
            am = s2("am", [P, 16])
            sc = s2("sc", [P, 2])
            mx = s2("mx", [P, J3 * RG])
            rden = s2("rden", [P, 4 * RG])
            block = c2.enter_context(nc.Block())
            PAIRS = TILES // 2

            def schedule(eng, body):
                body(0, 0, 0, True, False)
                body(1, 1, 0, False, False)
                with eng.Fori(1, PAIRS - 1) as i:
                    for par in range(2):
                        body(2 * i + par, par, i, False, False)
                body(TILES - 2, 0, PAIRS - 1, False, False)
                body(TILES - 1, 1, PAIRS - 1, False, True)

            @block.sync
            def _(sp):
                sp.dma_start(irep[:], a["irep"].rearrange("(k p) n -> p k n", p=P)).then_inc(sem("ld_mix"), 16)
                sp.dma_start(m4, a["c_m4"]).then_inc(sem("ld_mix"), 16)
                sp.dma_start(ip, a["c_ip"]).then_inc(sem("ld_mix"), 16)
                sp.dma_start(amp[:], a["amp"].partition_broadcast(P)).then_inc(sem("ld_mix"), 16)
                sp.dma_start(ident16[:], a["c_ident16"]).then_inc(sem("ld_mix"), 16)
                for par in range(2):
                    sp.dma_start(eT[:, par], ctxTv[par]).then_inc(sem(f"ld_x3_{par}"), 16)
                sp.dma_start(FG.bitcast(I32).rearrange("p (k n) -> p k n", k=KD),
                             a["gate_t"].rearrange("(k p) n -> p k n", p=P)).then_inc(sem("ld_ffn"), 16)
                sp.wait_ge(sem("fold_mm"), 15)
                sp.dma_start(FU.bitcast(I32).rearrange("p (k n) -> p k n", k=KD),
                             a["up_t"].rearrange("(k p) n -> p k n", p=P)).then_inc(sem("ld_ffn"), 16)
                sp.dma_start(bo, a["bo3"].partition_broadcast(P)).then_inc(sem("ld_bo"), 16)
                sp.dma_start(FD.bitcast(I32).rearrange("p (k n) -> p k n", k=FC)[:, 0:FC - LATE_FC],
                             a["down_t"].rearrange("(k p) n -> p k n", p=P)[:, 0:FC - LATE_FC]).then_inc(sem("ld_ffn"), 16)

                def more(t, par):
                    sp.wait_ge(sem("x3_v"), t - 1)
                    sp.dma_start(eT[:, par], ctxTv[t]).then_inc(sem(f"ld_x3_{par}"), 16)
                all_tiles(sp, more, 2)

            @block.gpsimd
            def _(pool):
                nc.gpsimd.memset(qrow[:, :, 3, :], 0.0).then_inc(sem("zeros3"), 1)
                nc.gpsimd.memset(krow[:, :, 3, :], 0.0).then_inc(sem("zeros3"), 1)
                nc.gpsimd.memset(vd[:].rearrange("p b g j h w -> p (b g j h w)"), 0.0).then_inc(sem("zeros3"), 1)
                pool.wait_ge(sem("zeros3"), 3)
                for hd in range(2):
                    r = slice(hd * C, (hd + 1) * C)
                    nc.gpsimd.memset(vd[r].rearrange("p b g j h w -> p (b g j) h w")[:, :, hd, 24:25], 1.0).then_inc(
                        sem("zeros3"), 1)
                pool.wait_ge(sem("ld_bo"), 16)

                def kmax(t):
                    pool.wait_ge(sem("k_steps"), NK * t + 2)
                    hold_pool()
                    nc.gpsimd.partition_all_reduce(am[:, 9:10], am[:, 8:9], P, RMAX).then_inc(sem("k_all"), 1)

                def body(t, par, pair, first, last, conv):
                    pool.wait_ge(sem("x3_xn"), t + 1)
                    nc.gpsimd.tensor_tensor(x[:, t, :], x[:, t, :], bo, ALU.add).then_inc(sem("x3_biased"), 1)
                    if not last:
                        kmax(t + 1)
                    if not first:
                        pool_rstd(pool, 7, t - 1)
                    if conv is not None:
                        n = LATE // (TILES // 2)
                        at = slice(conv * n, (conv + 1) * n) if isinstance(conv, int) else bass.ds(conv * n, n)
                        nc.gpsimd.tensor_copy(wide[:, at], wide[:, at].bitcast(I32)).then_inc(sem("converted"), 1)
                kmax(0)
                body(0, 0, 0, True, False, None)
                body(1, 1, 0, False, False, None)
                with pool.Fori(1, PAIRS // 2) as i:
                    for par in range(2):
                        body(2 * i + par, par, i, False, False, None)
                pool.wait_ge(sem("ld_ffn"), 48)
                with pool.Fori(PAIRS // 2, PAIRS - 1) as i:
                    for par in range(2):
                        body(2 * i + par, par, i, False, False, 2 * i + par - TILES // 2)
                body(TILES - 2, 0, 0, False, False, TILES // 2 - 2)
                body(TILES - 1, 1, 0, False, True, TILES // 2 - 1)
                pool_rstd(pool, 7, TILES - 1)

            @block.vector
            def _(dve):
                ms = sem("mix_steps")
                dve.wait_ge(sem("ld_mix"), 80)
                nc.vector.tensor_scalar(irep[:], irep[:], amp[:, 0:1], 0.1, ALU.mult, ALU.mult).then_inc(ms, 1)
                dve.wait_ge(ms, 1)
                for c in range(KD):
                    nc.vector.tensor_tensor(tmix[:, c, :].rearrange("p (h m d) -> p h m d", h=4, m=M3),
                                            irep[:, c, :].unsqueeze(1).unsqueeze(3).broadcast_to([P, 4, M3, DK3]),
                                            m4.rearrange("p (h m d) -> p h m d", h=4, m=M3), ALU.mult).then_inc(ms, 1)
                dve.wait_ge(ms, 1 + KD)
                for c in range(KD):
                    nc.vector.tensor_tensor(tmix[:, c, :], tmix[:, c, :], ip, ALU.add).then_inc(ms, 1)
                for n in range(1, 15, 2):
                    dve.wait_ge(sem("fold_mm"), n + 1)
                    dst = wf[:, n // 4, n % 4, :] if n < 12 else b3[:, n - 12, :]
                    nc.vector.tensor_copy(dst, bk(n % 8)).then_inc(sem("fold_dve"), 1)
                dve.wait_ge(sem("fold_act"), 8)
                dve.wait_ge(sem("fold_dve"), 7)
                dve.wait_ge(sem("zeros3"), 5)

                def norm(t):
                    normalise(dve, 6, t, xn[:], sem("x3_xn"))

                def heads(v):
                    return v.rearrange("p (h d) -> p h d", d=DK3)

                def q_scale(t, par):
                    s, n = sem("q_steps"), NQ * t
                    dve.wait_ge(sem("x3_q"), t + 1)
                    nc.vector.tensor_tensor(t32[:, 0, :], bk(6), b3[:, 0, :], ALU.add).then_inc(s, 1)
                    dve.wait_ge(s, n + 1)
                    nc.vector.tensor_reduce(am[:, 0:1], t32[:, 0, :], AX.X, ALU.max, apply_absolute_value=True).then_inc(s, 1)
                    dve.wait_ge(s, n + 2)
                    nc.vector.tensor_scalar(am[:, 1:2], am[:, 0:1], 1e-30, 1.0 / SPLIT_TOP, ALU.max, ALU.mult).then_inc(s, 1)
                    dve.wait_ge(s, n + 3)
                    nc.vector.reciprocal(am[:, 2:3], am[:, 1:2]).then_inc(s, 1)
                    nc.vector.scalar_tensor_tensor(sc[:, par:par + 1], am[:, 1:2], float(DK3) ** -0.5, am[:, 10:11],
                                                   ALU.mult, ALU.mult).then_inc(s, 1)

                def q_low(t):
                    s, n = sem("q_steps"), NQ * t
                    dve.wait_ge(s, n + 4)
                    dve.wait_ge(sem("q_hi"), t + 1)
                    nc.vector.scalar_tensor_tensor(qrow[:, :, 2, :], heads(t32[:, 0, :]), am[:, 2:3], qrow[:, :, 0, :],
                                                   ALU.mult, ALU.subtract).then_inc(s, 1)

                def k_largest(t):
                    s, n = sem("k_steps"), NK * t
                    dve.wait_ge(sem("x3_k"), t + 1)
                    nc.vector.tensor_tensor(t32[:, 1, :], bk(6), b3[:, 1, :], ALU.add).then_inc(s, 1)
                    dve.wait_ge(s, n + 1)
                    nc.vector.tensor_reduce(am[:, 8:9], t32[:, 1, :], AX.X, ALU.max, apply_absolute_value=True).then_inc(s, 1)

                def k_scale(t):
                    s, n = sem("k_steps"), NK * t
                    dve.wait_ge(sem("k_all"), t + 1)
                    nc.vector.tensor_scalar(am[:, 10:11], am[:, 9:10], 1e-30, 1.0 / SPLIT_TOP, ALU.max, ALU.mult).then_inc(s, 1)
                    dve.wait_ge(s, n + 3)
                    nc.vector.reciprocal(am[:, 11:12], am[:, 10:11]).then_inc(s, 1)

                def k_low(t):
                    s, n = sem("k_steps"), NK * t
                    dve.wait_ge(sem("k_hi"), t + 1)
                    dve.wait_ge(s, n + 4)
                    nc.vector.scalar_tensor_tensor(krow[:, :, 1, :], heads(t32[:, 1, :]), am[:, 11:12], krow[:, :, 0, :],
                                                   ALU.mult, ALU.subtract).then_inc(s, 1)

                def v_ops(t):
                    s, n = sem("v_steps"), NV * t
                    dve.wait_ge(sem("q_steps"), NQ * t + NQ)
                    dve.wait_ge(sem("x3_v"), t + 1)
                    nc.vector.tensor_tensor(t32[:, 0, :], bk(6), b3[:, 2, :], ALU.add).then_inc(s, 1)
                    dve.wait_ge(s, n + 1)
                    nc.vector.tensor_copy(vc[:, :, 0, :], heads(t32[:, 0, :])).then_inc(s, 1)
                    dve.wait_ge(s, n + 2)
                    nc.vector.tensor_tensor(heads(t32[:, 1, :]), heads(t32[:, 0, :]), vc[:, :, 0, :], ALU.subtract).then_inc(s, 1)
                    dve.wait_ge(s, n + 3)
                    nc.vector.tensor_copy(vc[:, :, 1, :], heads(t32[:, 1, :])).then_inc(s, 1)
                    dve.wait_ge(s, n + 4)
                    nc.vector.tensor_tensor(vc[:, :, 2, :], heads(t32[:, 1, :]), vc[:, :, 1, :], ALU.subtract).then_inc(s, 1)

                def vd_ops(t):
                    dve.wait_ge(sem("v_steps"), NV * t + NV)
                    for b in range(BT):
                        for hd in range(2):
                            src = vc[b * C:(b + 1) * C].rearrange("p (g h j) m d -> p g h (j m d)", h=2, j=J3)[:, :, hd, :]
                            dst = vd[hd * C:(hd + 1) * C, b, :, :, hd, 0:24]
                            nc.vector.tensor_copy(dst, src.rearrange("p g (j w) -> p g j w", j=J3)).then_inc(sem("x3_vd"), 1)

                def out_norm(rr, r, t):
                    so = sem("o_steps")
                    if r == 0:
                        after(dve, sem("x3_otr"), t)
                    for n in range(2):
                        o = ps[:, n, OPC:OPC + 4 * 2 * VW].rearrange("p (h w) -> p h w", w=VW)
                        nc.vector.reciprocal(rden[:, 8 * n:8 * n + 8], o[:, :, 24]).then_inc(so, 1)
                        nc.vector.tensor_reduce(osum[:, 8 * n:8 * n + 8, :],
                                                o[:, :, 0:24].rearrange("p h (m d) -> p h d m", m=3), AX.X,
                                                ALU.add).then_inc(so, 1)
                    dve.wait_ge(so, (NO + 1) * rr + NO)
                    dst = orow[:, r * RG * 32:(r + 1) * RG * 32].rearrange("p (g j d) -> p j g d", g=RG, j=J3)
                    nc.vector.tensor_tensor(dst, osum[:].rearrange("p (j g) d -> p j g d", j=J3),
                                            rden[:].rearrange("p (j g) -> p j g", j=J3).unsqueeze(3).broadcast_to(
                                                [P, J3, RG, DK3]), ALU.mult).then_inc(so, 1)

                def finish(t):
                    dve.wait_ge(sem("x3_wo"), t + 1)
                    dve.wait_ge(sem("x3_biased"), t + 1)
                    nc.vector.tensor_tensor(x[:, t, :], x[:, t, :], bk(6), ALU.add).then_inc(sem("x3_x"), 1)
                    dve.wait_ge(sem("x3_x"), t + 1)
                    hold(dve)
                    stats(dve, 7, t)

                norm(0)
                k_largest(0)
                k_scale(0)
                k_low(0)
                q_scale(0, 0)
                q_low(0)
                v_ops(0)
                dve.wait_ge(sem("x3_tr"), 1)
                norm(1)

                def low_parts(rr):
                    dve.wait_ge(sem("x3_pt"), rr + 1)
                    dve.wait_ge(sem("x3_pth"), rr + 1)
                    nc.vector.scalar_tensor_tensor(ptl[:].rearrange("p n q -> p (n q)"),
                                                   ps[:, 4:6, :].rearrange("p b n -> p (b n)"), P_SCALE,
                                                   pth[:].rearrange("p n q -> p (n q)"), ALU.mult,
                                                   ALU.subtract).then_inc(sem("x3_ptl"), 1)

                def body(t, par, pair, first, last):
                    for r in range(ROUNDS):
                        rr = ROUNDS * t + r
                        s_ps = ps[:, 0:J3, 0:RG * C].rearrange("p j (g k) -> p j g k", g=RG)
                        dve.wait_ge(sem("x3_s"), rr + 1)
                        nc.vector.tensor_reduce(mx[:].rearrange("p (j g) -> p j g", j=J3), s_ps, AX.X, ALU.max).then_inc(
                            sem("x3_max"), 1)
                        dve.wait_ge(sem("x3_max"), rr + 1)
                        after(dve, sem("x3_pt"), rr)
                        for j in range(J3):
                            last_sub = nc.vector.tensor_tensor(
                                p32[:, j], s_ps[:, j], mx[:, j * RG:(j + 1) * RG].unsqueeze(2).broadcast_to([P, RG, C]),
                                ALU.subtract)
                        last_sub.then_inc(sem("x3_sub"), 1)
                        if not (first and r < 2):
                            out_norm(rr - 2, (r - 2) % ROUNDS, t)
                        if r == 1:
                            vd_ops(t)
                        if not (first and r == 0):
                            low_parts(rr - 1)
                        if r == 0 and not last:
                            k_largest(t + 1)
                        elif r == 1 and not last:
                            k_scale(t + 1)
                            k_low(t + 1)
                            q_scale(t + 1, 1 - par)
                        elif r == 2 and not last:
                            q_low(t + 1)
                            v_ops(t + 1)
                        elif r == 3:
                            if inside(t + 2):
                                norm(t + 2)
                            if not first:
                                finish(t - 1)
                schedule(dve, body)
                low_parts(ROUNDS * TILES - 1)
                out_norm(ROUNDS * TILES - 2, ROUNDS - 2, TILES)
                dve.wait_ge(sem("x3_pv"), ROUNDS * TILES)
                out_norm(ROUNDS * TILES - 1, ROUNDS - 1, TILES)
                finish(TILES - 1)

            @block.scalar
            def _(act):
                for n in range(0, 15, 2):
                    act.wait_ge(sem("fold_mm"), n + 1)
                    dst = wf[:, n // 4, n % 4, :] if n < 12 else b3[:, n - 12, :]
                    nc.scalar.activation(dst, bk(n % 8), ACT.Copy).then_inc(sem("fold_act"), 1)

                def xT_copy(tr, k, done):
                    act.wait_ge(sem(tr), k)
                    nc.scalar.activation(xT[:].rearrange("p k n -> p (k n)"), bk(7), ACT.Copy).then_inc(sem(done), 1)

                def hi(row, lo_part, src, scale, steps, need, done):
                    act.wait_ge(sem(steps), need)
                    dst = row[:, :, 0:2, :] if lo_part == 2 else row[:, :, 0:3:2, :]
                    nc.scalar.activation(dst, src.rearrange("p (h d) -> p h d", d=DK3).unsqueeze(2).broadcast_to(
                        [P, HEADS, 2, DK3]), ACT.Copy, scale=scale).then_inc(sem(done), 1)

                def q_hi(t):
                    hi(qrow, 2, t32[:, 0, :], am[:, 2:3], "q_steps", NQ * t + 4, "q_hi")

                def k_hi(t):
                    hi(krow, 1, t32[:, 1, :], am[:, 11:12], "k_steps", NK * t + 4, "k_hi")

                def t_copy(dst, par, n, tr, t, done):
                    act.wait_ge(sem(tr), 2 * t + n + 1)
                    nc.scalar.activation(dst[:, par, 8 * n:8 * n + 8, :].rearrange("p g n -> p (g n)"),
                                         bk(7).bitcast(F16), ACT.Copy).then_inc(sem(done), 1)

                act.wait_ge(sem("zeros3"), 5)
                xT_copy("x3_tr", 1, "x3_xT")
                k_hi(0)
                t_copy(kT, 0, 0, "x3_ktr", 0, "x3_kT")
                q_hi(0)
                t_copy(kT, 0, 1, "x3_ktr", 0, "x3_kT")
                t_copy(qT, 0, 0, "x3_qtr", 0, "x3_qT")
                t_copy(qT, 0, 1, "x3_qtr", 0, "x3_qT")

                def high_parts(rr):
                    act.wait_ge(sem("x3_pt"), rr + 1)
                    nc.scalar.activation(pth[:].rearrange("p n q -> p (n q)"),
                                         ps[:, 4:6, :].rearrange("p b n -> p (b n)"), ACT.Copy,
                                         scale=P_SCALE).then_inc(sem("x3_pth"), 1)

                def body(t, par, pair, first, last):
                    nxt = 1 - par
                    for r in range(ROUNDS):
                        rr = ROUNDS * t + r
                        if not (first and r == 0):
                            high_parts(rr - 1)
                        if r == 2 and not last:
                            t_copy(kT, nxt, 0, "x3_ktr", t + 1, "x3_kT")
                        elif r == 3 and not last:
                            t_copy(qT, nxt, 0, "x3_qtr", t + 1, "x3_qT")
                        act.wait_ge(sem("x3_sub"), rr + 1)
                        nc.scalar.activation(pf, pf, ACT.Exp, scale=sc[:, par:par + 1]).then_inc(sem("x3_exp"), 1)
                        if r == 0 and not last:
                            xT_copy("x3_tr", t + 2, "x3_xT")
                        elif r == 1:
                            if not last:
                                k_hi(t + 1)
                            if not first:
                                xT_copy("x3_otr", t, "x3_oT")
                            if not last:
                                q_hi(t + 1)
                        elif r == 2 and not last:
                            t_copy(kT, nxt, 1, "x3_ktr", t + 1, "x3_kT")
                        elif r == 3 and not last:
                            t_copy(qT, nxt, 1, "x3_qtr", t + 1, "x3_qT")
                schedule(act, body)
                high_parts(ROUNDS * TILES - 1)
                xT_copy("x3_otr", TILES, "x3_oT")

            @block.tensor
            def _(pe):
                pe.wait_ge(sem("f2_x"), TILES)
                pe.wait_ge(sem("ld_w3"), 48)
                pe.wait_ge(sem("mix_steps"), 1 + 2 * KD)
                for n in range(15):
                    if n >= 8:
                        m = n - 8
                        pe.wait_ge(sem("fold_dve" if m % 2 else "fold_act"), m // 2 + 1)
                    for c in range(KD):
                        w = wnat[:, n // 4, c, n % 4 * P:n % 4 * P + P] if n < 12 else b3rep[:, n - 12, c, :]
                        last = nc.tensor.matmul(ps[:, n % 8, c * P:(c + 1) * P], w, tmix[:, c, :], start=True, stop=True)
                    last.then_inc(sem("fold_mm"), 1)
                pe.wait_ge(sem("fold_act"), 8)
                pe.wait_ge(sem("fold_dve"), 7)

                def project(lhs, w, done):
                    for k in range(KD):
                        last = nc.tensor.matmul(bk(6), lhs[:, k, :], w[:, k, :], start=k == 0, stop=k == KD - 1)
                    last.then_inc(sem(done), 1)

                def rows(t):
                    pe.wait_ge(sem("x3_xn"), t + 1)
                    transpose4(bk(7), xn[:, :]).then_inc(sem("x3_tr"), 1)

                def q_mm(t):
                    pe.wait_ge(sem("x3_xT"), t + 1)
                    project(xT, wf[:, 0], "x3_q")

                def k_mm(t, par, pair):
                    pe.wait_ge(sem(f"ld_x3_{par}"), 16 * pair + 16)
                    project(eT[:, par], wf[:, 1], "x3_k")

                def v_mm(t, par):
                    pe.wait_ge(sem("q_steps"), NQ * t + 1)
                    project(eT[:, par], wf[:, 2], "x3_v")

                def stack_tr(row, n, done):
                    for g in range(8):
                        h = 4 * (8 * n + g)
                        last = nc.tensor.transpose(bk(7).bitcast(F16)[:, g * P:(g + 1) * P],
                                                   row[:, h:h + 4].rearrange("p h m d -> p (h m d)"), ident16[:, :])
                    last.then_inc(sem(done), 1)

                def k_tr(t, n):
                    if n == 0:
                        pe.wait_ge(sem("k_steps"), NK * t + NK)
                        pe.wait_ge(sem("x3_xT"), t + 1)
                    else:
                        pe.wait_ge(sem("x3_kT"), 2 * t + 1)
                    stack_tr(krow, n, "x3_ktr")

                def q_tr(t, n):
                    if n == 0:
                        pe.wait_ge(sem("q_steps"), NQ * t + NQ)
                        pe.wait_ge(sem("x3_kT"), 2 * t + 2)
                    else:
                        pe.wait_ge(sem("x3_qT"), 2 * t + 1)
                    stack_tr(qrow, n, "x3_qtr")

                def pv(rr, r, t):
                    pe.wait_ge(sem("x3_pth"), rr + 1)
                    pe.wait_ge(sem("x3_ptl"), rr + 1)
                    after(pe, sem("o_steps"), (NO + 1) * rr)
                    if r == 0:
                        pe.wait_ge(sem("x3_vd"), 4 * t + 4)
                    for j in range(J3):
                        for u in range(2):
                            n = 2 * j + u
                            c = OPC + n % 4 * 2 * VW
                            for b in range(BT):
                                for pt in (pth, ptl):
                                    last = nc.tensor.matmul(
                                        ps[b * C:(b + 1) * C, n // 4, c:c + 2 * VW], pt[:, n, b * C:(b + 1) * C],
                                        vd[:, b, 2 * r + u, j].rearrange("p h w -> p (h w)"), start=pt is pth, stop=pt is ptl)
                    last.then_inc(sem("x3_pv"), 1)

                def o_tr(t):
                    pe.wait_ge(sem("o_steps"), (NO + 1) * ROUNDS * (t + 1))
                    transpose4(bk(7), orow[:, :]).then_inc(sem("x3_otr"), 1)

                def wo_mm(t):
                    pe.wait_ge(sem("x3_oT"), t + 1)
                    project(xT, wo, "x3_wo")

                rows(0)
                k_mm(0, 0, 0)
                k_tr(0, 0)
                pe.wait_ge(sem("k_steps"), 1)
                q_mm(0)
                k_tr(0, 1)
                v_mm(0, 0)
                q_tr(0, 0)
                q_tr(0, 1)

                def prob_tr(rr):
                    pe.wait_ge(sem("x3_exp"), rr + 1)
                    after(pe, sem("x3_ptl"), rr)
                    for j in range(J3):
                        for u in range(2):
                            n = 2 * j + u
                            mm = nc.tensor.transpose(ps[:, 4 + n // 4, n % 4 * P:(n % 4 + 1) * P],
                                                     p32[:, j, 2 * u:2 * u + 2, :].rearrange("p g k -> p (g k)"),
                                                     ident[:, :])
                    mm.then_inc(sem("x3_pt"), 1)

                def body(t, par, pair, first, last):
                    nxt = 1 - par
                    npair = pair + 1 if par else pair
                    for r in range(ROUNDS):
                        rr = ROUNDS * t + r
                        after(pe, sem("x3_sub"), rr)
                        if r == 0:
                            pe.wait_ge(sem("x3_qT"), 2 * t + 2)
                        for g in range(RG):
                            for b in range(BT):
                                for j in range(J3):
                                    rows_j, cols_b = slice(32 * j, 32 * j + 32), slice(b * C, (b + 1) * C)
                                    mm = nc.tensor.matmul(ps[cols_b, j, g * C:(g + 1) * C],
                                                          qT[rows_j, par, RG * r + g, cols_b],
                                                          kT[rows_j, par, RG * r + g, cols_b], start=True, stop=True)
                        mm.then_inc(sem("x3_s"), 1)
                        if not (first and r == 0):
                            prob_tr(rr - 1)
                        if r == 0 and not last:
                            rows(t + 1)
                            after(pe, sem("x3_x"), t - 1)
                            if first:
                                pe.wait_ge(sem("v_steps"), 1)
                            k_mm(t + 1, nxt, npair)
                        elif r == 1:
                            if not last:
                                pe.wait_ge(sem("k_steps"), NK * (t + 1) + 1)
                                q_mm(t + 1)
                            if not first:
                                o_tr(t - 1)
                        elif r == 2 and not last:
                            after(pe, sem("x3_oT"), t)
                            k_tr(t + 1, 0)
                            v_mm(t + 1, nxt)
                            k_tr(t + 1, 1)
                        elif r == 3:
                            if not last:
                                q_tr(t + 1, 0)
                            if not first:
                                if last:
                                    pe.wait_ge(sem("x3_x"), t - 1)
                                else:
                                    pe.wait_ge(sem("v_steps"), NV * (t + 1) + 1)
                                wo_mm(t - 1)
                            if not last:
                                q_tr(t + 1, 1)
                        if not (first and r == 0):
                            pe.wait_ge(sem("x3_sub"), rr + 1)
                            pv(rr - 1, (r - 1) % ROUNDS, t)
                schedule(pe, body)
                prob_tr(ROUNDS * TILES - 1)
                pv(ROUNDS * TILES - 1, ROUNDS - 1, TILES)
                pe.wait_ge(sem("x3_x"), TILES - 1)
                o_tr(TILES - 1)
                wo_mm(TILES - 1)

        GT = 4
        GROUPS = TILES // GT
        with ExitStack() as c3:
            def s3(name, shape, dt=F32):
                return sb(name, shape, dt, c3)
            xn = s3("xn8", [P, GT, D])
            xT = s3("xT8", [P, KD, GT * P])
            sg = s3("sg", [P, 2, GT * P])
            hid = s3("hid", [P, 2, GT * P])
            scaled = s3("scaled", [P, 2, D])
            gsc = s3("gsc", [P, FC])
            usc = s3("usc", [P, FC])
            dsc = s3("dsc", [P, D])
            block = c3.enter_context(nc.Block())
            gate_w = FG.rearrange("p (k n) -> p k n", k=KD)
            up_w = FU.rearrange("p (k n) -> p k n", k=KD)
            down_w = FD.rearrange("p (k n) -> p k n", k=FC)

            def groups(eng, body):
                body(0, False)
                with eng.Fori(1, GROUPS - 1) as g:
                    body(g, False)
                body(GROUPS - 1, True)

            @block.sync
            def _(sp):
                sp.dma_start(gsc[:], a["gate_s"]).then_inc(sem("ld_scales"), 16)
                sp.dma_start(usc[:], a["up_s"]).then_inc(sem("ld_scales"), 16)
                sp.dma_start(dsc[:], a["down_s"].partition_broadcast(P)).then_inc(sem("ld_scales"), 16)
                sp.wait_ge(sem("x3_x"), TILES)
                sp.dma_start(down_w[:, FC - LATE_FC:].bitcast(I32),
                             a["down_t"].rearrange("(k p) n -> p k n", p=P)[:, FC - LATE_FC:]).then_inc(sem("ld_late"), 16)
                with sp.Fori(0, TILES) as t:
                    sp.wait_ge(sem("f3_x"), 2 * t + 2)
                    sp.dma_start(outv[t], x[:, t, :]).then_inc(sem("stored"), 16)
                sp.wait_ge(sem("stored"), 16 * TILES)

            @block.gpsimd
            def _(pool):
                pool.wait_ge(sem("ld_late"), 16)
                nc.gpsimd.tensor_copy(wide[:, LATE:], wide[:, LATE:].bitcast(I32)).then_inc(sem("converted"), 1)

            @block.vector
            def _(dve):
                def norms(g):
                    for j in range(GT):
                        normalise(dve, 7, GT * g + j, xn[:, j, :], sem("f3_xn"))
                norms(0)
                dve.wait_ge(sem("ld_scales"), 48)

                def body(g, last):
                    for f in range(FC):
                        n = FC * g + f
                        dve.wait_ge(sem("f3_gu"), n + 1)
                        dve.wait_ge(sem("f3_silu"), n + 1)
                        nc.vector.scalar_tensor_tensor(hid[:, f % 2, :], bk(5 + 2 * (f % 2)), usc[:, f:f + 1], sg[:, f % 2, :],
                                                       ALU.mult, ALU.mult).then_inc(sem("f3_hid"), 1)
                        if f == FC // 2 and not last:
                            norms(g + 1)
                    for j in range(GT):
                        t = GT * g + j
                        dve.wait_ge(sem("f3_down"), t + 1)
                        nc.vector.tensor_tensor(scaled[:, j % 2, :], bk(j), dsc[:], ALU.mult).then_inc(sem("f3_x"), 1)
                        dve.wait_ge(sem("f3_x"), 2 * t + 1)
                        nc.vector.tensor_tensor(x[:, t, :], x[:, t, :], scaled[:, j % 2, :], ALU.add).then_inc(sem("f3_x"), 1)
                groups(dve, body)

            @block.scalar
            def _(act):
                def xT_copy(g):
                    for j in range(GT):
                        act.wait_ge(sem("f3_tr"), GT * g + j + 1)
                        nc.scalar.activation(xT[:, :, j * P:(j + 1) * P], bk(4 + j).rearrange("p (k n) -> p k n", k=KD),
                                             ACT.Copy).then_inc(sem("f3_xT"), 1)
                xT_copy(0)
                act.wait_ge(sem("ld_scales"), 48)

                def body(g, last):
                    for f in range(FC):
                        act.wait_ge(sem("f3_gu"), FC * g + f + 1)
                        if f >= 2:
                            act.wait_ge(sem("f3_hid"), FC * g + f - 1)
                        nc.scalar.activation(sg[:, f % 2, :], bk(4 + 2 * (f % 2)), ACT.Silu, scale=gsc[:, f:f + 1]).then_inc(
                            sem("f3_silu"), 1)
                    if not last:
                        xT_copy(g + 1)
                groups(act, body)

            @block.tensor
            def _(pe):
                pe.wait_ge(sem("x3_x"), TILES)
                pe.wait_ge(sem("converted"), TILES // 2)

                def rows(g, j):
                    pe.wait_ge(sem("f3_xn"), GT * g + j + 1)
                    transpose4(bk(4 + j), xn[:, j, :]).then_inc(sem("f3_tr"), 1)

                def gate_up(g, f):
                    for w, b in ((gate_w, 4 + 2 * (f % 2)), (up_w, 5 + 2 * (f % 2))):
                        for k in range(KD):
                            last = nc.tensor.matmul(bk(b), w[:, k, f * P:(f + 1) * P], xT[:, k, :], start=k == 0,
                                                    stop=k == KD - 1)
                    last.then_inc(sem("f3_gu"), 1)

                def down(g, f):
                    pe.wait_ge(sem("f3_hid"), FC * g + f + 1)
                    if f == FC - LATE_FC:
                        pe.wait_ge(sem("converted"), TILES // 2 + 1)
                    for j in range(GT):
                        mm = nc.tensor.matmul(bk(j), hid[:, f % 2, j * P:(j + 1) * P], down_w[:, f, :], start=f == 0,
                                              stop=f == FC - 1)
                        if f == FC - 1:
                            mm.then_inc(sem("f3_down"), 1)

                for j in range(GT):
                    rows(0, j)

                def body(g, last):
                    pe.wait_ge(sem("f3_xT"), GT * g + GT)
                    gate_up(g, 0)
                    gate_up(g, 1)
                    after(pe, sem("f3_x"), 2 * GT * g)
                    for f in range(FC):
                        down(g, f)
                        if f + 2 < FC:
                            gate_up(g, f + 2)
                        elif not last:
                            for j in (0, 1) if f + 2 == FC else (2, 3):
                                rows(g + 1, j)
                groups(pe, body)


_CORE_INPUTS = ["x", "ctx"]


def kernel(**inputs):
    import numpy as np
    import concourse.bacc as bacc
    from concourse.bass_utils import run_bass_kernel_spmd

    v = {k: np.asarray(w) for k, w in inputs.items()}
    f32 = np.float32
    tiles, kd = TILES, KD
    ctx = v["ctx_4096"].reshape(B * C, D)
    ar = {
        "x": v["x"].reshape(B * C, D),
        "ctx": ctx,
        "ctxT": ctx.reshape(tiles, P, kd, P).transpose(0, 3, 2, 1),
        "f0_base": v["L0_ffn_W_base"].T,
        "f0_ag": np.concatenate([v["L0_ffn_A_w"].reshape(E0 * R0, D), v["L0_ffn_W_gate"], v["L0_ffn_W_thr"][None]]).T,
        "f0_b": v["L0_ffn_B_w"].transpose(0, 2, 1).reshape(E0 * R0, D),
        "f0_bias": v["L0_ffn_b_base"],
        "thr_b": v["L0_ffn_b_thr"],
        "f1_base": v["L1_ffn_base_W"].T,
        "f1_ag": np.concatenate([v["L1_ffn_A"].reshape(E0 * R0, D), v["L1_ffn_router_W"]]).T,
        "f1_b": v["L1_ffn_B"].transpose(0, 2, 1).reshape(E0 * R0, D),
        "f1_bias": v["L1_ffn_base_b"],
        "router_b": v["L1_ffn_router_b"],
        "expert_map": v["L1_ffn_expert_map"],
        "f2_base": v["L2_ffn_W"].T,
        "f2_ag": np.concatenate([v["L2_ffn_A"], v["L2_ffn_gate_w"]]).T,
        "f2_b": v["L2_ffn_B"].T,
        "f2_bias": v["L2_ffn_b"],
        "gate_b2": v["L2_ffn_gate_b"],
        "w3": np.stack([v["L3_xattn_Wq"], v["L3_xattn_Wk"], v["L3_xattn_Wv"]]),
        "b3rep": np.stack([np.repeat(v[f"L3_xattn_b{c}"][:, None], P, 1) for c in "qkv"]),
        "wo3": v["L3_xattn_Wo"].T.reshape(H3, DK3, M3, D).transpose(0, 2, 1, 3).reshape(D, D),
        "bo3": v["L3_xattn_bo"],
        "irep": np.repeat(v["L3_xattn_interference"][:, None], DK3, 1).reshape(D, M3),
        "amp": v["L3_xattn_amp"],
        "gate_t": v["L3_ffn_gate_t"].T,
        "up_t": v["L3_ffn_up_t"].T,
        "down_t": v["L3_ffn_down_t"].T,
        "gate_s": v["L3_ffn_gate_s"].reshape(FC, P).T,
        "up_s": v["L3_ffn_up_s"].reshape(FC, P).T,
        "down_s": v["L3_ffn_down_s"],
    }
    w = v["L0_xattn_weight"].transpose(1, 2, 0)
    conv = np.zeros((BT, C, TAPS, BT, C), f32)
    for b in range(BT):
        conv[b, :, :, b, :] = w
    ar["convw"] = conv.reshape(P, TAPS, P)
    ar["c_ident"] = np.eye(P, dtype=f32)
    ar["c_ident16"] = np.eye(P, dtype=np.float16)
    ar["c_g8"] = np.kron(np.eye(P // 8), np.ones((8, 8))).astype(f32)
    pick = np.zeros((P, tiles, B), f32)
    for t in range(tiles):
        for b in range(BT):
            pick[b * C:(b + 1) * C, t, BT * t + b] = 1
    ar["c_pick"] = pick
    sel = np.zeros((TAPS, B, tiles, TAPS, BT, C), np.float16)
    for t in range(tiles):
        for b in range(BT):
            for k in range(TAPS):
                for c in range(C):
                    sel[(TAPS * c + k) // C, BT * t + b, t, k, b, c] = 1
    ar["c_sel"] = sel.reshape(TAPS * B, tiles, TAPS, P)
    hdi = np.arange(P)
    h_in, d_in, m_in = hdi // 32, hdi // 4 % 8, hdi % 4
    h_out, m_out, d_out = hdi // 32, hdi // 8 % 4, hdi % 8
    same = (h_in[:, None] == h_out) & (d_in[:, None] == d_out)
    ar["c_m4"] = same.astype(f32)
    ar["c_ip"] = (same & (m_in[:, None] == m_out)).astype(f32)

    nc = bacc.Bacc("TRN2", target_bir_lowering=False, num_devices=1)
    arrays, dram = {}, {}
    for name, arr in ar.items():
        arr = np.ascontiguousarray(arr)
        arrays[f"in_{name}"] = arr
        dram[name] = nc.dram_tensor(f"in_{name}", arr.shape, mybir.dt.from_np(arr.dtype), kind="ExternalInput").ap()
    out = nc.dram_tensor("out", (B * C, D), F32, kind="ExternalOutput").ap()
    xattn_ffn_program(nc, dram, out)
    r = run_bass_kernel_spmd(nc, [arrays], core_ids=[0])
    return np.asarray(r.results[0]["out"]).reshape(B, C, D)
```

```python
import concourse.bass as bass
from concourse import mybir
from contextlib import ExitStack

F32 = mybir.dt.float32
F16 = mybir.dt.float16
BF16 = mybir.dt.bfloat16
F32R = mybir.dt.float32r
I32 = mybir.dt.int32
ALU = mybir.AluOpType
ACT = mybir.ActivationFunctionType
AX = mybir.AxisListType

P = 128
B, C, D = 32, 64, 512
BT = P // C
TILES = B * C // P
KD = D // P
EPS_LN = 1e-5
EPS_COS = 1e-8
TAPS = 3
SIM_SCALE = 1024.0
E0, R0 = 8, 16
LORA_SCALE = 2.0
MAX_THR = 0.125
HD1 = P // 8
NR1 = 2 * E0 - 1
R2 = 64
RANK_CUTS = [0, 8, 16, 32, 64]
H3, M3, DK3 = 16, 4, 8
HEADS = H3 * M3
FF = 1792
FC = FF // P
SPLIT_TOP = 4096.0
P_SCALE = 1024.0
SMALL_INT = 1024.0
X_SCALE = 2048.0
RMAX = bass.bass_isa.ReduceOp.max
STAT_OPS = 2
RSTD_OPS = 3


def xattn_ffn_program(nc, a, out):
    top = ExitStack()
    sems = {}

    def sem(name):
        if name not in sems:
            sems[name] = top.enter_context(nc.semaphore(name))
        return sems[name]

    with top:
        def sb(name, shape, dt, ctx=top):
            return ctx.enter_context(nc.sbuf_tensor(name, shape, dt))

        x = sb("x", [P, TILES, D], F32)
        wide = sb("wide", [P, 3 * FC * D], F32)
        wf = sb("wf", [P, 3, KD, D], F32)
        wo = sb("wo", [P, KD, D], F32)
        ident = sb("ident", [P, P], F32)
        ident16 = sb("ident16", [P, P], F16)
        scratch = sb("scratch", [P, D], BF16)
        ln_const = sb("ln_const", [P, 3], F32)
        mean_var = sb("mean_var", [P, 2, TILES, 2], F32)
        rstd = sb("rstd", [P, 2, TILES], F32)
        nmr = sb("nmr", [P, TILES], F32)
        small = sb("small", [P, 8], F32)
        held = sb("held", [P, 4], F32)
        wmax = sb("wmax", [P, TILES // 2 + 1], F32)
        ps = top.enter_context(nc.psum_tensor("ps", [P, 8, D], F32))

        def bk(n):
            return ps[:, n, :]

        at = [0]

        def carve(shape, dt=F32):
            n = 1
            for s in shape:
                n *= s
            words = n * (2 if dt == F16 else 4) // 4
            v = wide[:, at[0]:at[0] + words]
            at[0] += words
            v = v if dt == F32 else v.bitcast(dt)
            if len(shape) == 2:
                v = v.rearrange("p (a b) -> p a b", a=shape[0])
            elif len(shape) == 3:
                v = v.rearrange("p (a b c) -> p a b c", a=shape[0], b=shape[1])
            return v

        HC = {"f0": E0 * R0 + E0 + 1, "f1": E0 * R0 + NR1, "f2": R2 + 4}
        RK = {"f0": E0 * R0, "f1": E0 * R0, "f2": R2}
        FFN = {"f0": 0, "f1": 1, "f2": 2}
        LNQ = {"x0": 0, "f0": 1, "x1": 2, "f1": 3, "x2": 4, "f2": 5, "x3": 6, "f3": 7}
        wbase = {f: carve([KD, D]) for f in HC}
        wag = {f: carve([KD, HC[f]]) for f in HC}
        wb = {f: carve([D]) for f in HC}
        bias = {f: carve([D]) for f in HC}
        wnat = carve([3, KD, D])
        b3rep = carve([3, KD, P])
        csel = carve([TILES, TAPS, P], F16)
        assert at[0] <= 3 * FC * D, at[0]

        mixv = wide[:, 0:KD * D]
        tmix = mixv[:, 0:KD * P].rearrange("p (c n) -> p c n", c=KD)
        m4 = mixv[:, KD * P:(KD + 1) * P]
        ip = mixv[:, (KD + 1) * P:(KD + 2) * P]
        irep = mixv[:, (KD + 2) * P:(KD + 2) * P + KD * M3].rearrange("p (c n) -> p c n", c=KD)
        amp = mixv[:, (KD + 2) * P + KD * M3:(KD + 2) * P + KD * M3 + 1]
        LATE_FC = 4
        LATE = (3 * FC - LATE_FC) * D
        b3 = wide[:, LATE:LATE + 3 * D].rearrange("p (w n) -> p w n", w=3)
        bo = wide[:, LATE + 3 * D:LATE + 4 * D]

        def hold(dve):
            nc.vector.memset(small[0:1, 0:1], 0.0)

        def hold_pool(cell=3):
            nc.gpsimd.tensor_tensor(held[0:1, cell:cell + 1], ln_const[0:1, 0:1], ln_const[0:1, 1:2], ALU.add)

        def after(eng, s, value):
            if not isinstance(value, int) or value > 0:
                eng.wait_ge(s, value)

        def stats(act, q, t):
            s, n = sem("stats"), STAT_OPS * (TILES * q + t)
            after(act, s, n)
            nc.scalar.activation(scratch[:, :], x[:, t, :], ACT.Copy, scale=-1.0 / D,
                                 accum_out=mean_var[:, q % 2, t, 0:1]).then_inc(s, 1)
            act.wait_ge(s, n + 1)
            nc.scalar.activation(scratch[:, :], x[:, t, :], ACT.Square, bias=mean_var[:, q % 2, t, 0:1],
                                 accum_out=mean_var[:, q % 2, t, 1:2]).then_inc(s, 1)

        def pool_rstd(pool, q, t):
            s, n = sem("rstd"), RSTD_OPS * (TILES * q + t)
            r = col(rstd[:, q % 2, :], t)
            pool.wait_ge(sem("stats"), STAT_OPS * (TILES * q + t + 1))
            hold_pool(0)
            nc.gpsimd.tensor_tensor(small[:, 5:6], mean_var[:, q % 2, t, 1:2], ln_const[:, 0:1], ALU.add).then_inc(s, 1)
            pool.wait_ge(s, n + 1)
            nc.gpsimd.tensor_tensor(small[:, 6:7], small[:, 5:6], ln_const[:, 1:2], ALU.pow).then_inc(s, 1)
            pool.wait_ge(s, n + 2)
            hold_pool(1)
            nc.gpsimd.tensor_tensor(r, small[:, 6:7], ln_const[:, 2:3], ALU.mult).then_inc(s, 1)

        def col(v, t):
            return v[:, t:t + 1] if isinstance(t, int) else v[:, bass.ds(t, 1)]

        def normalise(dve, q, t, dst, done):
            dve.wait_ge(sem("rstd"), RSTD_OPS * (TILES * q + t + 1))
            nc.vector.tensor_scalar(dst, x[:, t, :], mean_var[:, q % 2, t, 0:1], col(rstd[:, q % 2, :], t),
                                    ALU.add, ALU.mult).then_inc(done, 1)

        def all_tiles(eng, body, first=0, last=TILES):
            if first == 0:
                body(0, 0)
                body(1, 1)
                first = 2
            with eng.Fori(first // 2, last // 2) as i:
                for par in range(2):
                    body(2 * i + par, par)

        def pipelined(eng, body):
            for t in (0, 1):
                body(t, t, 0)
            with eng.Fori(1, TILES // 2 - 2) as i:
                for par in range(2):
                    body(2 * i + par, par, i)
            for t in range(TILES - 4, TILES):
                body(t, t % 2, t // 2)

        def inside(t):
            return not isinstance(t, int) or 0 <= t < TILES

        def loads(n, par, pair, ahead=0):
            return n * (pair + (par + ahead) // 2 + 1)

        def folds_at(t):
            outside = [0, 1] + list(range(TILES - 4, TILES))
            if isinstance(t, int) and t in outside:
                n = outside.index(t)
                return (2 * n, 2 * n + 1)
            return ()

        def transpose4(dst, src, idm=ident):
            for k in range(KD):
                last = nc.tensor.transpose(dst[:, k * P:(k + 1) * P], src[:, k * P:(k + 1) * P], idm[:, :])
            return last

        xv = a["x"].rearrange("(t p) d -> t p d", p=P)
        ctxv = a["ctx"].rearrange("(t p) d -> t p d", p=P)
        ctxTv = a["ctxT"]
        outv = out.rearrange("(t p) d -> t p d", p=P)

        with ExitStack() as c1:
            def s1(name, shape, dt=F32):
                return sb(name, shape, dt, c1)
            erow = s1("erow", [P, 2, D])
            eT = s1("eT", [P, 2, KD, P])
            xn = s1("xn", [P, 2, D])
            xnT = s1("xnT", [P, 2, KD, P])
            fpad = s1("fpad", [P, 2, D + 2])
            fs = wf[:].rearrange("p w k n -> p (w k n)")[:, 0:2 * TAPS * D].rearrange("p (b k n) -> p b k n", b=2,
                                                                                      k=TAPS)
            ebuf = s1("ebuf", [P, 2, D])
            ebuf2 = s1("ebuf2", [P, 2, D])
            simr = s1("simr", [32, 5, D])
            sim_h = s1("sim_h", [96, D], F16)
            sim_l = s1("sim_l", [96, D], F16)
            pick = s1("pick", [P, TILES, B])
            convw = s1("convw", [P, TAPS, P])
            g8 = s1("g8", [P, P])
            kvm = s1("kvm", [P, 2, P])
            pmat = s1("pmat", [P, 2, P])
            hw = s1("hw", [P, 2, P])
            hwT = s1("hwT", [P, 2, P])
            gs = s1("gs", [P, 2, 64])
            sm = s1("sm", [P, 2, 8])
            tmp15 = s1("tmp15", [P, E0, NR1])
            emap = s1("emap", [P, E0, NR1])
            emap_i = s1("emap_i", [P, NR1], I32)
            emap_f = s1("emap_f", [P, NR1])
            rb1 = s1("rb1", [P, NR1])
            gb2 = s1("gb2", [P, 4])
            nbthr = s1("nbthr", [P, 2])
            CROWS = 12
            CTX_LOADS = ((0, 2), (2, 4), (4, 8), (8, 12), (12, TILES))
            crow = wf[:].rearrange("p w k n -> p (w k) n")
            block = c1.enter_context(nc.Block())

            def context_tiles(eng, body):
                for n, (lo, hi) in enumerate(CTX_LOADS):
                    eng.wait_ge(sem(f"ld_c{n}"), 16)
                    if hi - lo < 4:
                        for t in range(lo, hi):
                            body(t, t % 2, t)
                    else:
                        with eng.Fori(lo // 2, hi // 2) as i:
                            for par in range(2):
                                body(2 * i + par, par, 2 * i + par - lo // CROWS * CROWS)

            @block.sync
            def _(sp):
                sp.dma_start(pick[:], a["c_pick"]).then_inc(sem("ld_pick"), 16)
                for n, (lo, hi) in enumerate(CTX_LOADS):
                    if hi > CROWS:
                        sp.wait_ge(sem("sq_done"), hi - CROWS)
                        sp.wait_ge(sem("dp_done"), hi - CROWS)
                    sp.dma_start(crow[:, lo % CROWS:lo % CROWS + hi - lo, :],
                                 ctxv[lo:hi].rearrange("t p d -> p t d")).then_inc(sem(f"ld_c{n}"), 16)
                for h in range(2):
                    sp.dma_start(x[:, 8 * h:8 * h + 8, :], xv[8 * h:8 * h + 8].rearrange("t p d -> p t d")).then_inc(
                        sem(f"ld_x_{h}"), 16)
                sp.dma_start(csel[0:96], a["c_sel"]).then_inc(sem("ld_conv"), 16)
                sp.dma_start(convw[:], a["convw"]).then_inc(sem("ld_conv"), 16)
                sp.dma_start(ident[:], a["c_ident"]).then_inc(sem("ld_conv"), 16)
                sp.dma_start(nbthr[:, 0:1], a["thr_b"].partition_broadcast(P)).then_inc(sem("ld_small"), 16)
                sp.dma_start(rb1[:], a["router_b"].partition_broadcast(P)).then_inc(sem("ld_small"), 16)
                sp.dma_start(emap_i[:], a["expert_map"].partition_broadcast(P)).then_inc(sem("ld_small"), 16)
                sp.dma_start(gb2[:], a["gate_b2"].partition_broadcast(P)).then_inc(sem("ld_small"), 16)
                sp.dma_start(g8[:], a["c_g8"]).then_inc(sem("ld_small"), 16)
                for f in ("f0", "f1", "f2"):
                    w = sem(f"ld_{f}")
                    sp.dma_start(wbase[f], a[f"{f}_base"].rearrange("(k p) n -> p k n", p=P)).then_inc(w, 16)
                    sp.dma_start(wag[f], a[f"{f}_ag"].rearrange("(k p) n -> p k n", p=P)).then_inc(w, 16)
                    sp.dma_start(wb[f][0:RK[f]], a[f"{f}_b"]).then_inc(w, 16)
                    sp.dma_start(bias[f], a[f"{f}_bias"].partition_broadcast(P)).then_inc(w, 16)

                def load_rows(t, par):
                    sp.dma_start(erow[:, par, :], ctxv[t]).then_inc(sem(f"ld_rows_{par}"), 16)

                def load_T(t, par):
                    sp.dma_start(eT[:, par], ctxTv[t]).then_inc(sem(f"ld_cols_{par}"), 16)

                for par in range(2):
                    load_rows(par, par)
                    load_T(par, par)

                def more1(t, par):
                    sp.wait_ge(sem("x1_ek"), t - 1)
                    load_rows(t, par)
                    sp.wait_ge(sem("x1_kv"), t - 1)
                    load_T(t, par)
                all_tiles(sp, more1, 2)
                sp.dma_start(wnat, a["w3"].rearrange("w (k p) n -> p w k n", p=P)).then_inc(sem("ld_w3"), 16)
                sp.dma_start(wo[:], a["wo3"].rearrange("(k p) n -> p k n", p=P)).then_inc(sem("ld_w3"), 16)
                sp.dma_start(b3rep, a["b3rep"].rearrange("w (k p) n -> p w k n", p=P)).then_inc(sem("ld_w3"), 16)
                sp.dma_start(irep, a["irep"].rearrange("(k p) n -> p k n", p=P)).then_inc(sem("ld_mix"), 16)
                sp.dma_start(m4, a["c_m4"]).then_inc(sem("ld_mix"), 16)
                sp.dma_start(ip, a["c_ip"]).then_inc(sem("ld_mix"), 16)
                sp.dma_start(amp, a["amp"].partition_broadcast(P)).then_inc(sem("ld_mix"), 16)
                sp.dma_start(ident16[:], a["c_ident16"]).then_inc(sem("ld_mix"), 16)
                sp.wait_ge(sem("x1_ek"), TILES)
                sp.wait_ge(sem("x1_kv"), TILES)
                for par in range(2):
                    load_T(par, par)
                    load_rows(par, par)

                def more2(t, par):
                    sp.wait_ge(sem("x2_s"), t - 1)
                    load_T(t, par)
                    sp.wait_ge(sem("x2_out"), t - 1)
                    load_rows(t, par)
                all_tiles(sp, more2, 2)

            @block.gpsimd
            def _(pool):
                nc.gpsimd.memset(ln_const[:, 0:1], D * EPS_LN)
                nc.gpsimd.memset(ln_const[:, 1:2], -0.5)
                nc.gpsimd.memset(ln_const[:, 2:3], float(D) ** 0.5)
                nc.gpsimd.memset(ebuf2[:, :, 0:1], 0.0)
                nc.gpsimd.memset(fpad[:, :, 0:1], 0.0)
                nc.gpsimd.memset(fpad[:, :, D + 1:D + 2], 0.0)
                nc.gpsimd.memset(pmat[:, :, :], 0.0).then_inc(sem("zeros"), 1)
                pool.wait_ge(sem("zeros"), 1)
                all_tiles(pool, lambda t, par: pool_rstd(pool, 0, t))
                for ph in ("x0", "f0", "x1", "f1", "x2", "f2"):
                    q = LNQ[ph]
                    if ph[0] == "f":
                        pool.wait_ge(sem(f"ld_{ph}"), 64)

                    def rstd_of(t, q=q):
                        pool_rstd(pool, q + 1, t)
                        if q + 1 == 2:
                            pool.wait_ge(sem("rstd"), RSTD_OPS * (TILES * 2 + t + 1))
                            hold_pool(2)
                            nc.gpsimd.tensor_tensor(col(nmr, t), mean_var[:, 0, t, 0:1], col(rstd[:, 0, :], t),
                                                    ALU.mult).then_inc(sem("nmr"), 1)

                    def body(t, par, ph=ph):
                        if ph[0] == "f":
                            pool.wait_ge(sem(f"{ph}_xn"), t + 1)
                            nc.gpsimd.tensor_tensor(x[:, t, :], x[:, t, :], bias[ph], ALU.add).then_inc(
                                sem(f"{ph}_biased"), 1)
                        if inside(t - 2):
                            rstd_of(t - 2)
                    all_tiles(pool, body)
                    rstd_of(TILES - 2)
                    rstd_of(TILES - 1)

            @block.vector
            def _(dve):
                dve.wait_ge(sem("zeros"), 1)

                def neighbours(t, par, slot):
                    after(dve, sem("sim_mm"), t - 1)
                    nc.vector.tensor_tensor(ebuf2[:, par, 1:D], crow[:, slot, 1:D], crow[:, slot, 0:D - 1],
                                            ALU.mult).then_inc(sem("dp_done"), 1)
                context_tiles(dve, neighbours)
                ss = sem("sim_steps")
                dve.wait_ge(sem("sim_mm"), TILES)
                nn, dd = ps[0:32, 0, :], ps[0:32, 1, :]
                nc.vector.tensor_scalar(simr[:, 1, :], nn, EPS_COS * EPS_COS, None, ALU.max).then_inc(ss, 1)
                rs, rn = sem("rnorm"), simr[:, 2, :]
                dve.wait_ge(rs, 1)
                nc.vector.reciprocal(rn, simr[:, 3, :]).then_inc(rs, 1)
                dve.wait_ge(rs, 2)
                nc.vector.tensor_tensor(simr[:, 4, :], rn, rn, ALU.mult).then_inc(rs, 1)
                dve.wait_ge(rs, 3)
                nc.vector.tensor_tensor(simr[:, 4, :], simr[:, 4, :], simr[:, 1, :], ALU.mult).then_inc(rs, 1)
                dve.wait_ge(rs, 4)
                nc.vector.tensor_scalar(simr[:, 4, :], simr[:, 4, :], -0.5, 1.5, ALU.mult, ALU.add).then_inc(rs, 1)
                dve.wait_ge(rs, 5)
                nc.vector.tensor_tensor(rn, rn, simr[:, 4, :], ALU.mult).then_inc(rs, 1)
                dve.wait_ge(rs, 6)
                nc.vector.tensor_tensor(simr[:, 3, :], nn, rn, ALU.mult).then_inc(ss, 1)
                dve.wait_ge(ss, 2)
                nc.vector.scalar_tensor_tensor(simr[:, 3, :], simr[:, 3, :], SIM_SCALE, rn, ALU.mult, ALU.mult).then_inc(ss, 1)
                nc.vector.scalar_tensor_tensor(simr[:, 4, :], rn, SIM_SCALE, dd, ALU.mult, ALU.mult).then_inc(ss, 1)
                dve.wait_ge(ss, 4)
                nc.vector.memset(simr[:, 1, :], 0.0).then_inc(ss, 1)
                dve.wait_ge(ss, 5)
                nc.vector.tensor_tensor(simr[:, 1, 1:D], simr[:, 4, 1:D], simr[:, 2, 0:D - 1], ALU.mult).then_inc(ss, 1)
                dve.wait_ge(ss, 6)
                nc.vector.memset(simr[:, 0, :], 0.0).then_inc(ss, 1)
                dve.wait_ge(ss, 7)
                nc.vector.tensor_copy(simr[:, 0, 0:D - 1], simr[:, 1, 1:D]).then_inc(ss, 1)
                dve.wait_ge(ss, 8)
                for g, src in enumerate((1, 3, 0)):
                    nc.vector.tensor_copy(sim_h[32 * g:32 * g + 32, :], simr[:, src, :]).then_inc(ss, 1)
                for g, src in enumerate((1, 3, 0)):
                    dve.wait_ge(ss, 9 + g)
                    nc.vector.tensor_copy(simr[:, 4, :], sim_h[32 * g:32 * g + 32, :]).then_inc(ss, 1)
                    dve.wait_ge(ss, 12 + 2 * g)
                    nc.vector.tensor_tensor(sim_l[32 * g:32 * g + 32, :], simr[:, src, :], simr[:, 4, :],
                                            ALU.subtract).then_inc(ss, 1)
                    dve.wait_ge(ss, 13 + 2 * g)

                def taps_norm(t, par):
                    normalise(dve, 0, t, fpad[:, par, 1:D + 1], sem("x0_xn"))

                def x0_finish(t, par):
                    dve.wait_ge(sem("x0_conv"), t + 1)
                    nc.vector.tensor_tensor(x[:, t, :], x[:, t, :], bk(6 + par), ALU.add).then_inc(sem("x0_x"), 1)

                def taps(t, par, pair):
                    dve.wait_ge(sem("x0_xn"), t + 1)
                    dve.wait_ge(sem("x0_sel"), t + 1)
                    for k in range(TAPS):
                        nc.vector.scalar_tensor_tensor(fs[:, par, k, :], fpad[:, par, k:k + D], 1.0 / SIM_SCALE,
                                                       bk(TAPS * par + k), ALU.mult, ALU.mult).then_inc(sem("x0_fs"), 1)
                    if inside(t + 1):
                        after(dve, sem("x0_fs"), TAPS * t)
                        taps_norm(t + 1, 1 - par)
                    if inside(t - 1):
                        x0_finish(t - 1, 1 - par)
                taps_norm(0, 0)
                pipelined(dve, taps)
                x0_finish(TILES - 1, 1)

                def ffn(ph, gate, steps):
                    q = LNQ[ph]

                    def norm(t, par):
                        normalise(dve, q, t, xn[:, par, :], sem(f"{ph}_xn"))

                    def gates(t, par):
                        dve.wait_ge(sem(f"{ph}_h"), t + 1)
                        gate(t, par, steps * t)

                    def finish(t, par):
                        dve.wait_ge(sem(f"{ph}_out"), t + 1)
                        dve.wait_ge(sem(f"{ph}_biased"), t + 1)
                        nc.vector.tensor_tensor(x[:, t, :], x[:, t, :], bk(2 + par), ALU.add).then_inc(sem(f"{ph}_x"), 1)

                    def body(t, par, pair):
                        if inside(t + 1):
                            gates(t + 1, 1 - par)
                        if inside(t + 3):
                            norm(t + 3, 1 - par)
                        if inside(t - 1):
                            finish(t - 1, 1 - par)
                    norm(0, 0)
                    norm(1, 1)
                    gates(0, 0)
                    dve.wait_ge(sem(f"{ph}_tr"), 1)
                    norm(2, 0)
                    pipelined(dve, body)
                    finish(TILES - 1, 1)

                def gate0(t, par, n):
                    s, hb, g = sem("f0_gate"), bk(4 + par), gs[:, par, :]
                    hr = E0 * R0
                    nc.vector.reduce_max(g[:, 0:1], hb[:, hr:hr + E0], AX.X, negate=True).then_inc(s, 1)
                    dve.wait_ge(sem("f0_exp"), 2 * t + 2)
                    nc.vector.tensor_scalar(g[:, 2:3], g[:, 32:33], 1.0, None, ALU.add).then_inc(s, 1)
                    nc.vector.reciprocal(g[:, 3:4], g[:, 1:2]).then_inc(s, 1)
                    dve.wait_ge(s, n + 3)
                    nc.vector.reciprocal(g[:, 4:5], g[:, 2:3]).then_inc(s, 1)
                    dve.wait_ge(s, n + 4)
                    nc.vector.tensor_scalar(g[:, 5:6], g[:, 4:5], MAX_THR, None, ALU.mult).then_inc(s, 1)
                    dve.wait_ge(s, n + 5)
                    nc.vector.tensor_scalar(g[:, 16:24], g[:, 8:16], g[:, 3:4], g[:, 5:6], ALU.mult,
                                            ALU.subtract).then_inc(s, 1)
                    dve.wait_ge(s, n + 6)
                    nc.vector.tensor_scalar(g[:, 24:32], g[:, 16:24], 0.0, None, ALU.max).then_inc(s, 1)
                    dve.wait_ge(s, n + 7)
                    nc.vector.reduce_sum(g[:, 6:7], g[:, 24:32], AX.X).then_inc(s, 1)
                    dve.wait_ge(s, n + 8)
                    nc.vector.scalar_tensor_tensor(g[:, 7:8], g[:, 6:7], 0.0, g[:, 6:7], ALU.is_equal, ALU.add).then_inc(s, 1)
                    dve.wait_ge(s, n + 9)
                    nc.vector.reciprocal(g[:, 40:41], g[:, 7:8]).then_inc(s, 1)
                    dve.wait_ge(s, n + 10)
                    nc.vector.tensor_scalar(g[:, 48:56], g[:, 24:32], g[:, 40:41], LORA_SCALE, ALU.mult,
                                            ALU.mult).then_inc(s, 1)
                    dve.wait_ge(s, n + 11)
                    nc.vector.tensor_tensor(hw[:, par, :].rearrange("p (e r) -> p e r", e=E0),
                                            hb[:, 0:hr].rearrange("p (e r) -> p e r", e=E0),
                                            g[:, 48:56].unsqueeze(2).broadcast_to([P, E0, R0]), ALU.mult).then_inc(
                                                sem("hw_rows"), 1)

                def gate1(t, par, n):
                    s, hb, g = sem("f1_gate"), bk(4 + par), gs[:, par, :]
                    hr = E0 * R0
                    nc.vector.tensor_tensor(g[:, 16:16 + NR1], hb[:, hr:hr + NR1], rb1[:], ALU.add).then_inc(s, 1)
                    dve.wait_ge(s, n + 1)
                    nc.vector.reduce_max(g[:, 0:1], g[:, 16:16 + NR1], AX.X, negate=True).then_inc(s, 1)
                    dve.wait_ge(sem("f1_exp"), t + 1)
                    nc.vector.reciprocal(g[:, 3:4], g[:, 1:2]).then_inc(s, 1)
                    nc.vector.max(g[:, 8:16], g[:, 32:32 + NR1]).then_inc(s, 1)
                    dve.wait_ge(s, n + 4)
                    hold(dve)
                    nc.vector.match_replace(g[:, 48:48 + NR1], g[:, 8:16], g[:, 32:32 + NR1], -1.0).then_inc(s, 1)
                    dve.wait_ge(s, n + 5)
                    nc.vector.scalar_tensor_tensor(g[:, 48:48 + NR1], g[:, 48:48 + NR1], 0.0, g[:, 32:32 + NR1],
                                                   ALU.is_lt, ALU.mult).then_inc(s, 1)
                    dve.wait_ge(s, n + 6)
                    nc.vector.tensor_tensor(tmp15[:], emap[:], g[:, 48:48 + NR1].unsqueeze(1).broadcast_to([P, E0, NR1]),
                                            ALU.mult).then_inc(s, 1)
                    dve.wait_ge(s, n + 7)
                    nc.vector.reduce_sum(g[:, 8:16], tmp15[:], AX.X).then_inc(s, 1)
                    dve.wait_ge(s, n + 8)
                    nc.vector.tensor_scalar(g[:, 16:24], g[:, 8:16], g[:, 3:4], LORA_SCALE, ALU.mult, ALU.mult).then_inc(s, 1)
                    dve.wait_ge(s, n + 9)
                    nc.vector.tensor_tensor(hw[:, par, :].rearrange("p (e r) -> p e r", e=E0),
                                            hb[:, 0:hr].rearrange("p (e r) -> p e r", e=E0),
                                            g[:, 16:24].unsqueeze(2).broadcast_to([P, E0, R0]), ALU.mult).then_inc(
                                                sem("hw_rows"), 1)

                def gate2(t, par, n):
                    s, hb, g = sem("f2_gate"), bk(4 + par), gs[:, par, :]
                    nc.vector.tensor_tensor(g[:, 0:4], hb[:, R2:R2 + 4], gb2[:], ALU.add).then_inc(s, 1)
                    dve.wait_ge(s, n + 1)
                    nc.vector.tensor_tensor(g[:, 4:5], g[:, 0:1], g[:, 1:2], ALU.max).then_inc(s, 1)
                    nc.vector.tensor_tensor(g[:, 5:6], g[:, 2:3], g[:, 3:4], ALU.max).then_inc(s, 1)
                    dve.wait_ge(s, n + 3)
                    nc.vector.tensor_tensor(g[:, 6:7], g[:, 4:5], g[:, 2:3], ALU.max).then_inc(s, 1)
                    nc.vector.tensor_tensor(g[:, 7:8], g[:, 5:6], g[:, 1:2], ALU.max).then_inc(s, 1)
                    nc.vector.tensor_tensor(g[:, 10:11], g[:, 5:6], g[:, 4:5], ALU.is_gt).then_inc(s, 1)
                    dve.wait_ge(s, n + 5)
                    nc.vector.tensor_tensor(g[:, 9:10], g[:, 7:8], g[:, 0:1], ALU.is_gt).then_inc(s, 1)
                    nc.vector.tensor_tensor(g[:, 11:12], g[:, 3:4], g[:, 6:7], ALU.is_gt).then_inc(s, 1)
                    dve.wait_ge(s, n + 8)
                    nc.vector.tensor_copy(hw[:, par, 0:RANK_CUTS[1]], hb[:, 0:RANK_CUTS[1]]).then_inc(s, 1)
                    for c in range(1, 4):
                        lo, hi = RANK_CUTS[c], RANK_CUTS[c + 1]
                        last = nc.vector.tensor_scalar(hw[:, par, lo:hi], hb[:, lo:hi], g[:, 8 + c:9 + c], None, ALU.mult)
                        last.then_inc(s if c < 3 else sem("hw_rows"), 1)

                dve.wait_ge(sem("ld_small"), 80)
                nc.vector.tensor_scalar(nbthr[:, 1:2], nbthr[:, 0:1], -1.0, None, ALU.mult).then_inc(sem("nbthr"), 1)
                ffn("f0", gate0, 11)

                def kmax(t, par, count):
                    dve.wait_ge(sem(f"ld_rows_{par}"), count)
                    nc.vector.reduce_max(sm[:, par, 0:1], erow[:, par, :], AX.X, negate=True).then_inc(sem("x1_kmax"), 1)

                def rk(t, par):
                    dve.wait_ge(sem("x1_ek"), t + 1)
                    nc.vector.reciprocal(sm[:, par, 2:3], sm[:, par, 1:2]).then_inc(sem("x1_rk"), 1)

                def x1_finish(t, par):
                    dve.wait_ge(sem("x1_rd"), t + 1)
                    nc.vector.tensor_tensor(xn[:, par, :], xn[:, par, :], bk(4 + par), ALU.mult).then_inc(sem("x1_x"), 1)
                    dve.wait_ge(sem("x1_x"), 2 * t + 1)
                    nc.vector.tensor_tensor(x[:, t, :], x[:, t, :], xn[:, par, :], ALU.add).then_inc(sem("x1_x"), 1)

                def lin(t, par, pair):
                    dve.wait_ge(sem("x1_kv"), t + 1)
                    dve.wait_ge(sem("x1_rk"), t + 1)
                    nc.vector.scalar_tensor_tensor(kvm[:, par, :], ps[:, 2 + par, 0:P], sm[:, par, 2:3], g8[:], ALU.mult,
                                                   ALU.mult).then_inc(sem("x1_kvm"), 1)
                    dve.wait_ge(sem("x1_den"), t + 1)
                    nc.vector.reciprocal(gs[:, par, :], ps[:, par, 0:KD * HD1]).then_inc(sem("x1_rden"), 1)
                    if inside(t + 2):
                        kmax(t + 2, par, loads(16, par, pair, 2))
                    if inside(t + 1):
                        rk(t + 1, 1 - par)
                    if inside(t - 1):
                        x1_finish(t - 1, 1 - par)
                kmax(0, 0, 16)
                kmax(1, 1, 16)
                rk(0, 0)
                pipelined(dve, lin)
                x1_finish(TILES - 1, 1)

                nc.vector.tensor_copy(emap_f[:], emap_i[:]).then_inc(sem("emap"), 1)
                dve.wait_ge(sem("emap"), 1)
                for e in range(E0):
                    nc.vector.tensor_scalar(emap[:, e, :], emap_f[:], float(e), None, ALU.is_equal).then_inc(sem("emap"), 1)
                dve.wait_ge(sem("emap"), 1 + E0)
                ffn("f1", gate1, 9)

                ms = sem("mix_steps")
                dve.wait_ge(sem("ld_mix"), 80)
                nc.vector.tensor_scalar(irep, irep, amp[:, 0:1], 0.1, ALU.mult, ALU.mult).then_inc(ms, 1)
                dve.wait_ge(ms, 1)
                for c in range(KD):
                    nc.vector.tensor_tensor(tmix[:, c, :].rearrange("p (h m d) -> p h m d", h=4, m=M3),
                                            irep[:, c, :].unsqueeze(1).unsqueeze(3).broadcast_to([P, 4, M3, DK3]),
                                            m4.rearrange("p (h m d) -> p h m d", h=4, m=M3), ALU.mult).then_inc(ms, 1)
                dve.wait_ge(ms, 1 + KD)
                for c in range(KD):
                    nc.vector.tensor_tensor(tmix[:, c, :], tmix[:, c, :], ip, ALU.add).then_inc(ms, 1)

                def x2_norm(t, par):
                    normalise(dve, 4, t, xn[:, par, :], sem("x2_xn"))

                def x2_max(t, par):
                    dve.wait_ge(sem("x2_s"), t + 1)
                    for b in range(BT):
                        r = slice(b * C, (b + 1) * C)
                        nc.vector.reduce_max(sm[r, par, 0:1], ps[r, 2 + par, b * C:(b + 1) * C], AX.X).then_inc(
                            sem("x2_m"), 1)
                    dve.wait_ge(sem("x2_m"), 3 * t + 2)
                    nc.vector.tensor_scalar(sm[:, par, 1:2], sm[:, par, 0:1], -float(C) ** -0.5, None,
                                            ALU.mult).then_inc(sem("x2_m"), 1)

                def x2_scale(t, par):
                    dve.wait_ge(sem("x2_e"), 2 * t + 2)
                    nc.vector.reciprocal(sm[:, par, 3:4], sm[:, par, 2:3]).then_inc(sem("x2_r"), 1)
                    dve.wait_ge(sem("x2_r"), 2 * t + 1)
                    nc.vector.tensor_scalar(pmat[:, par, :], pmat[:, par, :], sm[:, par, 3:4], None,
                                            ALU.mult).then_inc(sem("x2_r"), 1)

                def x2_finish(t, par):
                    dve.wait_ge(sem("x2_out"), t + 1)
                    nc.vector.tensor_tensor(x[:, t, :], x[:, t, :], bk(4 + par), ALU.add).then_inc(sem("x2_x"), 1)

                def chan(t, par, pair):
                    if inside(t + 1):
                        x2_max(t + 1, 1 - par)
                    if inside(t - 1):
                        x2_finish(t - 1, 1 - par)
                    if inside(t + 1):
                        x2_scale(t + 1, 1 - par)
                    if inside(t + 3):
                        x2_norm(t + 3, 1 - par)
                x2_norm(0, 0)
                x2_norm(1, 1)
                x2_max(0, 0)
                x2_scale(0, 0)
                dve.wait_ge(sem("x2_tr"), 1)
                x2_norm(2, 0)
                pipelined(dve, chan)
                x2_finish(TILES - 1, 1)
                ffn("f2", gate2, 11)

            @block.scalar
            def _(act):
                def squares(t, par, slot):
                    after(act, sem("sim_mm"), t - 1)
                    nc.scalar.activation(ebuf[:, par, :], crow[:, slot, :], ACT.Square).then_inc(sem("sq_done"), 1)
                context_tiles(act, squares)

                act.wait_ge(sem("sim_steps"), 1)
                nc.scalar.activation(simr[:, 3, :], simr[:, 1, :], ACT.Sqrt).then_inc(sem("rnorm"), 1)

                act.wait_ge(sem("zeros"), 1)
                act.wait_ge(sem("ld_x_0"), 16)
                all_tiles(act, lambda t, par: stats(act, 0, t), 0, TILES // 2)
                act.wait_ge(sem("ld_x_1"), 16)
                all_tiles(act, lambda t, par: stats(act, 0, t), TILES // 2, TILES)

                def stats_of(ph, t, per_tile=1):
                    act.wait_ge(sem(f"{ph}_x"), per_tile * (t + 1))
                    stats(act, LNQ[ph] + 1, t)
                all_tiles(act, lambda t, par: stats_of("x0", t))

                def xt_copy(ph, t, par):
                    act.wait_ge(sem(f"{ph}_tr"), t + 1)
                    nc.scalar.activation(xnT[:, par].rearrange("p k n -> p (k n)"), bk(par), ACT.Copy).then_inc(
                        sem(f"{ph}_xnT"), 1)

                def ffn(ph, gate):
                    def body(t, par, pair):
                        if inside(t + 1):
                            gate(t + 1, 1 - par)
                        act.wait_ge(sem("hwTr"), TILES * FFN[ph] + t + 1)
                        nc.scalar.activation(hwT[0:RK[ph], par, :], ps[0:RK[ph], 4 + par, 256:384], ACT.Copy).then_inc(
                            sem("hwT"), 1)
                        if inside(t + 2):
                            xt_copy(ph, t + 2, par)
                        if inside(t - 2):
                            stats_of(ph, t - 2)
                    xt_copy(ph, 0, 0)
                    xt_copy(ph, 1, 1)
                    gate(0, 0)
                    pipelined(act, body)
                    stats_of(ph, TILES - 2)
                    stats_of(ph, TILES - 1)

                def gate0(t, par):
                    g, hb, hr = gs[:, par, :], bk(4 + par), E0 * R0
                    act.wait_ge(sem("f0_gate"), 11 * t + 1)
                    nc.scalar.activation(g[:, 8:16], hb[:, hr:hr + E0], ACT.Exp, bias=g[:, 0:1], accum_out=g[:, 1:2]).then_inc(
                        sem("f0_exp"), 1)
                    nc.scalar.activation(g[:, 32:33], hb[:, hr + E0:hr + E0 + 1], ACT.Exp, bias=nbthr[:, 1:2],
                                         scale=-1.0).then_inc(sem("f0_exp"), 1)

                def gate1(t, par):
                    g = gs[:, par, :]
                    act.wait_ge(sem("f1_gate"), 9 * t + 2)
                    nc.scalar.activation(g[:, 32:32 + NR1], g[:, 16:16 + NR1], ACT.Exp, bias=g[:, 0:1],
                                         accum_out=g[:, 1:2]).then_inc(sem("f1_exp"), 1)

                act.wait_ge(sem("nbthr"), 1)
                ffn("f0", gate0)

                def exp_k(t, par):
                    act.wait_ge(sem("x1_kmax"), t + 1)
                    nc.scalar.activation(ebuf2[:, par, :], erow[:, par, :], ACT.Exp, bias=sm[:, par, 0:1],
                                         accum_out=sm[:, par, 1:2]).then_inc(sem("x1_ek"), 1)

                def exp_q(t, par):
                    act.wait_ge(sem("nmr"), t + 1)
                    nc.scalar.activation(ebuf[:, par, :], x[:, t, :], ACT.Exp, bias=col(nmr, t),
                                         scale=col(rstd[:, 0, :], t)).then_inc(sem("x1_eq"), 1)

                def rden_spread(t, par):
                    act.wait_ge(sem("x1_rden"), t + 1)
                    nc.scalar.activation(xn[:, par, :].rearrange("p (h d) -> p h d", d=P // HD1),
                                         gs[:, par, :].unsqueeze(2).broadcast_to([P, KD * HD1, P // HD1]),
                                         ACT.Copy).then_inc(sem("x1_rx"), 1)

                def rd_copy(t, par):
                    act.wait_ge(sem("x1_nd"), t + 1)
                    nc.scalar.activation(xn[:, par, :], bk(6 + par), ACT.Copy).then_inc(sem("x1_rd"), 1)

                def lin(t, par, pair):
                    if inside(t + 1):
                        xt_copy("x1", t + 1, 1 - par)
                    if inside(t - 1):
                        rd_copy(t - 1, 1 - par)
                    rden_spread(t, par)
                    if inside(t + 2):
                        exp_k(t + 2, par)
                    if inside(t + 1):
                        exp_q(t + 1, 1 - par)
                    if inside(t - 2):
                        stats_of("x1", t - 2, 2)
                exp_k(0, 0)
                exp_k(1, 1)
                xt_copy("x1", 0, 0)
                exp_q(0, 0)
                pipelined(act, lin)
                rd_copy(TILES - 1, 1)
                stats_of("x1", TILES - 2, 2)
                stats_of("x1", TILES - 1, 2)
                ffn("f1", gate1)

                def exp_scores(t, par):
                    act.wait_ge(sem("x2_m"), 3 * t + 3)
                    after(act, sem("x2_out"), t - 1)
                    for b in range(BT):
                        r, cs = slice(b * C, (b + 1) * C), slice(b * C, (b + 1) * C)
                        nc.scalar.activation(pmat[r, par, cs], ps[r, 2 + par, cs], ACT.Exp, bias=sm[r, par, 1:2],
                                             scale=float(C) ** -0.5, accum_out=sm[r, par, 2:3]).then_inc(sem("x2_e"), 1)

                def fold_copy(n):
                    act.wait_ge(sem("fold_mm"), n + 1)
                    dst = wf[:, n // 4, n % 4, :] if n < 12 else b3[:, n - 12, :]
                    nc.scalar.activation(dst, bk(6 + n % 2), ACT.Copy).then_inc(sem("fold_out"), 1)

                def chan(t, par, pair):
                    if inside(t + 1):
                        exp_scores(t + 1, 1 - par)
                    if inside(t + 2):
                        xt_copy("x2", t + 2, par)
                    if inside(t - 2):
                        stats_of("x2", t - 2)
                    for n in folds_at(t):
                        fold_copy(n)
                xt_copy("x2", 0, 0)
                xt_copy("x2", 1, 1)
                exp_scores(0, 0)
                pipelined(act, chan)
                for n in range(12, 15):
                    fold_copy(n)
                stats_of("x2", TILES - 2)
                stats_of("x2", TILES - 1)
                ffn("f2", lambda t, par: None)

            @block.tensor
            def _(pe):
                pe.wait_ge(sem("ld_pick"), 16)
                for t in range(TILES):
                    par = t % 2
                    pe.wait_ge(sem("sq_done"), t + 1)
                    nc.tensor.matmul(ps[0:32, 0, :], pick[:, t, :], ebuf[:, par, :], start=t == 0, stop=t == TILES - 1)
                    pe.wait_ge(sem("dp_done"), t + 1)
                    nc.tensor.matmul(ps[0:32, 1, :], pick[:, t, :], ebuf2[:, par, :], start=t == 0,
                                     stop=t == TILES - 1).then_inc(sem("sim_mm"), 1)
                pe.wait_ge(sem("ld_conv"), 48)
                pe.wait_ge(sem("sim_steps"), 17)

                def spread(t, par):
                    after(pe, sem("x0_fs"), TAPS * (t - 1))
                    for k in range(TAPS):
                        sel = csel[0:96, t, k, :]
                        nc.tensor.matmul(bk(TAPS * par + k), sel, sim_h[:, :], start=True, stop=False)
                        last = nc.tensor.matmul(bk(TAPS * par + k), sel, sim_l[:, :], start=False, stop=True)
                    last.then_inc(sem("x0_sel"), 1)

                def conv(t, par, pair):
                    if inside(t + 1):
                        spread(t + 1, 1 - par)
                    pe.wait_ge(sem("x0_fs"), TAPS * t + TAPS)
                    after(pe, sem("x0_x"), t - 1)
                    for k in range(TAPS):
                        last = nc.tensor.matmul(bk(6 + par), convw[:, k, :], fs[:, par, k, :], start=k == 0,
                                                stop=k == TAPS - 1)
                    last.then_inc(sem("x0_conv"), 1)
                spread(0, 0)
                pipelined(pe, conv)
                pe.wait_ge(sem("x0_x"), TILES)

                def ffn(ph):
                    n, rk, hcols = sem(f"{ph}_xnT"), RK[ph], HC[ph]

                    def rows(t, par):
                        pe.wait_ge(sem(f"{ph}_xn"), t + 1)
                        transpose4(bk(par), xn[:, par, :]).then_inc(sem(f"{ph}_tr"), 1)

                    def low_rank(t, par):
                        pe.wait_ge(n, t + 1)
                        for k in range(KD):
                            last = nc.tensor.matmul(ps[:, 4 + par, 0:hcols], xnT[:, par, k, :], wag[ph][:, k, :],
                                                    start=k == 0, stop=k == KD - 1)
                        last.then_inc(sem(f"{ph}_h"), 1)

                    def body(t, par, pair):
                        if inside(t + 1):
                            low_rank(t + 1, 1 - par)
                        after(pe, sem(f"{ph}_x"), t - 1)
                        for k in range(KD):
                            nc.tensor.matmul(bk(2 + par), xnT[:, par, k, :], wbase[ph][:, k, :], start=k == 0, stop=False)
                        pe.wait_ge(sem("hw_rows"), TILES * FFN[ph] + t + 1)
                        nc.tensor.transpose(ps[:, 4 + par, 256:384], hw[:, par, :], ident[:, :]).then_inc(
                            sem("hwTr"), 1)
                        if inside(t + 2):
                            rows(t + 2, par)
                        pe.wait_ge(sem("hwT"), TILES * FFN[ph] + t + 1)
                        nc.tensor.matmul(bk(2 + par), hwT[0:rk, par, :], wb[ph][0:rk, :], start=False,
                                         stop=True).then_inc(sem(f"{ph}_out"), 1)
                    rows(0, 0)
                    rows(1, 1)
                    low_rank(0, 0)
                    pipelined(pe, body)

                pe.wait_ge(sem("ld_f0"), 64)
                ffn("f0")

                def x1_rows(t, par):
                    pe.wait_ge(sem("x1_ek"), t + 1)
                    transpose4(bk(par), ebuf2[:, par, :]).then_inc(sem("x1_tr"), 1)

                def lin(t, par, pair):
                    pe.wait_ge(sem(f"ld_cols_{par}"), loads(16, par, pair))
                    pe.wait_ge(sem("x1_xnT"), t + 1)
                    after(pe, sem("x1_kvm"), t - 1)
                    for k in range(KD):
                        last = nc.tensor.matmul(ps[:, 2 + par, 0:P], xnT[:, par, k, :], eT[:, par, k, :], start=k == 0,
                                                stop=k == KD - 1)
                    last.then_inc(sem("x1_kv"), 1)
                    if inside(t - 1):
                        rden_rows(t - 1, 1 - par)
                    if inside(t + 1):
                        x1_rows(t + 1, 1 - par)
                    pe.wait_ge(sem("x1_eq"), t + 1)
                    for k in range(KD):
                        last = nc.tensor.matmul(ps[:, par, k * HD1:(k + 1) * HD1], ebuf[:, par, k * P:(k + 1) * P],
                                                g8[:, 0:P:P // HD1], start=True, stop=True)
                    last.then_inc(sem("x1_den"), 1)
                    pe.wait_ge(sem("x1_kvm"), t + 1)
                    after(pe, sem("x1_x"), 2 * (t - 1))
                    nc.tensor.matmul(bk(4 + par), kvm[:, par, :], ebuf[:, par, :], start=True, stop=True)

                def rden_rows(t, par):
                    pe.wait_ge(sem("x1_rx"), t + 1)
                    transpose4(bk(6 + par), xn[:, par, :]).then_inc(sem("x1_nd"), 1)
                pe.wait_ge(sem("ld_small"), 80)
                pe.wait_ge(sem("f0_x"), TILES)
                x1_rows(0, 0)
                pipelined(pe, lin)
                rden_rows(TILES - 1, 1)
                pe.wait_ge(sem("x1_x"), 2 * TILES)
                pe.wait_ge(sem("ld_f1"), 64)
                ffn("f1")

                def rows2(t, par):
                    pe.wait_ge(sem("x2_xn"), t + 1)
                    transpose4(bk(par), xn[:, par, :]).then_inc(sem("x2_tr"), 1)

                def scores2(t, par, count):
                    pe.wait_ge(sem("x2_xnT"), t + 1)
                    pe.wait_ge(sem(f"ld_cols_{par}"), 16 * TILES // 2 + count)
                    after(pe, sem("x2_e"), 2 * (t - 1))
                    for k in range(KD):
                        last = nc.tensor.matmul(ps[:, 2 + par, 0:P], xnT[:, par, k, :], eT[:, par, k, :], start=k == 0,
                                                stop=k == KD - 1)
                    last.then_inc(sem("x2_s"), 1)

                def chan(t, par, pair):
                    if inside(t + 1):
                        scores2(t + 1, 1 - par, loads(16, par, pair, 1))
                    if inside(t + 2):
                        rows2(t + 2, par)
                    pe.wait_ge(sem("x2_r"), 2 * t + 2)
                    pe.wait_ge(sem(f"ld_rows_{par}"), 16 * TILES // 2 + loads(16, par, pair))
                    after(pe, sem("x2_x"), t - 1)
                    nc.tensor.matmul(bk(4 + par), pmat[:, par, :], erow[:, par, :], start=True, stop=True).then_inc(
                        sem("x2_out"), 1)
                    for n in folds_at(t):
                        fold(n)

                def fold(n):
                    if n >= 2:
                        pe.wait_ge(sem("fold_out"), n - 1)
                    for c in range(KD):
                        w = wnat[:, n // 4, c, n % 4 * P:n % 4 * P + P] if n < 12 else b3rep[:, n - 12, c, :]
                        last = nc.tensor.matmul(ps[:, 6 + n % 2, c * P:(c + 1) * P], w, tmix[:, c, :], start=True,
                                                stop=True)
                    last.then_inc(sem("fold_mm"), 1)
                pe.wait_ge(sem("ld_w3"), 48)
                pe.wait_ge(sem("mix_steps"), 1 + 2 * KD)
                pe.wait_ge(sem("f1_x"), TILES)
                rows2(0, 0)
                rows2(1, 1)
                scores2(0, 0, 16)
                pipelined(pe, chan)
                for n in range(12, 15):
                    fold(n)
                pe.wait_ge(sem("x2_x"), TILES)
                pe.wait_ge(sem("ld_f2"), 64)
                ffn("f2")

        G3, J3, RG = 16, 4, 4
        ROUNDS = G3 // RG
        OPC = 256
        VW = 26
        NQ, NK, NV, NO = 6, 5, 5, 3
        FG, FU, FD = (wide[:, n * FC * D:(n + 1) * FC * D] for n in range(3))
        with ExitStack() as c2:
            def s2(name, shape, dt=F32):
                return sb(name, shape, dt, c2)
            xn = s2("xn3", [P, D])
            xT = s2("xT3", [P, KD, P])
            eT = s2("eT3", [P, 2, KD, P])
            p32 = s2("p32", [P, J3, RG, C])
            pth = s2("pth", [P, 2 * J3, P], F16)
            ptl = s2("ptl", [P, 2 * J3, P], F16)
            qT = s2("qT", [P, 2, G3, P], F16)
            kT = s2("kT", [P, 2, G3, P], F16)
            qrow = s2("qrow", [P, HEADS, 4, DK3], F16)
            krow = s2("krow", [P, HEADS, 4, DK3], F16)
            t32 = s2("t32", [P, 2, D])
            vc = s2("vc", [P, HEADS, 3, DK3], BF16)
            vd = s2("vd", [P, BT, G3 // 2, J3, 2, VW], BF16)
            orow = s2("orow", [P, D])
            osum = s2("osum", [P, 4 * RG, DK3])
            pf = p32[:].rearrange("p j g k -> p (j g k)")
            am = s2("am", [P, 16])
            sc = s2("sc", [P, 2])
            mx = s2("mx", [P, J3 * RG])
            rden = s2("rden", [P, 4 * RG])
            block = c2.enter_context(nc.Block())
            PAIRS = TILES // 2

            def weights_part(c):
                n = LATE // PAIRS
                return slice(c * n, (c + 1) * n) if isinstance(c, int) else bass.ds(c * n, n)

            def schedule(eng, body):
                body(0, 0, 0, True, False)
                body(1, 1, 0, False, False)
                with eng.Fori(1, PAIRS - 1) as i:
                    for par in range(2):
                        body(2 * i + par, par, i, False, False)
                body(TILES - 2, 0, PAIRS - 1, False, False)
                body(TILES - 1, 1, PAIRS - 1, False, True)

            @block.sync
            def _(sp):
                for par in range(2):
                    sp.dma_start(eT[:, par], ctxTv[par]).then_inc(sem(f"ld_x3_{par}"), 16)
                sp.dma_start(FG.bitcast(I32).rearrange("p (k n) -> p k n", k=KD),
                             a["gate_t"].rearrange("(k p) n -> p k n", p=P)).then_inc(sem("ld_ffn"), 16)
                sp.dma_start(FU.bitcast(I32).rearrange("p (k n) -> p k n", k=KD),
                             a["up_t"].rearrange("(k p) n -> p k n", p=P)).then_inc(sem("ld_ffn"), 16)
                sp.dma_start(bo, a["bo3"].partition_broadcast(P)).then_inc(sem("ld_bo"), 16)
                sp.dma_start(FD.bitcast(I32).rearrange("p (k n) -> p k n", k=FC)[:, 0:FC - LATE_FC],
                             a["down_t"].rearrange("(k p) n -> p k n", p=P)[:, 0:FC - LATE_FC]).then_inc(sem("ld_ffn"), 16)

                def more(t, par):
                    sp.wait_ge(sem("x3_v"), t - 1)
                    sp.dma_start(eT[:, par], ctxTv[t]).then_inc(sem(f"ld_x3_{par}"), 16)
                all_tiles(sp, more, 2)
                sp.wait_ge(sem("v_steps"), NV * (TILES - 1) + 1)
                sp.wait_ge(sem("x3_biased"), TILES)
                sp.dma_start(FD.bitcast(I32).rearrange("p (k n) -> p k n", k=FC)[:, FC - LATE_FC:],
                             a["down_t"].rearrange("(k p) n -> p k n", p=P)[:, FC - LATE_FC:]).then_inc(sem("ld_late"), 16)

            @block.gpsimd
            def _(pool):
                nc.gpsimd.memset(krow[:, :, 3, :], 0.0).then_inc(sem("zeros3"), 1)
                nc.gpsimd.memset(qrow[:, :, 3, :], 0.0).then_inc(sem("zeros3"), 1)
                nc.gpsimd.memset(vd[:].rearrange("p b g j h w -> p (b g j h w)"), 0.0).then_inc(sem("zeros3"), 1)
                pool.wait_ge(sem("zeros3"), 3)
                for hd in range(2):
                    r = slice(hd * C, (hd + 1) * C)
                    nc.gpsimd.memset(vd[r].rearrange("p b g j h w -> p (b g j) h w")[:, :, hd, 24:25], 1.0).then_inc(
                        sem("zeros3"), 1)

                def kmax(t):
                    pool.wait_ge(sem("k_steps"), NK * t + 2)
                    hold_pool()
                    nc.gpsimd.partition_all_reduce(am[:, 9:10], am[:, 8:9], P, RMAX).then_inc(sem("k_all"), 1)

                def body(t, par, pair, first, last, conv):
                    if conv is not None:
                        at = weights_part(conv)
                        nc.gpsimd.tensor_copy(wide[:, at], wide[:, at].bitcast(I32)).then_inc(sem("converted"), 1)
                    pool.wait_ge(sem("x3_xn"), t + 1)
                    nc.gpsimd.tensor_tensor(x[:, t, :], x[:, t, :], bo, ALU.add).then_inc(sem("x3_biased"), 1)
                    if not last:
                        kmax(t + 1)
                    if inside(t - 2):
                        pool_rstd(pool, 7, t - 2)
                pool.wait_ge(sem("zeros3"), 5)
                kmax(0)
                pool.wait_ge(sem("ld_bo"), 16)
                body(0, 0, 0, True, False, None)
                body(1, 1, 0, False, False, None)
                with pool.Fori(1, PAIRS // 2) as i:
                    for par in range(2):
                        body(2 * i + par, par, i, False, False, None)
                pool.wait_ge(sem("ld_ffn"), 48)
                with pool.Fori(PAIRS // 2, PAIRS - 1) as i:
                    for par in range(2):
                        body(2 * i + par, par, i, False, False, 2 * i + par - TILES // 2)
                body(TILES - 2, 0, 0, False, False, TILES // 2 - 2)
                body(TILES - 1, 1, 0, False, True, TILES // 2 - 1)
                pool.wait_ge(sem("ld_late"), 16)
                nc.gpsimd.tensor_copy(wide[:, LATE:], wide[:, LATE:].bitcast(I32)).then_inc(sem("converted"), 1)
                pool_rstd(pool, 7, TILES - 2)
                pool_rstd(pool, 7, TILES - 1)
                pool.wait_ge(sem("wmax"), PAIRS + 2)
                nc.gpsimd.partition_all_reduce(small[:, 3:4], small[:, 2:3], P, RMAX).then_inc(sem("wmax_all"), 1)

            @block.vector
            def _(dve):
                dve.wait_ge(sem("fold_out"), 15)
                dve.wait_ge(sem("zeros3"), 2)

                def norm(t):
                    normalise(dve, 6, t, xn[:], sem("x3_xn"))

                def heads(v):
                    return v.rearrange("p (h d) -> p h d", d=DK3)

                def q_scale(t, par):
                    s, n = sem("q_steps"), NQ * t
                    dve.wait_ge(sem("x3_q"), t + 1)
                    nc.vector.tensor_tensor(t32[:, 0, :], bk(6), b3[:, 0, :], ALU.add).then_inc(s, 1)
                    dve.wait_ge(s, n + 1)
                    nc.vector.tensor_reduce(am[:, 0:1], t32[:, 0, :], AX.X, ALU.max, apply_absolute_value=True).then_inc(s, 1)
                    dve.wait_ge(s, n + 2)
                    nc.vector.tensor_scalar(am[:, 1:2], am[:, 0:1], 1e-30, 1.0 / SPLIT_TOP, ALU.max, ALU.mult).then_inc(s, 1)
                    dve.wait_ge(s, n + 3)
                    nc.vector.reciprocal(am[:, 2:3], am[:, 1:2]).then_inc(s, 1)
                    nc.vector.scalar_tensor_tensor(sc[:, par:par + 1], am[:, 1:2], float(DK3) ** -0.5, am[:, 10:11],
                                                   ALU.mult, ALU.mult).then_inc(s, 1)

                def q_low(t):
                    s, n = sem("q_steps"), NQ * t
                    dve.wait_ge(s, n + 4)
                    dve.wait_ge(sem("q_hi"), t + 1)
                    nc.vector.scalar_tensor_tensor(qrow[:, :, 2, :], heads(t32[:, 0, :]), am[:, 2:3], qrow[:, :, 0, :],
                                                   ALU.mult, ALU.subtract).then_inc(s, 1)

                def k_largest(t):
                    s, n = sem("k_steps"), NK * t
                    dve.wait_ge(sem("x3_k"), t + 1)
                    nc.vector.tensor_tensor(t32[:, 1, :], bk(6), b3[:, 1, :], ALU.add).then_inc(s, 1)
                    dve.wait_ge(s, n + 1)
                    nc.vector.tensor_reduce(am[:, 8:9], t32[:, 1, :], AX.X, ALU.max, apply_absolute_value=True).then_inc(s, 1)

                def k_scale(t):
                    s, n = sem("k_steps"), NK * t
                    dve.wait_ge(sem("k_all"), t + 1)
                    nc.vector.tensor_scalar(am[:, 10:11], am[:, 9:10], 1e-30, 1.0 / SPLIT_TOP, ALU.max, ALU.mult).then_inc(s, 1)
                    dve.wait_ge(s, n + 3)
                    nc.vector.reciprocal(am[:, 11:12], am[:, 10:11]).then_inc(s, 1)

                def k_low(t):
                    s, n = sem("k_steps"), NK * t
                    dve.wait_ge(sem("k_hi"), t + 1)
                    dve.wait_ge(s, n + 4)
                    nc.vector.scalar_tensor_tensor(krow[:, :, 1, :], heads(t32[:, 1, :]), am[:, 11:12], krow[:, :, 0, :],
                                                   ALU.mult, ALU.subtract).then_inc(s, 1)

                def v_ops(t):
                    s, n = sem("v_steps"), NV * t
                    dve.wait_ge(sem("q_steps"), NQ * t + NQ)
                    dve.wait_ge(sem("x3_v"), t + 1)
                    nc.vector.tensor_tensor(t32[:, 0, :], bk(6), b3[:, 2, :], ALU.add).then_inc(s, 1)
                    dve.wait_ge(s, n + 1)
                    nc.vector.tensor_copy(vc[:, :, 0, :], heads(t32[:, 0, :])).then_inc(s, 1)
                    dve.wait_ge(s, n + 2)
                    nc.vector.tensor_tensor(heads(t32[:, 1, :]), heads(t32[:, 0, :]), vc[:, :, 0, :], ALU.subtract).then_inc(s, 1)
                    dve.wait_ge(s, n + 3)
                    nc.vector.tensor_copy(vc[:, :, 1, :], heads(t32[:, 1, :])).then_inc(s, 1)
                    dve.wait_ge(s, n + 4)
                    nc.vector.tensor_tensor(vc[:, :, 2, :], heads(t32[:, 1, :]), vc[:, :, 1, :], ALU.subtract).then_inc(s, 1)

                def vd_ops(t):
                    dve.wait_ge(sem("v_steps"), NV * t + NV)
                    for b in range(BT):
                        for hd in range(2):
                            src = vc[b * C:(b + 1) * C].rearrange("p (g h j) m d -> p g h (j m d)", h=2, j=J3)[:, :, hd, :]
                            dst = vd[hd * C:(hd + 1) * C, b, :, :, hd, 0:24]
                            nc.vector.tensor_copy(dst, src.rearrange("p g (j w) -> p g j w", j=J3)).then_inc(sem("x3_vd"), 1)

                def out_norm(rr, r, t):
                    so = sem("o_steps")
                    if r == 0:
                        after(dve, sem("x3_otr"), t)
                    o2 = ps[:, 0:2, OPC:OPC + 4 * 2 * VW].rearrange("p n (h w) -> p n h w", w=VW)
                    nc.vector.reciprocal(rden[:].rearrange("p (n h) -> p n h", n=2), o2[:, :, :, 24]).then_inc(so, 1)
                    for n in range(2):
                        nc.vector.tensor_reduce(osum[:, 8 * n:8 * n + 8, :],
                                                o2[:, n, :, 0:24].rearrange("p h (m d) -> p h d m", m=3), AX.X,
                                                ALU.add).then_inc(so, 1)
                    dve.wait_ge(so, (NO + 1) * rr + NO)
                    dst = orow[:, r * RG * 32:(r + 1) * RG * 32].rearrange("p (g j d) -> p j g d", g=RG, j=J3)
                    nc.vector.tensor_tensor(dst, osum[:].rearrange("p (j g) d -> p j g d", j=J3),
                                            rden[:].rearrange("p (j g) -> p j g", j=J3).unsqueeze(3).broadcast_to(
                                                [P, J3, RG, DK3]), ALU.mult).then_inc(so, 1)

                def finish(t):
                    dve.wait_ge(sem("x3_wo"), t + 1)
                    dve.wait_ge(sem("x3_biased"), t + 1)
                    nc.vector.tensor_tensor(x[:, t, :], x[:, t, :], bk(6), ALU.add).then_inc(sem("x3_x"), 1)

                norm(0)
                k_largest(0)
                k_scale(0)
                k_low(0)
                q_scale(0, 0)
                q_low(0)
                v_ops(0)
                dve.wait_ge(sem("x3_tr"), 1)
                norm(1)

                def low_parts(rr):
                    dve.wait_ge(sem("x3_pt"), rr + 1)
                    dve.wait_ge(sem("x3_pth"), rr + 1)
                    nc.vector.scalar_tensor_tensor(ptl[:].rearrange("p n q -> p (n q)"),
                                                   ps[:, 4:6, :].rearrange("p b n -> p (b n)"), P_SCALE,
                                                   pth[:].rearrange("p n q -> p (n q)"), ALU.mult,
                                                   ALU.subtract).then_inc(sem("x3_ptl"), 1)

                def largest_weight(c):
                    dve.wait_ge(sem("converted"), c + 1)
                    at = weights_part(c) if not isinstance(c, int) or c < PAIRS else slice(LATE, 3 * FC * D)
                    nc.vector.tensor_reduce(col(wmax, c), wide[:, at], AX.X, ALU.max, apply_absolute_value=True).then_inc(
                        sem("wmax"), 1)

                def body(t, par, pair, first, last, part=None):
                    for r in range(ROUNDS):
                        rr = ROUNDS * t + r
                        s_ps = ps[:, 0:J3, 0:RG * C].rearrange("p j (g k) -> p j g k", g=RG)
                        dve.wait_ge(sem("x3_s"), rr + 1)
                        nc.vector.tensor_reduce(mx[:].rearrange("p (j g) -> p j g", j=J3), s_ps, AX.X, ALU.max).then_inc(
                            sem("x3_max"), 1)
                        dve.wait_ge(sem("x3_max"), rr + 1)
                        after(dve, sem("x3_pt"), rr)
                        nc.vector.tensor_tensor(
                            p32[:], s_ps, mx[:].rearrange("p (j g) -> p j g", j=J3).unsqueeze(3).broadcast_to(
                                [P, J3, RG, C]), ALU.subtract).then_inc(sem("x3_sub"), 1)
                        if not (first and r < 2):
                            out_norm(rr - 2, (r - 2) % ROUNDS, t)
                        if r == 1:
                            if first:
                                dve.wait_ge(sem("zeros3"), 5)
                            vd_ops(t)
                        if not (first and r == 0):
                            low_parts(rr - 1)
                        if r == 0 and not last:
                            k_largest(t + 1)
                        elif r == 1 and not last:
                            k_scale(t + 1)
                            k_low(t + 1)
                            q_scale(t + 1, 1 - par)
                        elif r == 2 and not last:
                            q_low(t + 1)
                            v_ops(t + 1)
                        elif r == 3:
                            if inside(t + 2):
                                norm(t + 2)
                            if not first:
                                finish(t - 1)
                            if part is not None:
                                largest_weight(part)
                body(0, 0, 0, True, False)
                body(1, 1, 0, False, False)
                with dve.Fori(1, PAIRS // 2) as i:
                    for par in range(2):
                        body(2 * i + par, par, i, False, False)
                with dve.Fori(PAIRS // 2, PAIRS - 1) as i:
                    for par in range(2):
                        body(2 * i + par, par, i, False, False, 2 * i + par - TILES // 2)
                body(TILES - 2, 0, PAIRS - 1, False, False, PAIRS - 2)
                body(TILES - 1, 1, PAIRS - 1, False, True, PAIRS - 1)
                low_parts(ROUNDS * TILES - 1)
                out_norm(ROUNDS * TILES - 2, ROUNDS - 2, TILES)
                dve.wait_ge(sem("x3_pv"), ROUNDS * TILES)
                out_norm(ROUNDS * TILES - 1, ROUNDS - 1, TILES)
                largest_weight(PAIRS)
                finish(TILES - 1)
                dve.wait_ge(sem("wmax"), PAIRS + 1)
                nc.vector.reduce_max(small[:, 2:3], wmax[:, :], AX.X).then_inc(sem("wmax"), 1)
                dve.wait_ge(sem("wmax_all"), 1)
                nc.vector.tensor_scalar(small[:, 4:5], small[:, 3:4], SMALL_INT, None, ALU.is_le).then_inc(
                    sem("is_small"), 1)

            @block.scalar
            def _(act):
                def xT_copy(tr, k, done):
                    act.wait_ge(sem(tr), k)
                    nc.scalar.activation(xT[:].rearrange("p k n -> p (k n)"), bk(7), ACT.Copy).then_inc(sem(done), 1)

                def hi(row, lo_part, src, scale, steps, need, done):
                    act.wait_ge(sem(steps), need)
                    dst = row[:, :, 0:2, :] if lo_part == 2 else row[:, :, 0:3:2, :]
                    nc.scalar.activation(dst, src.rearrange("p (h d) -> p h d", d=DK3).unsqueeze(2).broadcast_to(
                        [P, HEADS, 2, DK3]), ACT.Copy, scale=scale).then_inc(sem(done), 1)

                def q_hi(t):
                    hi(qrow, 2, t32[:, 0, :], am[:, 2:3], "q_steps", NQ * t + 4, "q_hi")

                def k_hi(t):
                    hi(krow, 1, t32[:, 1, :], am[:, 11:12], "k_steps", NK * t + 4, "k_hi")

                def t_copy(dst, par, n, tr, t, done):
                    act.wait_ge(sem(tr), 2 * t + n + 1)
                    nc.scalar.activation(dst[:, par, 8 * n:8 * n + 8, :].rearrange("p g n -> p (g n)"),
                                         bk(7).bitcast(F16), ACT.Copy).then_inc(sem(done), 1)

                act.wait_ge(sem("zeros3"), 2)
                xT_copy("x3_tr", 1, "x3_xT")
                k_hi(0)
                t_copy(kT, 0, 0, "x3_ktr", 0, "x3_kT")
                q_hi(0)
                t_copy(kT, 0, 1, "x3_ktr", 0, "x3_kT")
                t_copy(qT, 0, 0, "x3_qtr", 0, "x3_qT")
                t_copy(qT, 0, 1, "x3_qtr", 0, "x3_qT")

                def out_stats(t):
                    act.wait_ge(sem("x3_x"), t + 1)
                    stats(act, 7, t)

                def high_parts(rr):
                    act.wait_ge(sem("x3_pt"), rr + 1)
                    nc.scalar.activation(pth[:].rearrange("p n q -> p (n q)"),
                                         ps[:, 4:6, :].rearrange("p b n -> p (b n)"), ACT.Copy,
                                         scale=P_SCALE).then_inc(sem("x3_pth"), 1)

                def body(t, par, pair, first, last):
                    nxt = 1 - par
                    for r in range(ROUNDS):
                        rr = ROUNDS * t + r
                        if not (first and r == 0):
                            high_parts(rr - 1)
                        if r == 2 and not last:
                            t_copy(kT, nxt, 0, "x3_ktr", t + 1, "x3_kT")
                        elif r == 3 and not last:
                            t_copy(qT, nxt, 0, "x3_qtr", t + 1, "x3_qT")
                        act.wait_ge(sem("x3_sub"), rr + 1)
                        nc.scalar.activation(pf, pf, ACT.Exp, scale=sc[:, par:par + 1]).then_inc(sem("x3_exp"), 1)
                        if r == 0 and inside(t - 2):
                            out_stats(t - 2)
                        if r == 0 and not last:
                            xT_copy("x3_tr", t + 2, "x3_xT")
                        elif r == 1:
                            if not last:
                                k_hi(t + 1)
                            if not first:
                                xT_copy("x3_otr", t, "x3_oT")
                            if not last:
                                q_hi(t + 1)
                        elif r == 2 and not last:
                            t_copy(kT, nxt, 1, "x3_ktr", t + 1, "x3_kT")
                        elif r == 3 and not last:
                            t_copy(qT, nxt, 1, "x3_qtr", t + 1, "x3_qT")
                schedule(act, body)
                high_parts(ROUNDS * TILES - 1)
                out_stats(TILES - 2)
                xT_copy("x3_otr", TILES, "x3_oT")
                out_stats(TILES - 1)

            @block.tensor
            def _(pe):
                pe.wait_ge(sem("f2_x"), TILES)
                pe.wait_ge(sem("fold_out"), 15)

                def project(lhs, w, done):
                    for k in range(KD):
                        last = nc.tensor.matmul(bk(6), lhs[:, k, :], w[:, k, :], start=k == 0, stop=k == KD - 1)
                    last.then_inc(sem(done), 1)

                def rows(t):
                    pe.wait_ge(sem("x3_xn"), t + 1)
                    transpose4(bk(7), xn[:, :]).then_inc(sem("x3_tr"), 1)

                def q_mm(t):
                    pe.wait_ge(sem("x3_xT"), t + 1)
                    project(xT, wf[:, 0], "x3_q")

                def k_mm(t, par, pair):
                    pe.wait_ge(sem(f"ld_x3_{par}"), 16 * pair + 16)
                    project(eT[:, par], wf[:, 1], "x3_k")

                def v_mm(t, par):
                    pe.wait_ge(sem("q_steps"), NQ * t + 1)
                    project(eT[:, par], wf[:, 2], "x3_v")

                def stack_tr(row, n, done):
                    for g in range(8):
                        h = 4 * (8 * n + g)
                        last = nc.tensor.transpose(bk(7).bitcast(F16)[:, g * P:(g + 1) * P],
                                                   row[:, h:h + 4].rearrange("p h m d -> p (h m d)"), ident16[:, :])
                    last.then_inc(sem(done), 1)

                def k_tr(t, n):
                    if n == 0:
                        pe.wait_ge(sem("k_steps"), NK * t + NK)
                        pe.wait_ge(sem("x3_xT"), t + 1)
                    else:
                        pe.wait_ge(sem("x3_kT"), 2 * t + 1)
                    stack_tr(krow, n, "x3_ktr")

                def q_tr(t, n):
                    if n == 0:
                        pe.wait_ge(sem("q_steps"), NQ * t + NQ)
                        pe.wait_ge(sem("x3_kT"), 2 * t + 2)
                    else:
                        pe.wait_ge(sem("x3_qT"), 2 * t + 1)
                    stack_tr(qrow, n, "x3_qtr")

                def pv(rr, r, t):
                    pe.wait_ge(sem("x3_pth"), rr + 1)
                    pe.wait_ge(sem("x3_ptl"), rr + 1)
                    after(pe, sem("o_steps"), (NO + 1) * rr)
                    if r == 0:
                        pe.wait_ge(sem("x3_vd"), 4 * t + 4)
                    for j in range(J3):
                        for u in range(2):
                            n = 2 * j + u
                            c = OPC + n % 4 * 2 * VW
                            for b in range(BT):
                                for pt in (pth, ptl):
                                    last = nc.tensor.matmul(
                                        ps[b * C:(b + 1) * C, n // 4, c:c + 2 * VW], pt[:, n, b * C:(b + 1) * C],
                                        vd[:, b, 2 * r + u, j].rearrange("p h w -> p (h w)"), start=pt is pth, stop=pt is ptl)
                    last.then_inc(sem("x3_pv"), 1)

                def o_tr(t):
                    pe.wait_ge(sem("o_steps"), (NO + 1) * ROUNDS * (t + 1))
                    transpose4(bk(7), orow[:, :]).then_inc(sem("x3_otr"), 1)

                def wo_mm(t):
                    pe.wait_ge(sem("x3_oT"), t + 1)
                    project(xT, wo, "x3_wo")

                rows(0)
                k_mm(0, 0, 0)
                pe.wait_ge(sem("k_steps"), 1)
                q_mm(0)
                k_tr(0, 0)
                k_tr(0, 1)
                v_mm(0, 0)
                q_tr(0, 0)
                q_tr(0, 1)

                def prob_tr(rr):
                    pe.wait_ge(sem("x3_exp"), rr + 1)
                    after(pe, sem("x3_ptl"), rr)
                    for j in range(J3):
                        for u in range(2):
                            n = 2 * j + u
                            mm = nc.tensor.transpose(ps[:, 4 + n // 4, n % 4 * P:(n % 4 + 1) * P],
                                                     p32[:, j, 2 * u:2 * u + 2, :].rearrange("p g k -> p (g k)"),
                                                     ident[:, :])
                    mm.then_inc(sem("x3_pt"), 1)

                def body(t, par, pair, first, last):
                    nxt = 1 - par
                    npair = pair + 1 if par else pair
                    for r in range(ROUNDS):
                        rr = ROUNDS * t + r
                        after(pe, sem("x3_sub"), rr)
                        if r == 0:
                            pe.wait_ge(sem("x3_qT"), 2 * t + 2)
                        for g in range(RG):
                            for b in range(BT):
                                for j in range(J3):
                                    rows_j, cols_b = slice(32 * j, 32 * j + 32), slice(b * C, (b + 1) * C)
                                    mm = nc.tensor.matmul(ps[cols_b, j, g * C:(g + 1) * C],
                                                          qT[rows_j, par, RG * r + g, cols_b],
                                                          kT[rows_j, par, RG * r + g, cols_b], start=True, stop=True)
                        mm.then_inc(sem("x3_s"), 1)
                        if not (first and r == 0):
                            prob_tr(rr - 1)
                        if r == 0 and not last:
                            rows(t + 1)
                            after(pe, sem("x3_x"), t - 1)
                            if first:
                                pe.wait_ge(sem("v_steps"), 1)
                            k_mm(t + 1, nxt, npair)
                        elif r == 1:
                            if not last:
                                pe.wait_ge(sem("k_steps"), NK * (t + 1) + 1)
                                q_mm(t + 1)
                            if not first:
                                o_tr(t - 1)
                        elif r == 2 and not last:
                            after(pe, sem("x3_oT"), t)
                            k_tr(t + 1, 0)
                            v_mm(t + 1, nxt)
                            k_tr(t + 1, 1)
                        elif r == 3:
                            if not last:
                                q_tr(t + 1, 0)
                            if not first:
                                if last:
                                    pe.wait_ge(sem("x3_x"), t - 1)
                                else:
                                    pe.wait_ge(sem("v_steps"), NV * (t + 1) + 1)
                                wo_mm(t - 1)
                            if not last:
                                q_tr(t + 1, 1)
                        if not (first and r == 0):
                            pe.wait_ge(sem("x3_sub"), rr + 1)
                            pv(rr - 1, (r - 1) % ROUNDS, t)
                schedule(pe, body)
                prob_tr(ROUNDS * TILES - 1)
                pv(ROUNDS * TILES - 1, ROUNDS - 1, TILES)
                pe.wait_ge(sem("x3_x"), TILES - 1)
                o_tr(TILES - 1)
                wo_mm(TILES - 1)

        GT = 4
        GROUPS = TILES // GT
        UP0 = 2
        with ExitStack() as c3:
            def s3(name, shape, dt=F32):
                return sb(name, shape, dt, c3)
            xn = s3("xn8", [P, 2, D])
            xT_words = s3("xT8", [P, KD * GT * P])
            xT = xT_words[:].rearrange("p (k n) -> p k n", k=KD)
            xT_parts = xT_words[:].bitcast(F16).rearrange("p (b k n) -> p b k n", b=2, k=KD)
            sg = s3("sg", [P, 2, GT * P])
            hid_r = s3("hid_r", [P, 2, 2, GT * P], F32R)
            scaled = s3("scaled", [P, 2, D])
            gsc = s3("gsc", [P, FC])
            passed = s3("passed", [P, GT])
            usc = s3("usc", [P, FC])
            down_r = s3("down_r", [P, FC, D], F32R)
            dsc = wf[:].rearrange("p w k n -> p (w k n)")[:, (3 * KD - 1) * D:]
            block = c3.enter_context(nc.Block())
            gate_w = FG.rearrange("p (k n) -> p k n", k=KD)
            up_w = FU.rearrange("p (k n) -> p k n", k=KD)
            down_w = FD.rearrange("p (k n) -> p k n", k=FC)
            wf16 = wf[:].rearrange("p w k n -> p (w k n)").bitcast(F16)
            wo16 = wo[:].rearrange("p k n -> p (k n)").bitcast(F16)
            gate16 = wf16[:, 0:KD * FF].rearrange("p (k n) -> p k n", k=KD)
            up16a = wf16[:, KD * FF:(KD + UP0) * FF].rearrange("p (k n) -> p k n", k=UP0)
            up16b = wo16[:, 0:(KD - UP0) * FF].rearrange("p (k n) -> p k n", k=KD - UP0)
            PARTS = ((0, 2), (2, 6), (6, 10), (10, FC))

            def groups(eng, body):
                body(0, False)
                with eng.Fori(1, GROUPS - 1) as g:
                    body(g, False)
                body(GROUPS - 1, True)

            @block.sync
            def _(sp):
                sp.dma_start(gsc[:], a["gate_s"]).then_inc(sem("ld_scales"), 16)
                sp.dma_start(usc[:], a["up_s"]).then_inc(sem("ld_scales"), 16)
                sp.dma_start(dsc, a["down_s"].partition_broadcast(P)).then_inc(sem("ld_scales"), 16)
                with sp.Fori(0, TILES) as t:
                    sp.wait_ge(sem("f3_x"), 2 * t + 2)
                    sp.dma_start(outv[t], x[:, t, :]).then_inc(sem("stored"), 16)
                sp.wait_ge(sem("stored"), 16 * TILES)

            @block.gpsimd
            def _(pool):
                pool.wait_ge(sem("converted"), PAIRS + 1)
                for f in range(FC):
                    nc.gpsimd.tensor_copy(down_r[:, f, :], down_w[:, f, :]).then_inc(sem("down_r"), 1)

            @block.vector
            def _(dve):
                def norm(g, j):
                    if isinstance(g, int) and g == 0:
                        if j >= 2:
                            dve.wait_ge(sem("f3_tr"), j - 1)
                    else:
                        dve.wait_ge(sem("f3_tr"), GT * g + j - 1)
                    normalise(dve, 7, GT * g + j, xn[:, j % 2, :], sem("f3_xn"))

                def low_rows(g):
                    for j in range(GT):
                        c = slice(j * P, (j + 1) * P)
                        with dve.If(small_ints > 0):
                            dve.wait_ge(sem("f3_xT"), GT * g + j + 1)
                            nc.vector.scalar_tensor_tensor(xT_parts[:, 1, :, c],
                                                           bk(4 + j).rearrange("p (k n) -> p k n", k=KD), X_SCALE,
                                                           xT_parts[:, 0, :, c], ALU.mult, ALU.subtract).then_inc(
                                                               sem("f3_xTl"), 1)
                        with dve.Else():
                            dve.wait_ge(sem("f3_xT"), GT * g + j + 1)
                            nc.vector.memset(passed[0:1, j:j + 1], 0.0).then_inc(sem("f3_xTl"), 1)

                norm(0, 0)
                norm(0, 1)
                dve.wait_ge(sem("x3_wo"), TILES)
                dve.wait_ge(sem("converted"), PAIRS + 1)
                for n, (lo, hi) in enumerate(PARTS):
                    cols = slice(lo * P, hi * P)
                    nc.vector.tensor_copy(gate16[:, :, cols], gate_w[:, :, cols]).then_inc(sem("gate16"), 1)
                    if n == 0:
                        dve.wait_ge(sem("is_small"), 1)
                        small_ints = dve.value_load(small[0:1, 4:5].bitcast(I32))
                        norm(0, 2)
                        norm(0, 3)
                        low_rows(0)
                dve.wait_ge(sem("ld_scales"), 48)
                nc.vector.tensor_scalar(usc[:], usc[:], 1.0 / X_SCALE, None, ALU.mult).then_inc(sem("scales3"), 1)
                nc.vector.tensor_scalar(gsc[:], gsc[:], 1.0 / X_SCALE, None, ALU.mult).then_inc(sem("scales3"), 1)
                dve.wait_ge(sem("scales3"), 2)

                def body(g, last):
                    for f in range(FC):
                        n, b = FC * g + f, f % 2
                        hs = sem("f3_parts")
                        dve.wait_ge(sem("f3_gu"), n + 1)
                        dve.wait_ge(sem("f3_silu"), n + 1)
                        nc.vector.scalar_tensor_tensor(sg[:, b, :], bk(5 + 2 * b), usc[:, f:f + 1], sg[:, b, :],
                                                       ALU.mult, ALU.mult).then_inc(hs, 1)
                        dve.wait_ge(hs, 3 * n + 1)
                        nc.vector.tensor_copy(hid_r[:, b, 0, :], sg[:, b, :]).then_inc(hs, 1)
                        dve.wait_ge(hs, 3 * n + 2)
                        nc.vector.tensor_tensor(hid_r[:, b, 1, :], sg[:, b, :], hid_r[:, b, 0, :],
                                                ALU.subtract).then_inc(hs, 1)
                        if f == FC // 2 and not last:
                            norm(g + 1, 0)
                            norm(g + 1, 1)
                    if not last:
                        norm(g + 1, 2)
                        norm(g + 1, 3)
                        low_rows(g + 1)
                    for j in range(GT):
                        t = GT * g + j
                        dve.wait_ge(sem("f3_down"), t + 1)
                        nc.vector.tensor_tensor(scaled[:, j % 2, :], bk(j), dsc, ALU.mult).then_inc(sem("f3_x"), 1)
                        dve.wait_ge(sem("f3_x"), 2 * t + 1)
                        nc.vector.tensor_tensor(x[:, t, :], x[:, t, :], scaled[:, j % 2, :], ALU.add).then_inc(sem("f3_x"), 1)
                groups(dve, body)

            @block.scalar
            def _(act):
                def xT_copy(g):
                    for j in range(GT):
                        c = slice(j * P, (j + 1) * P)
                        src = bk(4 + j).rearrange("p (k n) -> p k n", k=KD)
                        with act.If(small_ints > 0):
                            act.wait_ge(sem("f3_tr"), GT * g + j + 1)
                            nc.scalar.activation(xT_parts[:, 0, :, c], src, ACT.Copy, scale=X_SCALE).then_inc(
                                sem("f3_xT"), 1)
                        with act.Else():
                            act.wait_ge(sem("f3_tr"), GT * g + j + 1)
                            nc.scalar.activation(xT[:, :, c], src, ACT.Copy, scale=X_SCALE).then_inc(sem("f3_xT"), 1)

                act.wait_ge(sem("x3_wo"), TILES)
                act.wait_ge(sem("converted"), PAIRS + 1)
                for n, (lo, hi) in enumerate(PARTS):
                    cols = slice(lo * P, hi * P)
                    for k, dst in ((0, up16a), (UP0, up16b)):
                        nc.scalar.activation(dst[:, :, cols], up_w[:, k:k + UP0, cols], ACT.Copy).then_inc(sem("up16"), 1)
                    if n == 0:
                        act.wait_ge(sem("is_small"), 1)
                        small_ints = act.value_load(small[0:1, 4:5].bitcast(I32))
                        xT_copy(0)
                act.wait_ge(sem("scales3"), 2)

                def body(g, last):
                    for f in range(FC):
                        act.wait_ge(sem("f3_gu"), FC * g + f + 1)
                        if f >= 2:
                            act.wait_ge(sem("f3_parts"), 3 * (FC * g + f - 1))
                        nc.scalar.activation(sg[:, f % 2, :], bk(4 + 2 * (f % 2)), ACT.Silu, scale=gsc[:, f:f + 1]).then_inc(
                            sem("f3_silu"), 1)
                    if not last:
                        xT_copy(g + 1)
                groups(act, body)

            @block.tensor
            def _(pe):
                pe.wait_ge(sem("x3_x"), TILES)
                pe.wait_ge(sem("converted"), PAIRS + 1)

                def rows(g, j):
                    pe.wait_ge(sem("f3_xn"), GT * g + j + 1)
                    transpose4(bk(4 + j), xn[:, j % 2, :]).then_inc(sem("f3_tr"), 1)

                def products(small_ints):
                    def gate_up(g, f, first):
                        cols = slice(f * P, (f + 1) * P)
                        if first and small_ints and f in [lo for lo, hi in PARTS]:
                            n = [lo for lo, hi in PARTS].index(f)
                            pe.wait_ge(sem("gate16"), n + 1)
                            pe.wait_ge(sem("up16"), 2 * n + 2)
                        for w, b in ((0, 4 + 2 * (f % 2)), (1, 5 + 2 * (f % 2))):
                            for k in range(KD):
                                if small_ints:
                                    w16 = gate16[:, k, cols] if w == 0 else (
                                        up16a[:, k, cols] if k < UP0 else up16b[:, k - UP0, cols])
                                    nc.tensor.matmul(bk(b), w16, xT_parts[:, 0, k, :], start=k == 0, stop=False)
                                    last = nc.tensor.matmul(bk(b), w16, xT_parts[:, 1, k, :], start=False, stop=k == KD - 1)
                                else:
                                    last = nc.tensor.matmul(bk(b), (gate_w, up_w)[w][:, k, cols], xT[:, k, :],
                                                            start=k == 0, stop=k == KD - 1)
                        last.then_inc(sem("f3_gu"), 1)

                    def down(g, f, first):
                        pe.wait_ge(sem("f3_parts"), 3 * (FC * g + f + 1))
                        if first and small_ints:
                            pe.wait_ge(sem("down_r"), f + 1)
                        for j in range(GT):
                            c = slice(j * P, (j + 1) * P)
                            if small_ints:
                                for m in range(2):
                                    mm = nc.tensor.matmul(bk(j), hid_r[:, f % 2, m, c], down_r[:, f, :],
                                                          start=f == 0 and m == 0, stop=f == FC - 1 and m == 1)
                            else:
                                mm = nc.tensor.matmul(bk(j), sg[:, f % 2, c], down_w[:, f, :], start=f == 0,
                                                      stop=f == FC - 1)
                            if f == FC - 1:
                                mm.then_inc(sem("f3_down"), 1)

                    def body(g, last, first=False):
                        pe.wait_ge(sem("f3_xTl"), GT * g + GT)
                        gate_up(g, 0, first)
                        gate_up(g, 1, first)
                        after(pe, sem("f3_x"), 2 * GT * g)
                        for f in range(FC):
                            if f == FC - 1 and not last:
                                pe.wait_ge(sem("f3_parts"), 3 * (FC * g + f) + 1)
                                for j in (2, 3):
                                    rows(g + 1, j)
                            down(g, f, first)
                            if f + 2 < FC:
                                gate_up(g, f + 2, first)
                            elif f + 2 == FC and not last:
                                for j in (0, 1):
                                    rows(g + 1, j)
                    body(0, False, True)
                    with pe.Fori(1, GROUPS - 1) as g:
                        body(g, False)
                    body(GROUPS - 1, True)

                for j in range(GT):
                    rows(0, j)
                pe.wait_ge(sem("is_small"), 1)
                is_small = pe.value_load(small[0:1, 4:5].bitcast(I32))
                with pe.If(is_small > 0):
                    products(True)
                with pe.Else():
                    products(False)


_CORE_INPUTS = ["x", "ctx"]


def kernel(**inputs):
    import numpy as np
    import concourse.bacc as bacc
    from concourse.bass_utils import run_bass_kernel_spmd

    v = {k: np.asarray(w) for k, w in inputs.items()}
    f32 = np.float32
    tiles, kd = TILES, KD
    ctx = v["ctx_4096"].reshape(B * C, D)
    ar = {
        "x": v["x"].reshape(B * C, D),
        "ctx": ctx,
        "ctxT": ctx.reshape(tiles, P, kd, P).transpose(0, 3, 2, 1),
        "f0_base": v["L0_ffn_W_base"].T,
        "f0_ag": np.concatenate([v["L0_ffn_A_w"].reshape(E0 * R0, D), v["L0_ffn_W_gate"], v["L0_ffn_W_thr"][None]]).T,
        "f0_b": v["L0_ffn_B_w"].transpose(0, 2, 1).reshape(E0 * R0, D),
        "f0_bias": v["L0_ffn_b_base"],
        "thr_b": v["L0_ffn_b_thr"],
        "f1_base": v["L1_ffn_base_W"].T,
        "f1_ag": np.concatenate([v["L1_ffn_A"].reshape(E0 * R0, D), v["L1_ffn_router_W"]]).T,
        "f1_b": v["L1_ffn_B"].transpose(0, 2, 1).reshape(E0 * R0, D),
        "f1_bias": v["L1_ffn_base_b"],
        "router_b": v["L1_ffn_router_b"],
        "expert_map": v["L1_ffn_expert_map"],
        "f2_base": v["L2_ffn_W"].T,
        "f2_ag": np.concatenate([v["L2_ffn_A"], v["L2_ffn_gate_w"]]).T,
        "f2_b": v["L2_ffn_B"].T,
        "f2_bias": v["L2_ffn_b"],
        "gate_b2": v["L2_ffn_gate_b"],
        "w3": np.stack([v["L3_xattn_Wq"], v["L3_xattn_Wk"], v["L3_xattn_Wv"]]),
        "b3rep": np.stack([np.repeat(v[f"L3_xattn_b{c}"][:, None], P, 1) for c in "qkv"]),
        "wo3": v["L3_xattn_Wo"].T.reshape(H3, DK3, M3, D).transpose(0, 2, 1, 3).reshape(D, D),
        "bo3": v["L3_xattn_bo"],
        "irep": np.repeat(v["L3_xattn_interference"][:, None], DK3, 1).reshape(D, M3),
        "amp": v["L3_xattn_amp"],
        "gate_t": v["L3_ffn_gate_t"].T,
        "up_t": v["L3_ffn_up_t"].T,
        "down_t": v["L3_ffn_down_t"].T,
        "gate_s": v["L3_ffn_gate_s"].reshape(FC, P).T,
        "up_s": v["L3_ffn_up_s"].reshape(FC, P).T,
        "down_s": v["L3_ffn_down_s"],
    }
    w = v["L0_xattn_weight"].transpose(1, 2, 0)
    conv = np.zeros((BT, C, TAPS, BT, C), f32)
    for b in range(BT):
        conv[b, :, :, b, :] = w
    ar["convw"] = conv.reshape(P, TAPS, P)
    ar["c_ident"] = np.eye(P, dtype=f32)
    ar["c_ident16"] = np.eye(P, dtype=np.float16)
    ar["c_g8"] = np.kron(np.eye(P // 8), np.ones((8, 8))).astype(f32)
    pick = np.zeros((P, tiles, B), f32)
    for t in range(tiles):
        for b in range(BT):
            pick[b * C:(b + 1) * C, t, BT * t + b] = 1
    ar["c_pick"] = pick
    sel = np.zeros((TAPS, B, tiles, TAPS, BT, C), np.float16)
    for t in range(tiles):
        for b in range(BT):
            for k in range(TAPS):
                for c in range(C):
                    sel[(TAPS * c + k) // C, BT * t + b, t, k, b, c] = 1
    ar["c_sel"] = sel.reshape(TAPS * B, tiles, TAPS, P)
    hdi = np.arange(P)
    h_in, d_in, m_in = hdi // 32, hdi // 4 % 8, hdi % 4
    h_out, m_out, d_out = hdi // 32, hdi // 8 % 4, hdi % 8
    same = (h_in[:, None] == h_out) & (d_in[:, None] == d_out)
    ar["c_m4"] = same.astype(f32)
    ar["c_ip"] = (same & (m_in[:, None] == m_out)).astype(f32)

    nc = bacc.Bacc("TRN2", target_bir_lowering=False, num_devices=1)
    arrays, dram = {}, {}
    for name, arr in ar.items():
        arr = np.ascontiguousarray(arr)
        arrays[f"in_{name}"] = arr
        dram[name] = nc.dram_tensor(f"in_{name}", arr.shape, mybir.dt.from_np(arr.dtype), kind="ExternalInput").ap()
    out = nc.dram_tensor("out", (B * C, D), F32, kind="ExternalOutput").ap()
    xattn_ffn_program(nc, dram, out)
    r = run_bass_kernel_spmd(nc, [arrays], core_ids=[0])
    return np.asarray(r.results[0]["out"]).reshape(B, C, D)
```
